# Optimizing a Trainium2 kernel written in Bass

```python
import numpy as np
import jax
import jax.numpy as jnp

def _softmax(x, axis=-1):
    return jax.nn.softmax(x, axis=axis)

def _gelu(x):
    return jax.nn.gelu(x, approximate=True)

def _silu(x):
    return jax.nn.silu(x)

def _sigmoid(x):
    return jax.nn.sigmoid(x)

def _layernorm(x, axis=-1, eps=1e-05):
    m = jnp.mean(x, axis=axis, keepdims=True)
    v = jnp.var(x, axis=axis, keepdims=True)
    return (x - m) / jnp.sqrt(v + eps)

def _scatter_add(tgt, idx, src, axis=0):
    return tgt.at[idx].add(src)

def _segment_sum(src, seg, n):
    return jax.ops.segment_sum(src, seg, n)
kernel_name = 'mk_pixart_resid_d4_seqx_r8_049186'

def setup_inputs(seed: int=0):
    np.random.seed(seed)
    _w = jnp.asarray

    def _rec_inputs():
        import jax
        import jax.numpy as jnp
        _rk = jax.random.key(seed)
        x = -0.003379 + 0.9984 * jax.random.normal(jax.random.fold_in(_rk, 1), (32, 128, 128), jnp.float32)
        _lenS = 128 - jax.random.randint(jax.random.fold_in(_rk, 7), (32,), 0, max(1, 128 // 4) + 1, jnp.int32)
        _lenS2 = 77 - jax.random.randint(jax.random.fold_in(_rk, 8), (32,), 0, max(1, 77 // 4) + 1, jnp.int32)
        cond_1024 = -0.0142567 + 1.00875 * jax.random.normal(jax.random.fold_in(_rk, 11), (32, 128), jnp.float32)
        _ctx_1024P = jax.random.normal(jax.random.fold_in(_rk, 12), (32, 16, 128), jnp.float32)
        _ctx_1024c = jax.random.dirichlet(jax.random.fold_in(_rk, 512), 0.3 * jnp.ones((16,), jnp.float32), (32, 77))
        _ctx_1024t = jnp.einsum('bsk,bkd->bsd', _ctx_1024c, _ctx_1024P)
        _ctx_1024t = _ctx_1024t * jax.lax.rsqrt(jnp.mean(jnp.square(_ctx_1024t)) + 1e-12) * 0.953939
        ctx_1024 = -5.72187e-05 + 0.999849 * (_ctx_1024t + 0.3 * jax.random.normal(jax.random.fold_in(_rk, 612), (32, 77, 128), jnp.float32))
        _validS = jnp.arange(128)[None, :] < _lenS[:, None]
        _validS2 = jnp.arange(77)[None, :] < _lenS2[:, None]
        _causal = jnp.tril(jnp.ones((128, 128), dtype=bool))
        mask_BxS_bf0 = jnp.logical_not(jnp.ones((32, 128), dtype=bool))
        mask_BxS2_bf0 = jnp.logical_not(jnp.ones((32, 77), dtype=bool))
        return (x, cond_1024, ctx_1024, mask_BxS_bf0, mask_BxS2_bf0)
    x, cond_1024, ctx_1024, mask_BxS_bf0, mask_BxS2_bf0 = _rec_inputs()

    def _L0_xcond_setup():
        import jax, jax.numpy as jnp
        import numpy as np
        B, N, K, D, T = (16, 512, 16, 128, 3)
        EPS_ATTN = 1e-08
        LN_EPS = 1e-05

        def _ln(x, g, b):
            mu = jnp.mean(x, axis=-1, keepdims=True)
            var = jnp.mean(jnp.square(x - mu), axis=-1, keepdims=True)
            return (x - mu) * jax.lax.rsqrt(var + LN_EPS) * g + b
        key = jax.random.key(seed)
        ks = jax.random.split(key, 16)
        w = lambda k, i, o: jax.random.normal(k, (i, o), jnp.float32) * 0.02
        inp = {'x_cls': jax.random.normal(ks[0], (B, D), jnp.float32), 'x': jax.random.normal(ks[1], (B, N, D), jnp.float32), 'noise': jax.random.normal(ks[2], (B, K, D), jnp.float32), 'q_mu': jax.random.normal(ks[3], (1, 1, D), jnp.float32), 'q_logsig': jax.random.normal(ks[4], (1, 1, D), jnp.float32) * 0.02, 'lnkv_g': jnp.ones((D,), jnp.float32), 'lnkv_b': jnp.zeros((D,), jnp.float32), 'lnq_g': jnp.ones((D,), jnp.float32), 'lnq_b': jnp.zeros((D,), jnp.float32), 'lnm_g': jnp.ones((D,), jnp.float32), 'lnm_b': jnp.zeros((D,), jnp.float32), 'lnp_g': jnp.ones((D,), jnp.float32), 'lnp_b': jnp.zeros((D,), jnp.float32), 'wk': w(ks[5], D, D), 'bk': jnp.zeros((D,), jnp.float32), 'wv': w(ks[6], D, D), 'bv': jnp.zeros((D,), jnp.float32), 'wq': w(ks[7], D, D), 'bq': jnp.zeros((D,), jnp.float32), 'wu': w(ks[8], D, D), 'bu': jnp.zeros((D,), jnp.float32), 'w1': w(ks[9], D, D), 'b1': jnp.zeros((D,), jnp.float32), 'w2': w(ks[10], D, D), 'b2': jnp.zeros((D,), jnp.float32)}
        return inp
    _L0_xcond_all = _L0_xcond_setup()
    _L0_xcond_in = {k: v for k, v in _L0_xcond_all.items() if k in ('q_mu', 'q_logsig', 'lnkv_g', 'lnkv_b', 'lnq_g', 'lnq_b', 'lnm_g', 'lnm_b', 'lnp_g', 'lnp_b', 'wk', 'bk', 'wv', 'bv', 'wq', 'bq', 'wu', 'bu', 'w1', 'b1', 'w2', 'b2')}
    del _L0_xcond_all

    def _L0_ffn_setup():
        import jax, jax.numpy as jnp
        import numpy as np
        H = 8
        QD = 32
        HALF = QD // 2
        DIMS = (32, 32)
        TOPK = 16
        DTK = 4
        EPS_BN = 1e-05
        EPS_NORM = 1e-12

        def _l2norm(x):
            n = jnp.linalg.norm(x, axis=-1, keepdims=True)
            return x / jnp.maximum(n, EPS_NORM)
        key = jax.random.key(seed)
        ks = jax.random.split(key, 6)
        B, S, D, O, E = (2, 64, 128, 128, 128)
        hidden_states = jax.random.normal(ks[0], (B, S, D), jnp.float32)
        Wq = jax.random.normal(ks[1], (D, H * QD), jnp.float32) * 0.02
        bq = jnp.zeros((H * QD,), jnp.float32)
        bn_gamma = jnp.ones((QD,), jnp.float32)
        bn_beta = jnp.zeros((QD,), jnp.float32)
        sub_key0 = jax.random.normal(ks[2], (DIMS[0], HALF), jnp.float32) * 0.02
        sub_key1 = jax.random.normal(ks[3], (DIMS[1], HALF), jnp.float32) * 0.02
        expert_down = jax.random.normal(ks[4], (E, D), jnp.float32) * 0.02
        expert_up = jax.random.normal(ks[5], (E, O), jnp.float32) * 0.02
        return {'hidden_states': hidden_states, 'Wq': Wq, 'bq': bq, 'bn_gamma': bn_gamma, 'bn_beta': bn_beta, 'sub_key0': sub_key0, 'sub_key1': sub_key1, 'expert_down': expert_down, 'expert_up': expert_up}
    _L0_ffn_all = _L0_ffn_setup()
    _L0_ffn_in = {k: v for k, v in _L0_ffn_all.items() if k in ('Wq', 'bq', 'bn_gamma', 'bn_beta', 'sub_key0', 'sub_key1', 'expert_down', 'expert_up')}
    del _L0_ffn_all

    def _L1_xcond_setup():
        import jax, jax.numpy as jnp
        import numpy as np
        import math
        B, S, CTX, D, H, DH = (2, 256, 32, 128, 16, 64)
        INNER = H * DH
        DFF = 4 * D

        def layernorm(x, eps=1e-05):
            m = jnp.mean(x, axis=-1, keepdims=True)
            v = jnp.var(x, axis=-1, keepdims=True)
            return (x - m) * jax.lax.rsqrt(v + eps)

        def adaln(x, t, w, b):
            emb = t @ w + b
            scale, shift = jnp.split(emb, 2, axis=-1)
            return layernorm(x) * (1.0 + scale) + shift

        def mha(xq, ctx, wq, wk, wv, wo, bo):
            b, sq, _ = xq.shape
            sk = ctx.shape[1]
            q = (xq @ wq).reshape(b, sq, H, DH).transpose(0, 2, 1, 3)
            k = (ctx @ wk).reshape(b, sk, H, DH).transpose(0, 2, 1, 3)
            v = (ctx @ wv).reshape(b, sk, H, DH).transpose(0, 2, 1, 3)
            scores = jnp.einsum('bhqd,bhkd->bhqk', q, k) / math.sqrt(DH)
            attn = jax.nn.softmax(scores, axis=-1)
            out = jnp.einsum('bhqk,bhkd->bhqd', attn, v)
            out = out.transpose(0, 2, 1, 3).reshape(b, sq, INNER)
            return out @ wo + bo

        def glu_ff(x, w1, b1, w2, b2):
            u = x @ w1 + b1
            a, gate = jnp.split(u, 2, axis=-1)
            return a * jax.nn.gelu(gate, approximate=False) @ w2 + b2
        key = jax.random.key(seed)
        ks = jax.random.split(key, 24)
        s = 1.0 / math.sqrt(D)

        def n(k, shape, scale=1.0):
            return jax.random.normal(k, shape, dtype=jnp.float32) * scale
        return {'x': n(ks[0], (B, S, D)), 't': n(ks[1], (B, 1, D)), 'context': n(ks[2], (B, CTX, D)), 'attn1_wq': n(ks[3], (D, INNER), s), 'attn1_wk': n(ks[4], (D, INNER), s), 'attn1_wv': n(ks[5], (D, INNER), s), 'attn1_wo': n(ks[6], (INNER, D), s), 'attn1_bo': n(ks[7], (D,), 0.01), 'attn2_wq': n(ks[8], (D, INNER), s), 'attn2_wk': n(ks[9], (D, INNER), s), 'attn2_wv': n(ks[10], (D, INNER), s), 'attn2_wo': n(ks[11], (INNER, D), s), 'attn2_bo': n(ks[12], (D,), 0.01), 'ff_w1': n(ks[13], (D, 2 * DFF), s), 'ff_b1': n(ks[14], (2 * DFF,), 0.01), 'ff_w2': n(ks[15], (DFF, D), 1.0 / math.sqrt(DFF)), 'ff_b2': n(ks[16], (D,), 0.01), 'norm1_w': n(ks[17], (D, 2 * D), s), 'norm1_b': n(ks[18], (2 * D,), 0.01), 'norm2_w': n(ks[19], (D, 2 * D), s), 'norm2_b': n(ks[20], (2 * D,), 0.01), 'norm3_w': n(ks[21], (D, 2 * D), s), 'norm3_b': n(ks[22], (2 * D,), 0.01)}
    _L1_xcond_all = _L1_xcond_setup()
    _L1_xcond_in = {k: v for k, v in _L1_xcond_all.items() if k in ('attn1_wq', 'attn1_wk', 'attn1_wv', 'attn1_wo', 'attn1_bo', 'attn2_wq', 'attn2_wk', 'attn2_wv', 'attn2_wo', 'attn2_bo', 'ff_w1', 'ff_b1', 'ff_w2', 'ff_b2', 'norm1_w', 'norm1_b', 'norm2_w', 'norm2_b', 'norm3_w', 'norm3_b')}
    del _L1_xcond_all

    def _L1_ffn_setup():
        import jax, jax.numpy as jnp
        import numpy as np
        NUM_HEADS = 16
        TOP_K = 2
        key = jax.random.key(seed)
        ks = jax.random.split(key, 5)
        B, S, D, E = (4, 256, 128, 8)
        scale = 0.02
        return {'x': jax.random.normal(ks[0], (B, S, D), dtype=jnp.float32), 'W_qkv': jax.random.normal(ks[1], (D, 3 * D), dtype=jnp.float32) * scale, 'b_qkv': jnp.zeros((3 * D,), dtype=jnp.float32), 'W_gate': jax.random.normal(ks[2], (D, E), dtype=jnp.float32) * scale, 'b_gate': jnp.zeros((E,), dtype=jnp.float32), 'W_experts': jax.random.normal(ks[3], (E, D, D), dtype=jnp.float32) * scale, 'b_experts': jnp.zeros((E, D), dtype=jnp.float32)}
    _L1_ffn_all = _L1_ffn_setup()
    _L1_ffn_in = {k: v for k, v in _L1_ffn_all.items() if k in ('W_qkv', 'b_qkv', 'W_gate', 'b_gate', 'W_experts', 'b_experts')}
    del _L1_ffn_all

    def _L2_xcond_setup():
        import jax, jax.numpy as jnp
        import numpy as np
        B, T, S, H, E = (32, 64, 64, 128, 128)
        key = jax.random.key(seed)
        ks = jax.random.split(key, 7)
        sc = 0.02
        return {'dec_seq': jax.random.normal(ks[0], (B, T, E), jnp.float32), 'enc_hiddens': jax.random.normal(ks[1], (B, S, H), jnp.float32), 'last_hidden': jax.random.normal(ks[2], (B, H), jnp.float32), 'W': jax.random.normal(ks[3], (H, H), jnp.float32) * sc, 'kernel': jax.random.normal(ks[4], (E + H, 3 * H), jnp.float32) * sc, 'recurrent_kernel': jax.random.normal(ks[5], (H, 3 * H), jnp.float32) * sc, 'bias': jnp.zeros((3 * H,), jnp.float32)}
    _L2_xcond_all = _L2_xcond_setup()
    _L2_xcond_in = {k: v for k, v in _L2_xcond_all.items() if k in ('W', 'kernel', 'recurrent_kernel', 'bias')}
    del _L2_xcond_all

    def _L2_ffn_setup():
        import jax, jax.numpy as jnp
        import numpy as np
        HIDDEN = 128
        FFN = 4 * HIDDEN
        NUM_EXPERTS = 8
        TOP_K = 2
        B, S = (4, 256)
        key = jax.random.key(seed)
        ks = jax.random.split(key, 7)
        scale = 0.02
        return {'x': jax.random.normal(ks[0], (B, S, HIDDEN), dtype=jnp.float32), 'gate_w': jax.random.normal(ks[1], (HIDDEN, NUM_EXPERTS), dtype=jnp.float32) * scale, 'gate_b': jnp.zeros((NUM_EXPERTS,), dtype=jnp.float32), 'w1': jax.random.normal(ks[2], (NUM_EXPERTS, HIDDEN, FFN), dtype=jnp.float32) * scale, 'b1': jnp.zeros((NUM_EXPERTS, FFN), dtype=jnp.float32), 'w2': jax.random.normal(ks[3], (NUM_EXPERTS, FFN, HIDDEN), dtype=jnp.float32) * scale, 'b2': jnp.zeros((NUM_EXPERTS, HIDDEN), dtype=jnp.float32)}
    _L2_ffn_all = _L2_ffn_setup()
    _L2_ffn_in = {k: v for k, v in _L2_ffn_all.items() if k in ('gate_w', 'gate_b', 'w1', 'b1', 'w2', 'b2')}
    del _L2_ffn_all

    def _L3_xcond_setup():
        import jax, jax.numpy as jnp
        import numpy as np
        NL, D, H, DFF = (6, 128, 16, 512)
        HD = D // H

        def _rope(x):
            L = x.shape[1]
            half = HD // 2
            inv = 1.0 / 10000.0 ** (jnp.arange(half, dtype=jnp.float32) / half)
            ang = jnp.arange(L, dtype=jnp.float32)[:, None] * inv
            cos = jnp.cos(ang)[None, :, None, :]
            sin = jnp.sin(ang)[None, :, None, :]
            x1, x2 = (x[..., :half], x[..., half:])
            return jnp.concatenate([x1 * cos - x2 * sin, x1 * sin + x2 * cos], axis=-1)

        def _ln(x, eps=1e-05):
            m = jnp.mean(x, axis=-1, keepdims=True)
            v = jnp.var(x, axis=-1, keepdims=True)
            return (x - m) * jax.lax.rsqrt(v + eps)

        def _adaln(x, emb, w, b):
            gb = emb[:, 0, :] @ w.T + b
            g, be = jnp.split(gb, 2, axis=-1)
            return _ln(x) * (1.0 + g[:, None, :]) + be[:, None, :]

        def _attn(q, k, v, mask):
            scores = jnp.einsum('bqhd,bkhd->bhqk', q, k) / np.float32(np.sqrt(HD))
            scores = jnp.where(mask[:, None, None, :], jnp.float32(-jnp.inf), scores)
            w = jax.nn.softmax(scores, axis=-1)
            return jnp.einsum('bhqk,bkhd->bqhd', w, v)
        key = jax.random.key(seed)
        ks = jax.random.split(key, 20)
        B, L, LC = (4, 128, 64)
        s = 0.02
        inp = {'x': jax.random.normal(ks[0], (B, L, D), jnp.float32), 'noise_emb': jax.random.normal(ks[1], (B, 1, D), jnp.float32), 'context': jax.random.normal(ks[2], (B, LC, D), jnp.float32), 'src_mask': jnp.zeros((B, L), bool), 'ctx_mask': jnp.zeros((B, LC), bool), 'n1_w': jax.random.normal(ks[3], (NL, 2 * D, D), jnp.float32) * s, 'n1_b': jnp.zeros((NL, 2 * D), jnp.float32), 'n2_w': jax.random.normal(ks[4], (NL, 2 * D, D), jnp.float32) * s, 'n2_b': jnp.zeros((NL, 2 * D), jnp.float32), 'n3_w': jax.random.normal(ks[5], (NL, 2 * D, D), jnp.float32) * s, 'n3_b': jnp.zeros((NL, 2 * D), jnp.float32), 'qkv_w': jax.random.normal(ks[6], (NL, 3 * D, D), jnp.float32) * s, 'so_w': jax.random.normal(ks[7], (NL, D, D), jnp.float32) * s, 'cq_w': jax.random.normal(ks[8], (NL, D, D), jnp.float32) * s, 'ck_w': jax.random.normal(ks[9], (NL, D, D), jnp.float32) * s, 'cv_w': jax.random.normal(ks[10], (NL, D, D), jnp.float32) * s, 'co_w': jax.random.normal(ks[11], (NL, D, D), jnp.float32) * s, 'f1_w': jax.random.normal(ks[12], (NL, DFF, D), jnp.float32) * s, 'f1_b': jnp.zeros((NL, DFF), jnp.float32), 'f2_w': jax.random.normal(ks[13], (NL, D, DFF), jnp.float32) * s, 'f2_b': jnp.zeros((NL, D), jnp.float32)}
        return inp
    _L3_xcond_all = _L3_xcond_setup()
    _L3_xcond_in = {k: v for k, v in _L3_xcond_all.items() if k in ('n1_w', 'n1_b', 'n2_w', 'n2_b', 'n3_w', 'n3_b', 'qkv_w', 'so_w', 'cq_w', 'ck_w', 'cv_w', 'co_w', 'f1_w', 'f1_b', 'f2_w', 'f2_b')}
    del _L3_xcond_all

    def _L3_ffn_setup():
        import jax, jax.numpy as jnp
        import numpy as np
        EPS = 1e-06
        LN_EPS = 1e-05

        def _absmean_core(W):
            gamma = jnp.mean(jnp.abs(W)) + EPS
            Ws = W / gamma
            Wq = jnp.sign(Ws) * jnp.minimum(jnp.round(jnp.abs(Ws)), 1.0)
            return (Wq, gamma)

        @jax.custom_vjp
        def absmean(W):
            return _absmean_core(W)[0]

        def _absmean_fwd(W):
            Wq, gamma = _absmean_core(W)
            return (Wq, gamma)

        def _absmean_bwd(gamma, g):
            return (g / gamma,)
        absmean.defvjp(_absmean_fwd, _absmean_bwd)

        def layernorm(x, w, b, eps=LN_EPS):
            mu = jnp.mean(x, axis=-1, keepdims=True)
            var = jnp.mean((x - mu) ** 2, axis=-1, keepdims=True)
            return (x - mu) * jax.lax.rsqrt(var + eps) * w + b
        key = jax.random.key(seed)
        k1, k2, k3 = jax.random.split(key, 3)
        d, h = (128, 512)
        B, T = (8, 256)
        return {'x': jax.random.normal(k1, (B, T, d), jnp.float32), 'W_fc': jax.random.normal(k2, (h, d), jnp.float32), 'ln_w': jnp.ones((h,), jnp.float32), 'ln_b': jnp.zeros((h,), jnp.float32), 'W_proj': jax.random.normal(k3, (d, h), jnp.float32)}
    _L3_ffn_all = _L3_ffn_setup()
    _L3_ffn_in = {k: v for k, v in _L3_ffn_all.items() if k in ('W_fc', 'ln_w', 'ln_b', 'W_proj')}
    del _L3_ffn_all
    return {'x': x, 'cond_1024': cond_1024, 'ctx_1024': ctx_1024, 'mask_BxS_bf0': mask_BxS_bf0, 'mask_BxS2_bf0': mask_BxS2_bf0, 'L0_xcond_q_mu': _L0_xcond_in['q_mu'], 'L0_xcond_q_logsig': _L0_xcond_in['q_logsig'], 'L0_xcond_lnkv_g': _L0_xcond_in['lnkv_g'], 'L0_xcond_lnkv_b': _L0_xcond_in['lnkv_b'], 'L0_xcond_lnq_g': _L0_xcond_in['lnq_g'], 'L0_xcond_lnq_b': _L0_xcond_in['lnq_b'], 'L0_xcond_lnm_g': _L0_xcond_in['lnm_g'], 'L0_xcond_lnm_b': _L0_xcond_in['lnm_b'], 'L0_xcond_lnp_g': _L0_xcond_in['lnp_g'], 'L0_xcond_lnp_b': _L0_xcond_in['lnp_b'], 'L0_xcond_wk': _L0_xcond_in['wk'], 'L0_xcond_bk': _L0_xcond_in['bk'], 'L0_xcond_wv': _L0_xcond_in['wv'], 'L0_xcond_bv': _L0_xcond_in['bv'], 'L0_xcond_wq': _L0_xcond_in['wq'], 'L0_xcond_bq': _L0_xcond_in['bq'], 'L0_xcond_wu': _L0_xcond_in['wu'], 'L0_xcond_bu': _L0_xcond_in['bu'], 'L0_xcond_w1': _L0_xcond_in['w1'], 'L0_xcond_b1': _L0_xcond_in['b1'], 'L0_xcond_w2': _L0_xcond_in['w2'], 'L0_xcond_b2': _L0_xcond_in['b2'], 'L0_ffn_Wq': _L0_ffn_in['Wq'], 'L0_ffn_bq': _L0_ffn_in['bq'], 'L0_ffn_bn_gamma': _L0_ffn_in['bn_gamma'], 'L0_ffn_bn_beta': _L0_ffn_in['bn_beta'], 'L0_ffn_sub_key0': _L0_ffn_in['sub_key0'], 'L0_ffn_sub_key1': _L0_ffn_in['sub_key1'], 'L0_ffn_expert_down': _L0_ffn_in['expert_down'], 'L0_ffn_expert_up': _L0_ffn_in['expert_up'], 'L1_xcond_attn1_wq': _L1_xcond_in['attn1_wq'], 'L1_xcond_attn1_wk': _L1_xcond_in['attn1_wk'], 'L1_xcond_attn1_wv': _L1_xcond_in['attn1_wv'], 'L1_xcond_attn1_wo': _L1_xcond_in['attn1_wo'], 'L1_xcond_attn1_bo': _L1_xcond_in['attn1_bo'], 'L1_xcond_attn2_wq': _L1_xcond_in['attn2_wq'], 'L1_xcond_attn2_wk': _L1_xcond_in['attn2_wk'], 'L1_xcond_attn2_wv': _L1_xcond_in['attn2_wv'], 'L1_xcond_attn2_wo': _L1_xcond_in['attn2_wo'], 'L1_xcond_attn2_bo': _L1_xcond_in['attn2_bo'], 'L1_xcond_ff_w1': _L1_xcond_in['ff_w1'], 'L1_xcond_ff_b1': _L1_xcond_in['ff_b1'], 'L1_xcond_ff_w2': _L1_xcond_in['ff_w2'], 'L1_xcond_ff_b2': _L1_xcond_in['ff_b2'], 'L1_xcond_norm1_w': _L1_xcond_in['norm1_w'], 'L1_xcond_norm1_b': _L1_xcond_in['norm1_b'], 'L1_xcond_norm2_w': _L1_xcond_in['norm2_w'], 'L1_xcond_norm2_b': _L1_xcond_in['norm2_b'], 'L1_xcond_norm3_w': _L1_xcond_in['norm3_w'], 'L1_xcond_norm3_b': _L1_xcond_in['norm3_b'], 'L1_ffn_W_qkv': _L1_ffn_in['W_qkv'], 'L1_ffn_b_qkv': _L1_ffn_in['b_qkv'], 'L1_ffn_W_gate': _L1_ffn_in['W_gate'], 'L1_ffn_b_gate': _L1_ffn_in['b_gate'], 'L1_ffn_W_experts': _L1_ffn_in['W_experts'], 'L1_ffn_b_experts': _L1_ffn_in['b_experts'], 'L2_xcond_W': _L2_xcond_in['W'], 'L2_xcond_kernel': _L2_xcond_in['kernel'], 'L2_xcond_recurrent_kernel': _L2_xcond_in['recurrent_kernel'], 'L2_xcond_bias': _L2_xcond_in['bias'], 'L2_ffn_gate_w': _L2_ffn_in['gate_w'], 'L2_ffn_gate_b': _L2_ffn_in['gate_b'], 'L2_ffn_w1': _L2_ffn_in['w1'], 'L2_ffn_b1': _L2_ffn_in['b1'], 'L2_ffn_w2': _L2_ffn_in['w2'], 'L2_ffn_b2': _L2_ffn_in['b2'], 'L3_xcond_n1_w': _L3_xcond_in['n1_w'], 'L3_xcond_n1_b': _L3_xcond_in['n1_b'], 'L3_xcond_n2_w': _L3_xcond_in['n2_w'], 'L3_xcond_n2_b': _L3_xcond_in['n2_b'], 'L3_xcond_n3_w': _L3_xcond_in['n3_w'], 'L3_xcond_n3_b': _L3_xcond_in['n3_b'], 'L3_xcond_qkv_w': _L3_xcond_in['qkv_w'], 'L3_xcond_so_w': _L3_xcond_in['so_w'], 'L3_xcond_cq_w': _L3_xcond_in['cq_w'], 'L3_xcond_ck_w': _L3_xcond_in['ck_w'], 'L3_xcond_cv_w': _L3_xcond_in['cv_w'], 'L3_xcond_co_w': _L3_xcond_in['co_w'], 'L3_xcond_f1_w': _L3_xcond_in['f1_w'], 'L3_xcond_f1_b': _L3_xcond_in['f1_b'], 'L3_xcond_f2_w': _L3_xcond_in['f2_w'], 'L3_xcond_f2_b': _L3_xcond_in['f2_b'], 'L3_ffn_W_fc': _L3_ffn_in['W_fc'], 'L3_ffn_ln_w': _L3_ffn_in['ln_w'], 'L3_ffn_ln_b': _L3_ffn_in['ln_b'], 'L3_ffn_W_proj': _L3_ffn_in['W_proj']}

def reference(x, cond_1024, ctx_1024, mask_BxS_bf0, mask_BxS2_bf0, L0_xcond_q_mu, L0_xcond_q_logsig, L0_xcond_lnkv_g, L0_xcond_lnkv_b, L0_xcond_lnq_g, L0_xcond_lnq_b, L0_xcond_lnm_g, L0_xcond_lnm_b, L0_xcond_lnp_g, L0_xcond_lnp_b, L0_xcond_wk, L0_xcond_bk, L0_xcond_wv, L0_xcond_bv, L0_xcond_wq, L0_xcond_bq, L0_xcond_wu, L0_xcond_bu, L0_xcond_w1, L0_xcond_b1, L0_xcond_w2, L0_xcond_b2, L0_ffn_Wq, L0_ffn_bq, L0_ffn_bn_gamma, L0_ffn_bn_beta, L0_ffn_sub_key0, L0_ffn_sub_key1, L0_ffn_expert_down, L0_ffn_expert_up, L1_xcond_attn1_wq, L1_xcond_attn1_wk, L1_xcond_attn1_wv, L1_xcond_attn1_wo, L1_xcond_attn1_bo, L1_xcond_attn2_wq, L1_xcond_attn2_wk, L1_xcond_attn2_wv, L1_xcond_attn2_wo, L1_xcond_attn2_bo, L1_xcond_ff_w1, L1_xcond_ff_b1, L1_xcond_ff_w2, L1_xcond_ff_b2, L1_xcond_norm1_w, L1_xcond_norm1_b, L1_xcond_norm2_w, L1_xcond_norm2_b, L1_xcond_norm3_w, L1_xcond_norm3_b, L1_ffn_W_qkv, L1_ffn_b_qkv, L1_ffn_W_gate, L1_ffn_b_gate, L1_ffn_W_experts, L1_ffn_b_experts, L2_xcond_W, L2_xcond_kernel, L2_xcond_recurrent_kernel, L2_xcond_bias, L2_ffn_gate_w, L2_ffn_gate_b, L2_ffn_w1, L2_ffn_b1, L2_ffn_w2, L2_ffn_b2, L3_xcond_n1_w, L3_xcond_n1_b, L3_xcond_n2_w, L3_xcond_n2_b, L3_xcond_n3_w, L3_xcond_n3_b, L3_xcond_qkv_w, L3_xcond_so_w, L3_xcond_cq_w, L3_xcond_ck_w, L3_xcond_cv_w, L3_xcond_co_w, L3_xcond_f1_w, L3_xcond_f1_b, L3_xcond_f2_w, L3_xcond_f2_b, L3_ffn_W_fc, L3_ffn_ln_w, L3_ffn_ln_b, L3_ffn_W_proj):
    import jax
    import jax.numpy as jnp

    def _L0_xcond_ref(x_cls, x, noise, q_mu, q_logsig, lnkv_g, lnkv_b, lnq_g, lnq_b, lnm_g, lnm_b, lnp_g, lnp_b, wk, bk, wv, bv, wq, bq, wu, bu, w1, b1, w2, b2):
        import jax, jax.numpy as jnp
        import numpy as np
        B, N, K, D, T = (16, 512, 16, 128, 3)
        EPS_ATTN = 1e-08
        LN_EPS = 1e-05

        def _ln(x, g, b):
            mu = jnp.mean(x, axis=-1, keepdims=True)
            var = jnp.mean(jnp.square(x - mu), axis=-1, keepdims=True)
            return (x - mu) * jax.lax.rsqrt(var + LN_EPS) * g + b
        scale = D ** (-0.5)
        x_in = _ln(x, lnkv_g, lnkv_b)
        k = x_in @ wk + bk
        v = x_in @ wv + bv
        slots = q_mu + jnp.exp(q_logsig) * noise
        for _ in range(T):
            prev = slots
            q = _ln(slots, lnq_g, lnq_b) @ wq + bq
            logits = jnp.einsum('bnd,bkd->bnk', k, q) / scale
            attn = jax.nn.softmax(logits, axis=-1) + EPS_ATTN
            attn = attn / jnp.sum(attn, axis=1, keepdims=True)
            upd = jnp.einsum('bnk,bnd->bkd', attn, v)
            slots = upd @ wu + bu + prev
            h = _ln(slots, lnm_g, lnm_b) @ w1 + b1
            slots = jax.nn.gelu(h, approximate=False) @ w2 + b2 + slots
            slots = _ln(slots + x_cls[:, None, :], lnp_g, lnp_b)
        return slots

    def _L0_ffn_ref(hidden_states, Wq, bq, bn_gamma, bn_beta, sub_key0, sub_key1, expert_down, expert_up):
        import jax, jax.numpy as jnp
        import numpy as np
        H = 8
        QD = 32
        HALF = QD // 2
        DIMS = (32, 32)
        TOPK = 16
        DTK = 4
        EPS_BN = 1e-05
        EPS_NORM = 1e-12

        def _l2norm(x):
            n = jnp.linalg.norm(x, axis=-1, keepdims=True)
            return x / jnp.maximum(n, EPS_NORM)
        B, S, D = hidden_states.shape
        q = (hidden_states @ Wq + bq).reshape(B, S, H, QD)
        mean = q.mean(axis=(0, 1, 2))
        var = q.var(axis=(0, 1, 2))
        q = (q - mean) / jnp.sqrt(var + EPS_BN) * bn_gamma + bn_beta
        q0 = _l2norm(q[..., :HALF])
        q1 = _l2norm(q[..., HALF:])
        k0 = _l2norm(sub_key0)
        k1 = _l2norm(sub_key1)
        s0 = jnp.einsum('bshq,kq->bshk', q0, k0)
        s1 = jnp.einsum('bshq,kq->bshk', q1, k1)
        ts0, ti0 = jax.lax.top_k(s0, DTK)
        ts1, ti1 = jax.lax.top_k(s1, DTK)
        comb_s = (ts0[..., :, None] + ts1[..., None, :]).reshape(B, S, H, DTK * DTK)
        comb_i = (ti0[..., :, None] * DIMS[1] + ti1[..., None, :]).reshape(B, S, H, DTK * DTK)
        top_s, pos = jax.lax.top_k(comb_s, TOPK)
        idx = jnp.take_along_axis(comb_i, pos, axis=-1)
        w = jax.nn.softmax(top_s, axis=-1)
        down = expert_down[idx]
        up = expert_up[idx]
        eh = jnp.einsum('bshkd,bsd->bshk', down, hidden_states)
        eh = jax.nn.gelu(eh, approximate=False)
        out = jnp.einsum('bshko,bshk->bso', up, eh * w)
        return out

    def _L1_xcond_ref(x, t, context, attn1_wq, attn1_wk, attn1_wv, attn1_wo, attn1_bo, attn2_wq, attn2_wk, attn2_wv, attn2_wo, attn2_bo, ff_w1, ff_b1, ff_w2, ff_b2, norm1_w, norm1_b, norm2_w, norm2_b, norm3_w, norm3_b):
        import jax, jax.numpy as jnp
        import numpy as np
        import math
        B, S, CTX, D, H, DH = (2, 256, 32, 128, 16, 64)
        INNER = H * DH
        DFF = 4 * D

        def layernorm(x, eps=1e-05):
            m = jnp.mean(x, axis=-1, keepdims=True)
            v = jnp.var(x, axis=-1, keepdims=True)
            return (x - m) * jax.lax.rsqrt(v + eps)

        def adaln(x, t, w, b):
            emb = t @ w + b
            scale, shift = jnp.split(emb, 2, axis=-1)
            return layernorm(x) * (1.0 + scale) + shift

        def mha(xq, ctx, wq, wk, wv, wo, bo):
            b, sq, _ = xq.shape
            sk = ctx.shape[1]
            q = (xq @ wq).reshape(b, sq, H, DH).transpose(0, 2, 1, 3)
            k = (ctx @ wk).reshape(b, sk, H, DH).transpose(0, 2, 1, 3)
            v = (ctx @ wv).reshape(b, sk, H, DH).transpose(0, 2, 1, 3)
            scores = jnp.einsum('bhqd,bhkd->bhqk', q, k) / math.sqrt(DH)
            attn = jax.nn.softmax(scores, axis=-1)
            out = jnp.einsum('bhqk,bhkd->bhqd', attn, v)
            out = out.transpose(0, 2, 1, 3).reshape(b, sq, INNER)
            return out @ wo + bo

        def glu_ff(x, w1, b1, w2, b2):
            u = x @ w1 + b1
            a, gate = jnp.split(u, 2, axis=-1)
            return a * jax.nn.gelu(gate, approximate=False) @ w2 + b2
        h1 = adaln(x, t, norm1_w, norm1_b)
        x = mha(h1, h1, attn1_wq, attn1_wk, attn1_wv, attn1_wo, attn1_bo) + x
        h2 = adaln(x, t, norm2_w, norm2_b)
        x = mha(h2, context, attn2_wq, attn2_wk, attn2_wv, attn2_wo, attn2_bo) + x
        h3 = adaln(x, t, norm3_w, norm3_b)
        x = glu_ff(h3, ff_w1, ff_b1, ff_w2, ff_b2) + x
        return x

    def _L1_ffn_ref(x, W_qkv, b_qkv, W_gate, b_gate, W_experts, b_experts):
        import jax, jax.numpy as jnp
        import numpy as np
        NUM_HEADS = 16
        TOP_K = 2
        B, S, D = x.shape
        H = NUM_HEADS
        hd = D // H
        E = W_gate.shape[-1]
        qkv = (x @ W_qkv + b_qkv).reshape(B, S, 3, H, hd)
        q, k, v = (qkv[:, :, 0], qkv[:, :, 1], qkv[:, :, 2])
        attn = jnp.einsum('bqhd,bkhd->bhqk', q, k) / jnp.sqrt(jnp.asarray(hd, x.dtype))
        attn = jax.nn.softmax(attn, axis=-1)
        attn_out = jnp.einsum('bhqk,bkhd->bqhd', attn, v).reshape(B, S, D)
        gate = jax.nn.softmax(x @ W_gate + b_gate, axis=-1)
        top_g, top_i = jax.lax.top_k(gate, TOP_K)
        combine = jnp.sum(jax.nn.one_hot(top_i, E, dtype=x.dtype) * top_g[..., None], axis=2)
        expert_out = jnp.einsum('bsd,edf->bsef', x, W_experts) + b_experts
        moe_out = jnp.einsum('bsef,bse->bsf', expert_out, combine)
        return attn_out + moe_out

    def _L2_xcond_ref(dec_seq, enc_hiddens, last_hidden, W, kernel, recurrent_kernel, bias):
        import jax, jax.numpy as jnp
        import numpy as np
        B, T, S, H, E = (32, 64, 64, 128, 128)
        Hd = last_hidden.shape[-1]

        def step(h, x_t):
            proj = h @ W
            score = jnp.einsum('bsh,bh->bs', enc_hiddens, proj)
            attn = jax.nn.softmax(score, axis=-1)
            context = jnp.einsum('bs,bsh->bh', attn, enc_hiddens)
            inp = jnp.concatenate([x_t, context], axis=-1)
            gx = inp @ kernel + bias
            gh = h @ recurrent_kernel
            xz, xr, xh = (gx[:, :Hd], gx[:, Hd:2 * Hd], gx[:, 2 * Hd:])
            hz, hr, hh = (gh[:, :Hd], gh[:, Hd:2 * Hd], gh[:, 2 * Hd:])
            z = jax.nn.sigmoid(xz + hz)
            r = jax.nn.sigmoid(xr + hr)
            cand = jnp.tanh(xh + r * hh)
            h_new = z * h + (1.0 - z) * cand
            return (h_new, h_new)
        xs = jnp.swapaxes(dec_seq, 0, 1)
        _, outs = jax.lax.scan(step, last_hidden, xs)
        return jnp.swapaxes(outs, 0, 1)

    def _L2_ffn_ref(x, gate_w, gate_b, w1, b1, w2, b2):
        import jax, jax.numpy as jnp
        import numpy as np
        HIDDEN = 128
        FFN = 4 * HIDDEN
        NUM_EXPERTS = 8
        TOP_K = 2
        B, S = (4, 256)
        b, s, h = x.shape
        xt = x.reshape(b * s, h)
        probs = jax.nn.softmax(xt @ gate_w + gate_b, axis=-1)
        _, idx = jax.lax.top_k(probs, TOP_K)
        one_hot = jax.nn.one_hot(idx, NUM_EXPERTS, dtype=xt.dtype)
        mask = (one_hot.sum(axis=1) > 0).astype(xt.dtype)
        h1 = jax.nn.relu(jnp.einsum('th,ehf->etf', xt, w1) + b1[:, None, :])
        out_e = jnp.einsum('etf,efh->eth', h1, w2) + b2[:, None, :]
        out = jnp.einsum('eth,te->th', out_e, mask)
        return out.reshape(b, s, h)

    def _L3_xcond_ref(x, noise_emb, context, src_mask, ctx_mask, n1_w, n1_b, n2_w, n2_b, n3_w, n3_b, qkv_w, so_w, cq_w, ck_w, cv_w, co_w, f1_w, f1_b, f2_w, f2_b):
        import jax, jax.numpy as jnp
        import numpy as np
        NL, D, H, DFF = (6, 128, 16, 512)
        HD = D // H

        def _rope(x):
            L = x.shape[1]
            half = HD // 2
            inv = 1.0 / 10000.0 ** (jnp.arange(half, dtype=jnp.float32) / half)
            ang = jnp.arange(L, dtype=jnp.float32)[:, None] * inv
            cos = jnp.cos(ang)[None, :, None, :]
            sin = jnp.sin(ang)[None, :, None, :]
            x1, x2 = (x[..., :half], x[..., half:])
            return jnp.concatenate([x1 * cos - x2 * sin, x1 * sin + x2 * cos], axis=-1)

        def _ln(x, eps=1e-05):
            m = jnp.mean(x, axis=-1, keepdims=True)
            v = jnp.var(x, axis=-1, keepdims=True)
            return (x - m) * jax.lax.rsqrt(v + eps)

        def _adaln(x, emb, w, b):
            gb = emb[:, 0, :] @ w.T + b
            g, be = jnp.split(gb, 2, axis=-1)
            return _ln(x) * (1.0 + g[:, None, :]) + be[:, None, :]

        def _attn(q, k, v, mask):
            scores = jnp.einsum('bqhd,bkhd->bhqk', q, k) / np.float32(np.sqrt(HD))
            scores = jnp.where(mask[:, None, None, :], jnp.float32(-jnp.inf), scores)
            w = jax.nn.softmax(scores, axis=-1)
            return jnp.einsum('bhqk,bkhd->bqhd', w, v)
        B, L, _ = x.shape
        LC = context.shape[1]
        for i in range(NL):
            xn = _adaln(x, noise_emb, n1_w[i], n1_b[i])
            qkv = xn @ qkv_w[i].T
            q, k, v = jnp.split(qkv, 3, axis=-1)
            q = _rope(q.reshape(B, L, H, HD))
            k = _rope(k.reshape(B, L, H, HD))
            v = v.reshape(B, L, H, HD)
            a = _attn(q, k, v, src_mask).reshape(B, L, D) @ so_w[i].T
            x = x + a
            xn = _adaln(x, noise_emb, n2_w[i], n2_b[i])
            q = _rope((xn @ cq_w[i].T).reshape(B, L, H, HD))
            k = _rope((context @ ck_w[i].T).reshape(B, LC, H, HD))
            v = (context @ cv_w[i].T).reshape(B, LC, H, HD)
            a = _attn(q, k, v, ctx_mask).reshape(B, L, D) @ co_w[i].T
            x = x + a
            xn = _adaln(x, noise_emb, n3_w[i], n3_b[i])
            h = jax.nn.gelu(xn @ f1_w[i].T + f1_b[i], approximate=False)
            x = x + (h @ f2_w[i].T + f2_b[i])
        return x

    def _L3_ffn_ref(x, W_fc, ln_w, ln_b, W_proj):
        import jax, jax.numpy as jnp
        import numpy as np
        EPS = 1e-06
        LN_EPS = 1e-05

        def _absmean_core(W):
            gamma = jnp.mean(jnp.abs(W)) + EPS
            Ws = W / gamma
            Wq = jnp.sign(Ws) * jnp.minimum(jnp.round(jnp.abs(Ws)), 1.0)
            return (Wq, gamma)

        @jax.custom_vjp
        def absmean(W):
            return _absmean_core(W)[0]

        def _absmean_fwd(W):
            Wq, gamma = _absmean_core(W)
            return (Wq, gamma)

        def _absmean_bwd(gamma, g):
            return (g / gamma,)
        absmean.defvjp(_absmean_fwd, _absmean_bwd)

        def layernorm(x, w, b, eps=LN_EPS):
            mu = jnp.mean(x, axis=-1, keepdims=True)
            var = jnp.mean((x - mu) ** 2, axis=-1, keepdims=True)
            return (x - mu) * jax.lax.rsqrt(var + eps) * w + b
        h = jnp.einsum('btd,hd->bth', x, absmean(W_fc))
        h = jax.nn.gelu(h, approximate=False)
        h = layernorm(h, ln_w, ln_b)
        return jnp.einsum('bth,dh->btd', h, absmean(W_proj))
    x = x + _L0_xcond_ref(cond_1024, ctx_1024, _layernorm(x, axis=-1), L0_xcond_q_mu, L0_xcond_q_logsig, L0_xcond_lnkv_g, L0_xcond_lnkv_b, L0_xcond_lnq_g, L0_xcond_lnq_b, L0_xcond_lnm_g, L0_xcond_lnm_b, L0_xcond_lnp_g, L0_xcond_lnp_b, L0_xcond_wk, L0_xcond_bk, L0_xcond_wv, L0_xcond_bv, L0_xcond_wq, L0_xcond_bq, L0_xcond_wu, L0_xcond_bu, L0_xcond_w1, L0_xcond_b1, L0_xcond_w2, L0_xcond_b2)
    x = x + _L0_ffn_ref(_layernorm(x, axis=-1), L0_ffn_Wq, L0_ffn_bq, L0_ffn_bn_gamma, L0_ffn_bn_beta, L0_ffn_sub_key0, L0_ffn_sub_key1, L0_ffn_expert_down, L0_ffn_expert_up)
    x = x + _L1_xcond_ref(_layernorm(x, axis=-1), cond_1024[:, None, :], ctx_1024, L1_xcond_attn1_wq, L1_xcond_attn1_wk, L1_xcond_attn1_wv, L1_xcond_attn1_wo, L1_xcond_attn1_bo, L1_xcond_attn2_wq, L1_xcond_attn2_wk, L1_xcond_attn2_wv, L1_xcond_attn2_wo, L1_xcond_attn2_bo, L1_xcond_ff_w1, L1_xcond_ff_b1, L1_xcond_ff_w2, L1_xcond_ff_b2, L1_xcond_norm1_w, L1_xcond_norm1_b, L1_xcond_norm2_w, L1_xcond_norm2_b, L1_xcond_norm3_w, L1_xcond_norm3_b)
    x = x + _L1_ffn_ref(_layernorm(x, axis=-1), L1_ffn_W_qkv, L1_ffn_b_qkv, L1_ffn_W_gate, L1_ffn_b_gate, L1_ffn_W_experts, L1_ffn_b_experts)
    x = x + _L2_xcond_ref(_layernorm(x, axis=-1), ctx_1024, cond_1024, L2_xcond_W, L2_xcond_kernel, L2_xcond_recurrent_kernel, L2_xcond_bias)
    x = x + _L2_ffn_ref(_layernorm(x, axis=-1), L2_ffn_gate_w, L2_ffn_gate_b, L2_ffn_w1, L2_ffn_b1, L2_ffn_w2, L2_ffn_b2)
    x = x + _L3_xcond_ref(_layernorm(x, axis=-1), cond_1024[:, None, :], ctx_1024, mask_BxS_bf0, mask_BxS2_bf0, L3_xcond_n1_w, L3_xcond_n1_b, L3_xcond_n2_w, L3_xcond_n2_b, L3_xcond_n3_w, L3_xcond_n3_b, L3_xcond_qkv_w, L3_xcond_so_w, L3_xcond_cq_w, L3_xcond_ck_w, L3_xcond_cv_w, L3_xcond_co_w, L3_xcond_f1_w, L3_xcond_f1_b, L3_xcond_f2_w, L3_xcond_f2_b)
    x = x + _L3_ffn_ref(_layernorm(x, axis=-1), L3_ffn_W_fc, L3_ffn_ln_w, L3_ffn_ln_b, L3_ffn_W_proj)
    return x

_drawn_inputs = setup_inputs


def setup_inputs(seed=0):
    import zlib

    import numpy as np

    out = dict(_drawn_inputs(seed))
    spreads = {'L0_xcond_lnkv_g': (1.0, 0.6),
     'L0_xcond_lnkv_b': (0.0, 0.8),
     'L0_xcond_lnq_g': (1.0, 0.6),
     'L0_xcond_lnq_b': (0.0, 0.8),
     'L0_xcond_lnm_g': (1.0, 0.6),
     'L0_xcond_lnm_b': (0.0, 0.8),
     'L0_xcond_lnp_g': (1.0, 0.2),
     'L0_xcond_lnp_b': (0.0, 0.1),
     'L0_xcond_bk': (0.0, 0.8),
     'L0_xcond_bv': (0.0, 0.514),
     'L0_xcond_bq': (0.0, 0.8),
     'L0_xcond_bu': (0.0, 0.1),
     'L0_xcond_b1': (0.0, 0.8),
     'L0_xcond_b2': (0.0, 0.1),
     'L0_ffn_bq': (0.0, 0.8),
     'L0_ffn_bn_gamma': (1.0, 0.6),
     'L0_ffn_bn_beta': (0.0, 0.8),
     'L1_ffn_b_qkv': (0.0, 0.356),
     'L1_ffn_b_gate': (0.0, 0.8),
     'L1_ffn_b_experts': (0.0, 0.8),
     'L2_xcond_bias': (0.0, 0.408),
     'L2_ffn_gate_b': (0.0, 0.271),
     'L2_ffn_b1': (0.0, 0.8),
     'L2_ffn_b2': (0.0, 0.1),
     'L3_xcond_n1_b': (0.0, 0.8),
     'L3_xcond_n2_b': (0.0, 0.8),
     'L3_xcond_n3_b': (0.0, 0.8),
     'L3_xcond_f1_b': (0.0, 0.745),
     'L3_xcond_f2_b': (0.0, 0.1),
     'L3_ffn_ln_w': (1.0, 0.2),
     'L3_ffn_ln_b': (0.0, 0.1)}
    factors = {'L0_xcond_q_logsig': 8.0,
     'L0_xcond_wk': 4.135,
     'L0_xcond_wq': 4.212,
     'L0_xcond_w1': 2.978,
     'L0_xcond_w2': 2.724,
     'L0_ffn_Wq': 8.0,
     'L0_ffn_sub_key0': 8.0,
     'L0_ffn_sub_key1': 8.0,
     'L0_ffn_expert_down': 4.637,
     'L0_ffn_expert_up': 6.157,
     'L1_xcond_attn1_bo': 8.0,
     'L1_xcond_attn2_bo': 8.0,
     'L1_xcond_ff_b1': 8.0,
     'L1_xcond_ff_b2': 8.0,
     'L1_xcond_norm1_b': 5.851,
     'L1_xcond_norm2_b': 8.0,
     'L1_xcond_norm3_b': 8.0,
     'L1_ffn_W_gate': 5.495,
     'L1_ffn_W_experts': 4.968,
     'L2_xcond_W': 7.476,
     'L2_xcond_recurrent_kernel': 8.0,
     'L2_ffn_w1': 3.162,
     'L3_xcond_n1_w': 8.0,
     'L3_xcond_n2_w': 8.0,
     'L3_xcond_n3_w': 7.423,
     'L3_xcond_cq_w': 8.0,
     'L3_xcond_ck_w': 8.0,
     'L3_xcond_cv_w': 4.852,
     'L3_xcond_co_w': 4.841}
    for name, (base, spread) in spreads.items():
        noise = np.random.default_rng([zlib.crc32(name.encode()), seed]).standard_normal(out[name].shape)
        drawn = base * np.exp(spread * noise) if base else spread * noise
        out[name] = jnp.asarray(drawn.astype(out[name].dtype))
    for name, factor in factors.items():
        out[name] = (out[name] * factor).astype(out[name].dtype)
    return out
```

```python
from contextlib import ExitStack

import numpy as np

import concourse.bass as bass
from concourse import mybir

SECTIONS = "ACDEFGHI"

F32 = mybir.dt.float32
U8 = mybir.dt.uint8
ALU = mybir.AluOpType
ACT = mybir.ActivationFunctionType
AX = mybir.AxisListType

B = 32
S = 128
D = 128
CL = 77
U = 4
NG = B // U
UC = U * CL
NH = 16
HD = D // NH
HL = 8
NU = U * NH // HL
SCORE, TURN, OUT = 0, 4, 6
LN_EPS = 1e-5
MASKED = -1e30
LAYERS = 6
FFN = 512
EXPERTS = 8

SIGNALS = [
    "loaded", "loaded_q", "stored", "vector_step", "scalar_step", "pool_step",
    "var_ready", "rstd_ready", "z_ready", "zT_done", "xnT_ready",
    "scores_done", "shifted", "exp_done", "turned", "pT_ready", "pv_done", "o_normed",
    "proj_done", "proj_read", "k_done", "k_read", "v_done", "v_read", "q_done", "q_read",
    "rope_done", "spread", "o_turned", "oT_ready", "mix_done", "mix_added",
    "hid_done", "hid_ready", "ffn_done", "ffn_added", "gate_done", "gate_ready",
    "upd_done", "upd_ready", "expert_done", "expert_ready", "x_ready", "gram_done",
    "saved", "table_ready", "outer_ready", "cand_ready",
]


class Steps:

    def __init__(self, eng, sem):
        self.eng, self.sem, self.n = eng, sem, 0

    def __call__(self, ins):
        ins.then_inc(self.sem, 1)
        self.n += 1
        self.eng.wait_ge(self.sem, self.n)


def build(nc, dram, out):
    with ExitStack() as ctx:
        def sb(name, shape, dt=F32, scope=ctx):
            return scope.enter_context(nc.sbuf_tensor(name, shape, dt))

        sem = {name: ctx.enter_context(nc.semaphore(name)) for name in SIGNALS}
        numbers = sorted(s.num for s in sem.values())
        all_signals = range(numbers[0], numbers[-1] + 1)
        assert len(numbers) == len(all_signals)

        def rest():
            nc.sync.sem_clear(all_signals)
            nc.all_engine_barrier()

        x_all = sb("x_all", [S, B, D])
        ctx_tm = sb("ctx_tm", [CL, B, D])
        ctxT = sb("ctxT", [D, B * CL])
        condT = sb("condT", [D, B])
        ident = sb("ident", [128, 128])
        ones = sb("ones", [128, 128])
        neghalf = sb("neghalf", [128, 64])
        zn = sb("zn", [128, U, D + 1])
        stats = sb("stats", [128, U, 6])
        mv = sb("mv", [128, U, 2])
        veps = sb("veps", [128, U])
        rstd = sb("rstd", [128, U])
        xnT = sb("xnT", [D, U * S])
        xs = sb("xs", [S, U, D])
        e = sb("e", [128, 2, HL * S])
        pT = sb("pT", [128, 2, HL, S])
        mx = sb("mx", [128, 2, HL])
        rec = sb("rec", [128, 2, HL])
        ps = ctx.enter_context(nc.psum_tensor("ps", [128, 8, 512], F32))

        def per(bank, n=D):
            return ps[:, bank, 0:U * n].rearrange("p (u d) -> p u d", u=U)

        def ln_vector(dve, step, r, src, dst=None, rows=128, n=U):
            dst = dst or (lambda u: zn[0:rows, u, 0:D])
            for u in range(n):
                last = nc.vector.bn_stats(stats[0:rows, u, :], src(u))
            step(last)
            for u in range(n):
                last = nc.vector.bn_aggr(mv[0:rows, u, :], stats[0:rows, u, :])
            step(last)
            nc.vector.tensor_scalar(veps[0:rows, 0:n], mv[0:rows, 0:n, 1], LN_EPS, None, ALU.add).then_inc(sem["var_ready"], 1)
            dve.wait_ge(sem["rstd_ready"], r + 1)
            for u in range(n):
                last = nc.vector.tensor_scalar(dst(u), src(u), mv[0:rows, u, 0:1], rstd[0:rows, u:u + 1],
                                               ALU.subtract, ALU.mult)
            return last

        def ln_pool(pool, r, rows=128, n=U):
            pool.wait_ge(sem["var_ready"], r + 1)
            nc.gpsimd.tensor_tensor(rstd[0:rows, 0:n], veps[0:rows, 0:n], neghalf[0:rows, 0:n],
                                    ALU.pow).then_inc(sem["rstd_ready"], 1)

        def turn_rows(pe, r, bank=0, rows=128):
            pe.wait_ge(sem["z_ready"], r + 1)
            for u in range(U):
                last = nc.tensor.transpose(ps[:, bank, u * rows:(u + 1) * rows], zn[0:rows, u, 0:D],
                                           ident[0:rows, 0:rows])
            last.then_inc(sem["zT_done"], 1)

        def slot_head(i, wide):
            return 2 * (i % 4) + i // 4 if wide else i

        def attn_tensor(pe, a, keys, wide, q_of, k_of, v_of):
            hd = D // 2 if wide else HD

            def scores(n):
                u, half = n // 2, n % 2
                if n >= 2:
                    pe.wait_ge(sem["shifted"], NU * a + n - 1)
                for slot in range(4):
                    for bank in range(2):
                        h = HL * half + slot_head(4 * bank + slot, wide)
                        last = nc.tensor.matmul(ps[:, SCORE + 2 * half + bank, slot * S:slot * S + keys],
                                                q_of(h, u), k_of(h, u), start=True, stop=True)
                last.then_inc(sem["scores_done"], 1)

            def turn(n):
                N = NU * a + n
                pe.wait_ge(sem["exp_done"], N + 1)
                if N >= 1:
                    pe.wait_ge(sem["pT_ready"], 2 * N)
                for i in range(HL):
                    last = nc.tensor.transpose(ps[0:keys, TURN + i // 4, (i % 4) * S:(i % 4 + 1) * S],
                                               e[:, n % 2, i * keys:(i + 1) * keys], ident[:, :])
                    if i % 4 == 3:
                        last.then_inc(sem["turned"], 1)

            def values(n):
                N, u, half = NU * a + n, n // 2, n % 2
                pe.wait_ge(sem["pT_ready"], 2 * N + 2)
                back = 1 if wide else 2
                if N >= back:
                    pe.wait_ge(sem["o_normed"], N + 1 - back)
                for i in range(HL):
                    hl = slot_head(i, wide)
                    last = nc.tensor.matmul(out_place(n, hl, wide), pT[0:keys, n % 2, i, :],
                                            v_of(HL * half + hl, u), start=True, stop=True)
                last.then_inc(sem["pv_done"], 1)

            scores(0)
            scores(1)
            for n in range(NU):
                turn(n)
                if n + 2 < NU:
                    scores(n + 2)
                values(n)

        def out_place(n, hl, wide):
            w = (D // 2 if wide else HD) + 1
            if wide:
                return ps[:, OUT + hl // 4, (hl % 4) * w:(hl % 4 + 1) * w]
            return ps[:, OUT + n % 2, hl * w:(hl + 1) * w]

        def attn_vector(dve, step, a, keys, wide, o_of):
            w = (D // 2 if wide else HD) + 1

            def shift(n):
                N, half = NU * a + n, n % 2
                view = ps[:, SCORE + 2 * half:SCORE + 2 * half + 2, :].rearrange(
                    "p b (s k) -> p (b s) k", s=4)[:, :, 0:keys]
                dve.wait_ge(sem["scores_done"], N + 1)
                m = mx[:, n % 2, :]
                step(nc.vector.tensor_reduce(m, view, AX.X, ALU.max))
                if N >= 2:
                    dve.wait_ge(sem["turned"], 2 * N - 2)
                nc.vector.tensor_tensor(
                    e[:, n % 2, 0:HL * keys].rearrange("p (h k) -> p h k", h=HL), view,
                    m.unsqueeze(2).broadcast_to([128, HL, keys]), ALU.subtract).then_inc(sem["shifted"], 1)

            def norm(n):
                N, u, half = NU * a + n, n // 2, n % 2
                dve.wait_ge(sem["pv_done"], N + 1)
                if wide:
                    p = ps[:, OUT:OUT + 2, 0:4 * w].rearrange("p b (h d) -> p b h d", d=w)
                    r = rec[:, n % 2, :].rearrange("p (b h) -> p b h", b=2)
                    step(nc.vector.reciprocal(r, p[:, :, :, w - 1]))
                    nc.vector.tensor_tensor(
                        o_of(u)[:, HL * half * (w - 1):HL * (half + 1) * (w - 1)].rearrange(
                            "p (b h d) -> p b h d", b=2, d=w - 1), p[:, :, :, 0:w - 1],
                        r.unsqueeze(3).broadcast_to([128, 2, 4, w - 1]), ALU.mult).then_inc(sem["o_normed"], 1)
                else:
                    p = ps[:, OUT + n % 2, 0:HL * w].rearrange("p (h d) -> p h d", d=w)
                    step(nc.vector.reciprocal(rec[:, n % 2, :], p[:, :, w - 1]))
                    nc.vector.tensor_tensor(
                        o_of(u)[:, HL * half * HD:HL * (half + 1) * HD].rearrange("p (h d) -> p h d", d=HD),
                        p[:, :, 0:HD], rec[:, n % 2, :].unsqueeze(2).broadcast_to([128, HL, HD]),
                        ALU.mult).then_inc(sem["o_normed"], 1)

            for n in range(NU):
                shift(n)
                if n >= 2:
                    norm(n - 2)
            norm(NU - 2)
            norm(NU - 1)

        def attn_scalar(act, a, keys, scale):
            def exponential(n):
                act.wait_ge(sem["shifted"], NU * a + n + 1)
                nc.scalar.activation(e[:, n % 2, 0:HL * keys], e[:, n % 2, 0:HL * keys], ACT.Exp,
                                     scale=scale).then_inc(sem["exp_done"], 1)

            exponential(0)
            for n in range(NU):
                N = NU * a + n
                if n + 1 < NU:
                    exponential(n + 1)
                if N >= 2:
                    act.wait_ge(sem["pv_done"], N - 1)
                for b in range(2):
                    act.wait_ge(sem["turned"], 2 * N + b + 1)
                    nc.scalar.activation(pT[0:keys, n % 2, 4 * b:4 * b + 4, :],
                                         ps[0:keys, TURN + b, :].rearrange("p (h s) -> p h s", h=4),
                                         ACT.Copy).then_inc(sem["pT_ready"], 1)

        with nc.Block() as block:
            @block.sync
            def _(sp):
                sp.dma_start(ident[:], dram["ident"]).then_inc(sem["loaded"], 16)
                sp.dma_start(ctx_tm[:], dram["ctx_1024"].rearrange("b t d -> t b d")).then_inc(sem["loaded"], 16)
                sp.dma_start(x_all[:], dram["x"].rearrange("b t d -> t b d")).then_inc(sem["loaded_q"], 16)
                sp.dma_start(condT[:], dram["condT"]).then_inc(sem["loaded_q"], 16)
                sp.wait_ge(sem["loaded_q"], 32)

            @block.vector
            def _(dve):
                nc.vector.memset(ones[:], 1.0)
                nc.vector.memset(neghalf[:], -0.5)
                nc.vector.memset(zn[:], 1.0)
                for b in range(B):
                    if b % U == U - 1:
                        g = b // U
                        dve.wait_ge(sem["zT_done"], g + 1)
                        nc.vector.tensor_copy(ctxT[:, g * UC:(g + 1) * UC],
                                              ps[:, g % 2, 0:UC]).then_inc(sem["xnT_ready"], 1)

            @block.tensor
            def _(pe):
                pe.wait_ge(sem["loaded"], 32)
                for g in range(NG):
                    if g >= 2:
                        pe.wait_ge(sem["xnT_ready"], g - 1)
                    for u in range(U):
                        last = nc.tensor.transpose(ps[:, g % 2, u * CL:(u + 1) * CL], ctx_tm[:, g * U + u, :],
                                                   ident[0:CL, 0:CL])
                    last.then_inc(sem["zT_done"], 1)
        rest()

        gram = sb("gram", [D, D + 1])
        def stage_slots():
            with ExitStack() as st:
                names = ["wk", "wv", "wq", "wu", "w1", "w2"]
                w = {n: sb("A_" + n, [D, D], scope=st) for n in names}
                cols = ["lnkv_g", "lnkv_b", "lnq_g", "lnq_b", "lnm_g", "lnm_b", "bk", "bv", "bq", "b1"]
                col = {n: sb("A_c_" + n, [D, 1], scope=st) for n in cols}
                wide = ["q_mu", "q_logsig", "lnp_g", "lnp_b"]
                row = {n: sb("A_r_" + n, [128, D], scope=st) for n in wide}
                bu = sb("A_bu", [1, D], scope=st)
                b2 = sb("A_b2", [1, D], scope=st)
                cond_bc = sb("A_cond", [128, B * D], scope=st)
                cT = sb("A_cT", [D, UC], scope=st)
                kT = sb("A_kT", [D, UC], scope=st)
                qT = sb("A_qT", [D, U * S], scope=st)
                v1 = sb("A_v1", [CL, U, D + 1], scope=st)
                attn = sb("A_attn", [CL, U, S], scope=st)
                am = sb("A_am", [CL, U], scope=st)
                ar = sb("A_ar", [CL, U], scope=st)
                ur = sb("A_ur", [128, U], scope=st)
                n_loads = len(names) + len(cols) + len(wide) + 3

                with nc.Block() as block:
                    @block.sync
                    def _(sp):
                        for n in names:
                            sp.dma_start(w[n][:], dram["L0_xcond_" + n]).then_inc(sem["loaded"], 16)
                        for n in cols:
                            sp.dma_start(col[n][:], dram["L0_xcond_" + n].unsqueeze(1)).then_inc(sem["loaded"], 16)
                        for n in wide:
                            src = dram["L0_xcond_" + n]
                            src = src.rearrange("a b d -> (a b d)") if n.startswith("q_") else src
                            sp.dma_start(row[n][:], src.partition_broadcast(128)).then_inc(sem["loaded"], 16)
                        sp.dma_start(bu[:], dram["L0_xcond_bu"].unsqueeze(0)).then_inc(sem["loaded"], 16)
                        sp.dma_start(b2[:], dram["L0_xcond_b2"].unsqueeze(0)).then_inc(sem["loaded"], 16)
                        sp.dma_start(cond_bc[:], dram["cond_1024"].rearrange("b d -> (b d)").partition_broadcast(128)).then_inc(sem["loaded"], 16)
                        sp.wait_ge(sem["loaded"], 16 * n_loads)

                    @block.scalar
                    def _(act):
                        act.wait_ge(sem["loaded"], 16 * n_loads)
                        nc.scalar.activation(row["q_logsig"][:], row["q_logsig"][:], ACT.Exp)

                    @block.vector
                    def _(dve):
                        nc.vector.memset(v1[:], 1.0)
                        nc.vector.memset(gram[:], 0.0)
                rest()

                def over(t):
                    return t[:].unsqueeze(1).broadcast_to([128, U, D])

                with nc.Fori(0, NG) as g:
                    with nc.Block() as block:
                        @block.vector
                        def _(dve):
                            step = Steps(dve, sem["vector_step"])
                            ln_vector(dve, step, 0, lambda u: ctx_tm[:, g * U + u, :], rows=CL).then_inc(sem["z_ready"], 1)
                            dve.wait_ge(sem["zT_done"], 1)
                            step(ln_vector(dve, step, 1, lambda u: x_all[:, g * U + u, :]))
                            step(nc.vector.tensor_tensor(xs[:], zn[:, :, 0:D], over(row["q_logsig"]), ALU.mult))
                            step(nc.vector.tensor_tensor(xs[:], xs[:], over(row["q_mu"]), ALU.add))
                            dve.wait_ge(sem["v_done"], 1)
                            nc.vector.tensor_copy(v1[:, :, 0:D], per(2)[0:CL]).then_inc(sem["v_read"], 1)
                            for it in range(3):
                                ln_vector(dve, step, 3 * it + 2, lambda u: xs[:, u, :]).then_inc(sem["z_ready"], 1)
                                dve.wait_ge(sem["scores_done"], it + 1)
                                step(nc.vector.tensor_reduce(am[:], per(2)[0:CL], AX.X, ALU.max))
                                nc.vector.tensor_tensor(attn[:], per(2)[0:CL], am[:].unsqueeze(2).broadcast_to([CL, U, S]),
                                                        ALU.subtract).then_inc(sem["shifted"], 1)
                                dve.wait_ge(sem["exp_done"], it + 1)
                                step(nc.vector.tensor_reduce(ar[:], attn[:], AX.X, ALU.add))
                                step(nc.vector.reciprocal(ar[:], ar[:]))
                                step(nc.vector.tensor_tensor(attn[:], attn[:], ar[:].unsqueeze(2).broadcast_to([CL, U, S]), ALU.mult))
                                nc.vector.tensor_scalar(attn[:], attn[:], 1e-8, None, ALU.add).then_inc(sem["upd_ready"], 1)
                                dve.wait_ge(sem["upd_done"], it + 1)
                                up = ps[:, 3:5, 0:2 * (D + 1)].rearrange("p b (u d) -> p b u d", u=2)
                                ur4 = ur[:].rearrange("p (b u) -> p b u", b=2)
                                step(nc.vector.reciprocal(ur4, up[:, :, :, D]))
                                nc.vector.tensor_tensor(zn[:, :, 0:D].rearrange("p (b u) d -> p b u d", b=2), up[:, :, :, 0:D],
                                                        ur4.unsqueeze(3).broadcast_to([128, 2, 2, D]), ALU.mult).then_inc(sem["o_normed"], 1)
                                dve.wait_ge(sem["mix_done"], it + 1)
                                step(nc.vector.tensor_tensor(xs[:], xs[:], per(5), ALU.add))
                                ln_vector(dve, step, 3 * it + 3, lambda u: xs[:, u, :]).then_inc(sem["z_ready"], 1)
                                dve.wait_ge(sem["ffn_done"], it + 1)
                                step(nc.vector.tensor_tensor(xs[:], xs[:], per(5), ALU.add))
                                step(nc.vector.tensor_tensor(xs[:].rearrange("p u d -> p (u d)"), xs[:].rearrange("p u d -> p (u d)"),
                                                             cond_bc[:, bass.ds(g * U * D, U * D)], ALU.add))
                                step(ln_vector(dve, step, 3 * it + 4, lambda u: xs[:, u, :]))
                                step(nc.vector.tensor_tensor(xs[:], zn[:, :, 0:D], over(row["lnp_g"]), ALU.mult))
                                step(nc.vector.tensor_tensor(xs[:], xs[:], over(row["lnp_b"]), ALU.add))
                            xg = x_all[:, bass.ds(g * U, U), :]
                            step(nc.vector.tensor_tensor(xg, xg, xs[:], ALU.add))
                            ln_vector(dve, step, 11, lambda u: x_all[:, g * U + u, :]).then_inc(sem["x_ready"], 1)
                            dve.wait_ge(sem["gram_done"], 1)
                            nc.vector.tensor_tensor(gram[:], gram[:], ps[:, 6, 0:D + 1], ALU.add)

                        @block.gpsimd
                        def _(pool):
                            ln_pool(pool, 0, rows=CL)
                            for r in range(1, 12):
                                ln_pool(pool, r)

                        @block.scalar
                        def _(act):
                            act.wait_ge(sem["zT_done"], 1)
                            nc.scalar.activation(cT[:], ps[:, 0, 0:UC], ACT.Identity, bias=col["lnkv_b"][:],
                                                 scale=col["lnkv_g"][:]).then_inc(sem["xnT_ready"], 1)
                            act.wait_ge(sem["k_done"], 1)
                            nc.scalar.activation(kT[:], ps[:, 1, 0:UC], ACT.Identity, bias=col["bk"][:]).then_inc(sem["k_read"], 1)
                            for it in range(3):
                                act.wait_ge(sem["zT_done"], 2 * it + 2)
                                nc.scalar.activation(xnT[:], ps[:, 0, :], ACT.Identity, bias=col["lnq_b"][:],
                                                     scale=col["lnq_g"][:]).then_inc(sem["xnT_ready"], 1)
                                act.wait_ge(sem["q_done"], it + 1)
                                nc.scalar.activation(qT[:], ps[:, 1, :], ACT.Identity, bias=col["bq"][:]).then_inc(sem["q_read"], 1)
                                act.wait_ge(sem["shifted"], it + 1)
                                nc.scalar.activation(attn[:], attn[:], ACT.Exp, scale=float(D) ** 0.5).then_inc(sem["exp_done"], 1)
                                act.wait_ge(sem["o_turned"], it + 1)
                                nc.scalar.activation(xnT[:], ps[:, 0, :], ACT.Identity, bias=col["bv"][:]).then_inc(sem["oT_ready"], 1)
                                act.wait_ge(sem["zT_done"], 2 * it + 3)
                                nc.scalar.activation(xnT[:], ps[:, 0, :], ACT.Identity, bias=col["lnm_b"][:],
                                                     scale=col["lnm_g"][:]).then_inc(sem["xnT_ready"], 1)
                                act.wait_ge(sem["hid_done"], it + 1)
                                nc.scalar.activation(qT[:], ps[:, 1, :], ACT.Gelu, bias=col["b1"][:]).then_inc(sem["hid_ready"], 1)

                        @block.tensor
                        def _(pe):
                            turn_rows(pe, 0, rows=CL)
                            pe.wait_ge(sem["xnT_ready"], 1)
                            nc.tensor.matmul(ps[:, 1, 0:UC], w["wk"][:], cT[:], start=True, stop=True).then_inc(sem["k_done"], 1)
                            for u in range(U):
                                last = nc.tensor.matmul(ps[0:CL, 2, u * D:(u + 1) * D], cT[:, u * CL:(u + 1) * CL], w["wv"][:],
                                                        start=True, stop=True)
                            last.then_inc(sem["v_done"], 1)
                            pe.wait_ge(sem["k_read"], 1)
                            pe.wait_ge(sem["v_read"], 1)
                            for it in range(3):
                                turn_rows(pe, 2 * it + 1)
                                pe.wait_ge(sem["xnT_ready"], 2 * it + 2)
                                nc.tensor.matmul(ps[:, 1, :], w["wq"][:], xnT[:], start=True, stop=True).then_inc(sem["q_done"], 1)
                                pe.wait_ge(sem["q_read"], it + 1)
                                for u in range(U):
                                    last = nc.tensor.matmul(ps[0:CL, 2, u * S:(u + 1) * S], kT[:, u * CL:(u + 1) * CL],
                                                            qT[:, u * S:(u + 1) * S], start=True, stop=True)
                                last.then_inc(sem["scores_done"], 1)
                                pe.wait_ge(sem["upd_ready"], it + 1)
                                for u in range(U):
                                    last = nc.tensor.matmul(ps[:, 3 + u // 2, (u % 2) * (D + 1):(u % 2 + 1) * (D + 1)],
                                                            attn[:, u, :], v1[:, u, :], start=True, stop=True)
                                last.then_inc(sem["upd_done"], 1)
                                pe.wait_ge(sem["o_normed"], it + 1)
                                for u in range(U):
                                    last = nc.tensor.transpose(ps[:, 0, u * S:(u + 1) * S], zn[:, u, 0:D], ident[:])
                                last.then_inc(sem["o_turned"], 1)
                                pe.wait_ge(sem["oT_ready"], it + 1)
                                for u in range(U):
                                    nc.tensor.matmul(per(5)[:, u, :], xnT[:, u * S:(u + 1) * S], w["wu"][:], start=True, stop=False)
                                    last = nc.tensor.matmul(per(5)[:, u, :], ones[0:1, :], bu[:], start=False, stop=True)
                                last.then_inc(sem["mix_done"], 1)
                                turn_rows(pe, 2 * it + 2)
                                pe.wait_ge(sem["xnT_ready"], 2 * it + 3)
                                nc.tensor.matmul(ps[:, 1, :], w["w1"][:], xnT[:], start=True, stop=True).then_inc(sem["hid_done"], 1)
                                pe.wait_ge(sem["hid_ready"], it + 1)
                                for u in range(U):
                                    nc.tensor.matmul(per(5)[:, u, :], qT[:, u * S:(u + 1) * S], w["w2"][:], start=True, stop=False)
                                    last = nc.tensor.matmul(per(5)[:, u, :], ones[0:1, :], b2[:], start=False, stop=True)
                                last.then_inc(sem["ffn_done"], 1)
                            pe.wait_ge(sem["x_ready"], 1)
                            for u in range(U):
                                last = nc.tensor.matmul(ps[:, 6, 0:D + 1], zn[:, u, 0:D], zn[:, u, :], start=(u == 0), stop=(u == U - 1))
                            last.then_inc(sem["gram_done"], 1)
                    rest()

        if "A" in SECTIONS or "C" in SECTIONS:
            stage_slots()

        def stage_product_keys():
            QH, KEYS, HALF, TOP, E = 8, 32, 16, 4, D
            QD = 2 * HALF
            NQ = QH * QD
            CELLS = 2 * QH
            PAD, TAKEN = 3e38, -3e38
            with ExitStack() as st:
                wq = sb("C_wq", [D, NQ], scope=st)
                bq = sb("C_bq", [128, NQ], scope=st)
                gamma = sb("C_gamma", [128, QD], scope=st)
                beta = sb("C_beta", [128, QD], scope=st)
                keys = sb("C_keys", [KEYS, 2, HALF], scope=st)
                ksq = sb("C_ksq", [KEYS, 2, HALF], scope=st)
                kn2 = sb("C_kn2", [KEYS, 2], scope=st)
                keys4 = sb("C_keys4", [KEYS, 4, QD], scope=st)
                kblk = sb("C_kblk", [128, 8, KEYS], scope=st)
                blocks = sb("C_blocks", [128, 8], scope=st)
                keysT = sb("C_keysT", [128, KEYS], scope=st)
                down = sb("C_down", [D, E], scope=st)
                up = sb("C_up", [E, D], scope=st)
                mean_h = sb("C_mean_h", [128, D], scope=st)
                prod = sb("C_prod", [128, NQ], scope=st)
                mean_q = sb("C_mean_q", [128, NQ], scope=st)
                var_q = sb("C_var_q", [128, NQ], scope=st)
                m_r = sb("C_m_r", [128, QD], scope=st)
                v_r = sb("C_v_r", [128, QD], scope=st)
                a_r = sb("C_a_r", [128, QD], scope=st)
                wT = sb("C_wT", [128, 2 * NQ], scope=st)
                wkey = sb("C_wkey", [D, 2 * NQ], scope=st)
                bkey = sb("C_bkey", [1, 2 * NQ], scope=st)
                sq = sb("C_sq", [128, 2, NQ], scope=st)
                n2 = sb("C_n2", [128, 2, CELLS], scope=st)
                rn = sb("C_rn", [128, 2, CELLS], scope=st)
                cand = sb("C_cand", [128, 2, CELLS, KEYS + TOP], scope=st)
                best = sb("C_best", [128, 2, CELLS, 8], scope=st)
                left = sb("C_left", [128, CELLS, KEYS + TOP], scope=st)
                ex = sb("C_ex", [128, 2, CELLS, KEYS], scope=st)
                z = sb("C_z", [128, CELLS], scope=st)
                tail = sb("C_tail", [128, 2], scope=st)
                outer = sb("C_outer", [128, 2, QH, 4, KEYS], scope=st)
                coef = sb("C_coef", [128, E], scope=st)
                act_g = sb("C_act", [128, U, E], scope=st)
                yT = sb("C_yT", [E, U * S], scope=st)

                with nc.Block() as block:
                    @block.sync
                    def _(sp):
                        pairs = [(wq[:], dram["L0_ffn_Wq"]), (bq[:], dram["L0_ffn_bq"].partition_broadcast(128)),
                                 (gamma[:], dram["L0_ffn_bn_gamma"].partition_broadcast(128)),
                                 (beta[:], dram["L0_ffn_bn_beta"].partition_broadcast(128)),
                                 (keys[:, 0, :], dram["L0_ffn_sub_key0"]), (keys[:, 1, :], dram["L0_ffn_sub_key1"]),
                                 (down[:], dram["L0_ffn_expert_down"]), (up[:], dram["L0_ffn_expert_up"]),
                                 (blocks[:], dram["block_mask"])]
                        for dst, src in pairs:
                            sp.dma_start(dst, src).then_inc(sem["loaded"], 16)

                    @block.vector
                    def _(dve):
                        step = Steps(dve, sem["vector_step"])
                        heads = lambda t: t[:].rearrange("p (h r) -> p h r", h=QH)
                        over_h = lambda t: t[:].unsqueeze(1).broadcast_to([128, QH, QD])
                        nc.vector.memset(cand[:], PAD)
                        step(nc.vector.tensor_scalar(gram[:], gram[:], 1.0 / (B * S), None, ALU.mult))
                        nc.vector.tensor_scalar(mean_h[:], ones[:], gram[:, D:D + 1], None, ALU.mult).then_inc(sem["x_ready"], 1)
                        dve.wait_ge(sem["loaded"], 16 * 9)
                        dve.wait_ge(sem["q_done"], 1)
                        step(nc.vector.tensor_copy(mean_q[:], ps[:, 1, 0:NQ]))
                        nc.vector.tensor_tensor(prod[:], ps[:, 0, 0:NQ], wq[:], ALU.mult).then_inc(sem["upd_ready"], 1)
                        dve.wait_ge(sem["upd_done"], 1)
                        step(nc.vector.tensor_tensor(var_q[:], mean_q[:], mean_q[:], ALU.mult))
                        step(nc.vector.tensor_tensor(var_q[:], ps[:, 2, 0:NQ], var_q[:], ALU.subtract))
                        step(nc.vector.tensor_tensor(mean_q[:], mean_q[:], bq[:], ALU.add))
                        step(nc.vector.tensor_reduce(m_r[:], mean_q[:].rearrange("p (h r) -> p r h", h=QH), AX.X, ALU.add))
                        step(nc.vector.tensor_scalar(m_r[:], m_r[:], 1.0 / QH, None, ALU.mult))
                        step(nc.vector.tensor_tensor(heads(prod), heads(mean_q), over_h(m_r), ALU.subtract))
                        step(nc.vector.tensor_tensor(prod[:], prod[:], prod[:], ALU.mult))
                        step(nc.vector.tensor_tensor(var_q[:], var_q[:], prod[:], ALU.add))
                        step(nc.vector.tensor_reduce(v_r[:], var_q[:].rearrange("p (h r) -> p r h", h=QH), AX.X, ALU.add))
                        step(nc.vector.tensor_scalar(v_r[:], v_r[:], 1.0 / QH, 1e-5, ALU.mult, ALU.add))
                        step(nc.vector.tensor_tensor(ksq[:], keys[:], keys[:], ALU.mult))
                        step(nc.vector.tensor_reduce(kn2[:], ksq[:], AX.X, ALU.add))
                        nc.vector.tensor_scalar(kn2[:], kn2[:], 1e-24, None, ALU.max).then_inc(sem["var_ready"], 1)
                        dve.wait_ge(sem["rstd_ready"], 2)
                        step(nc.vector.tensor_tensor(a_r[:], a_r[:], gamma[:], ALU.mult))
                        step(nc.vector.tensor_tensor(m_r[:], m_r[:], a_r[:], ALU.mult))
                        step(nc.vector.tensor_tensor(m_r[:], beta[:], m_r[:], ALU.subtract))
                        step(nc.vector.tensor_tensor(heads(wq), heads(wq), over_h(a_r), ALU.mult))
                        step(nc.vector.tensor_tensor(heads(bq), heads(bq), over_h(a_r), ALU.mult))
                        step(nc.vector.tensor_tensor(heads(bq), heads(bq), over_h(m_r), ALU.add))
                        step(nc.vector.tensor_tensor(keys[:], keys[:], kn2[:].unsqueeze(2).broadcast_to([KEYS, 2, HALF]), ALU.mult))
                        nc.vector.tensor_copy(keys4[:], keys[:].rearrange("p a r -> p (a r)").unsqueeze(1).broadcast_to([KEYS, 4, QD])).then_inc(sem["z_ready"], 1)
                        dve.wait_ge(sem["zT_done"], 1)
                        step(nc.vector.tensor_copy(keysT[:], ps[:, 3, 0:KEYS]))
                        nc.vector.tensor_copy(wT[:], ps[:, 4, :])
                        nc.vector.tensor_tensor(kblk[:], keysT[:].unsqueeze(1).broadcast_to([128, 8, KEYS]),
                                                blocks[:].unsqueeze(2).broadcast_to([128, 8, KEYS]), ALU.mult).then_inc(sem["table_ready"], 1)
                        dve.wait_ge(sem["k_done"], 1)
                        nc.vector.tensor_copy(wkey[:], ps[:, 5, :])
                        nc.vector.tensor_copy(bkey[:], ps[0:1, 6, :])

                    @block.gpsimd
                    def _(pool):
                        pool.wait_ge(sem["var_ready"], 1)
                        nc.gpsimd.tensor_tensor(a_r[:], v_r[:], neghalf[:, 0:QD], ALU.pow).then_inc(sem["rstd_ready"], 1)
                        nc.gpsimd.tensor_tensor(kn2[:], kn2[:], neghalf[0:KEYS, 0:2], ALU.pow).then_inc(sem["rstd_ready"], 1)

                    @block.tensor
                    def _(pe):
                        pe.wait_ge(sem["loaded"], 16 * 9)
                        pe.wait_ge(sem["x_ready"], 1)
                        nc.tensor.matmul(ps[:, 0, 0:NQ], gram[:, 0:D], wq[:], start=True, stop=True)
                        nc.tensor.matmul(ps[:, 1, 0:NQ], mean_h[:], wq[:], start=True, stop=True).then_inc(sem["q_done"], 1)
                        pe.wait_ge(sem["upd_ready"], 1)
                        nc.tensor.matmul(ps[:, 2, 0:NQ], ones[:], prod[:], start=True, stop=True).then_inc(sem["upd_done"], 1)
                        pe.wait_ge(sem["z_ready"], 1)
                        nc.tensor.transpose(ps[:, 3, 0:KEYS], keys4[:].rearrange("p a r -> p (a r)"), ident[0:KEYS, 0:KEYS])
                        for c in range(2):
                            nc.tensor.transpose(ps[:, 4, c * 128:(c + 1) * 128], wq[:, c * 128:(c + 1) * 128], ident[:])
                            last = nc.tensor.transpose(ps[:, 4, NQ + c * 128:NQ + (c + 1) * 128], bq[:, c * 128:(c + 1) * 128], ident[:])
                        last.then_inc(sem["zT_done"], 1)
                        pe.wait_ge(sem["table_ready"], 1)
                        kb = kblk[:].rearrange("p a k -> p (a k)")
                        for c in range(2):
                            nc.tensor.matmul(ps[:, 5, c * NQ:(c + 1) * NQ], wT[:, c * 128:(c + 1) * 128], kb, start=True, stop=True)
                            last = nc.tensor.matmul(ps[:, 6, c * NQ:(c + 1) * NQ], wT[:, NQ + c * 128:NQ + (c + 1) * 128], kb, start=True, stop=True)
                        last.then_inc(sem["k_done"], 1)
                rest()

                with nc.Fori(0, NG) as g:
                    with nc.Block() as block:
                        @block.vector
                        def _(dve):
                            step = Steps(dve, sem["vector_step"])
                            ln_vector(dve, step, 0, lambda u: x_all[:, g * U + u, :]).then_inc(sem["z_ready"], 1)

                            def select(u):
                                b = u % 2
                                dve.wait_ge(sem["q_read"], u + 1)
                                step(nc.vector.tensor_reduce(n2[:, b, :], sq[:, b, :].rearrange("p (c r) -> p c r", r=HALF), AX.X, ALU.add))
                                nc.vector.tensor_scalar(n2[:, b, :], n2[:, b, :], 1e-24, None, ALU.max).then_inc(sem["var_ready"], 1)
                                dve.wait_ge(sem["rstd_ready"], u + 2)
                                nc.vector.tensor_tensor(cand[:, b, :, 0:KEYS], ps[:, b, :].rearrange("p (c k) -> p c k", k=KEYS),
                                                        rn[:, b, :].unsqueeze(2).broadcast_to([128, CELLS, KEYS]), ALU.mult).then_inc(sem["cand_ready"], 1)
                                dve.wait_ge(sem["cand_ready"], u + 1)
                                for c in range(CELLS):
                                    last = nc.vector.max(best[:, b, c, :], cand[:, b, c, 0:KEYS])
                                step(last)
                                step(nc.vector.memset(best[:, b, :, TOP:8], PAD))
                                for c in range(CELLS):
                                    last = nc.vector.match_replace(left[:, c, :], best[:, b, c, :], cand[:, b, c, :], TAKEN)
                                step(last)
                                dve.wait_ge(sem["exp_done"], u + 1)
                                step(nc.vector.scalar_tensor_tensor(out=ex[:, b], in0=left[:, :, 0:KEYS], scalar=0.5 * TAKEN, in1=ex[:, b],
                                                                    op0=ALU.is_lt, op1=ALU.mult))
                                step(nc.vector.tensor_reduce(z[:], ex[:, b], AX.X, ALU.add))
                                step(nc.vector.reciprocal(z[:], z[:]))
                                nc.vector.tensor_tensor(ex[:, b], ex[:, b], z[:].unsqueeze(2).broadcast_to([128, CELLS, KEYS]),
                                                        ALU.mult).then_inc(sem["shifted"], 1)
                                dve.wait_ge(sem["shifted"], u + 1)
                                first = ex[:, b].rearrange("p (h a) k -> p h a k", a=2)[:, :, 0, 4:KEYS]
                                nc.vector.tensor_reduce(tail[:, b:b + 1], first, AX.XY, ALU.add)

                            def weigh(u):
                                b = u % 2
                                dve.wait_ge(sem["outer_ready"], u + 1)
                                step(nc.vector.tensor_reduce(coef[:], outer[:, b].rearrange("p h i k -> p (i k) h"), AX.X, ALU.add))
                                step(nc.vector.tensor_tensor(coef[:, E - 1:E], coef[:, E - 1:E], tail[:, b:b + 1], ALU.add))
                                if u == 0:
                                    dve.wait_ge(sem["hid_ready"], 1)
                                nc.vector.tensor_tensor(xs[:, u, :], act_g[:, u, :], coef[:], ALU.mult).then_inc(sem["expert_ready"], 1)
                                dve.wait_ge(sem["expert_ready"], u + 1)

                            for u in range(U):
                                select(u)
                                if u:
                                    weigh(u - 1)
                            weigh(U - 1)
                            dve.wait_ge(sem["mix_done"], 1)
                            xg = x_all[:, bass.ds(g * U, U), :]
                            nc.vector.tensor_tensor(xg, xg, per(6), ALU.add)

                        @block.gpsimd
                        def _(pool):
                            ln_pool(pool, 0)
                            for u in range(U):
                                b = u % 2
                                pool.wait_ge(sem["var_ready"], u + 2)
                                if u >= 2:
                                    pool.wait_ge(sem["cand_ready"], u - 1)
                                nc.gpsimd.tensor_tensor(rn[:, b, :], n2[:, b, :], neghalf[:, 0:CELLS], ALU.pow).then_inc(sem["rstd_ready"], 1)
                                pool.wait_ge(sem["shifted"], u + 1)
                                if u >= 2:
                                    pool.wait_ge(sem["expert_ready"], u - 1)
                                halves = ex[:, b].rearrange("p (h a) k -> p h a k", a=2)
                                for i in range(4):
                                    last = nc.gpsimd.tensor_tensor(outer[:, b, :, i, :], halves[:, :, 0, i:i + 1].broadcast_to([128, QH, KEYS]),
                                                                   halves[:, :, 1, :], ALU.mult)
                                last.then_inc(sem["outer_ready"], 1)

                        @block.scalar
                        def _(act):
                            act.wait_ge(sem["zT_done"], 1)
                            nc.scalar.activation(xnT[:], ps[:, 4, :], ACT.Copy).then_inc(sem["xnT_ready"], 1)
                            act.wait_ge(sem["hid_done"], 1)
                            nc.scalar.activation(act_g[:], per(7), ACT.Gelu).then_inc(sem["hid_ready"], 1)
                            for u in range(U):
                                b = u % 2
                                act.wait_ge(sem["scores_done"], u + 1)
                                nc.scalar.activation(sq[:, b, :], ps[:, 2 + b, 0:NQ], ACT.Square).then_inc(sem["q_read"], 1)
                                act.wait_ge(sem["cand_ready"], u + 1)
                                if u >= 2:
                                    act.wait_ge(sem["outer_ready"], u - 1)
                                nc.scalar.activation(ex[:, b], cand[:, b, :, 0:KEYS], ACT.Exp).then_inc(sem["exp_done"], 1)
                            act.wait_ge(sem["o_turned"], 1)
                            nc.scalar.activation(yT[:], ps[:, 5, :], ACT.Copy).then_inc(sem["oT_ready"], 1)

                        @block.tensor
                        def _(pe):
                            turn_rows(pe, 0, bank=4)
                            pe.wait_ge(sem["xnT_ready"], 1)
                            for u in range(U):
                                last = nc.tensor.matmul(per(7)[:, u, :], xnT[:, u * S:(u + 1) * S], down[:], start=True, stop=True)
                            last.then_inc(sem["hid_done"], 1)
                            for u in range(U):
                                b, z_u = u % 2, xnT[:, u * S:(u + 1) * S]
                                if u >= 2:
                                    pe.wait_ge(sem["cand_ready"], u - 1)
                                    pe.wait_ge(sem["q_read"], u - 1)
                                nc.tensor.matmul(ps[:, b, :], z_u, wkey[:], start=True, stop=False)
                                nc.tensor.matmul(ps[:, b, :], ones[0:1, :], bkey[:], start=False, stop=True)
                                nc.tensor.matmul(ps[:, 2 + b, 0:NQ], z_u, wq[:], start=True, stop=False)
                                nc.tensor.matmul(ps[:, 2 + b, 0:NQ], ones[0:1, :], bq[0:1, :], start=False, stop=True).then_inc(sem["scores_done"], 1)
                            pe.wait_ge(sem["expert_ready"], U)
                            for u in range(U):
                                last = nc.tensor.transpose(ps[:, 5, u * S:(u + 1) * S], xs[:, u, :], ident[:])
                            last.then_inc(sem["o_turned"], 1)
                            pe.wait_ge(sem["oT_ready"], 1)
                            for u in range(U):
                                last = nc.tensor.matmul(per(6)[:, u, :], yT[:, u * S:(u + 1) * S], up[:], start=True, stop=True)
                            last.then_inc(sem["mix_done"], 1)
                    rest()

        if "C" in SECTIONS:
            stage_product_keys()

        def wait_all(eng, names, value):
            for n in names:
                eng.wait_ge(sem[n], value)

        def job_bank(pe, k):
            if k >= 4:
                pe.wait_ge(sem["q_read" if k % 2 == 0 else "k_read"], (k - 4) // 2 + 1)
            return k % 4

        def jobs_read(pe, n):
            pe.wait_ge(sem["q_read"], n // 2)
            pe.wait_ge(sem["k_read"], n // 2)

        def copy_job(eng, k, dst, src):
            eng.wait_ge(sem["proj_done"], k + 1)
            if k % 2 == 0:
                nc.scalar.activation(dst, src, ACT.Copy).then_inc(sem["q_read"], 1)
            else:
                nc.vector.tensor_copy(dst, src).then_inc(sem["k_read"], 1)

        def stage_block():
            W, INNER, NB = D // 2, NH * D // 2, NH // 2
            with ExitStack() as st:
                wa = {}
                for a in (1, 2):
                    for n in ("wq", "wk", "wv"):
                        wa[a, n] = sb(f"D_{n}{a}", [D, INNER], scope=st)
                    wa[a, "wo"] = sb(f"D_wo{a}", [D, NB, D], scope=st)
                    wa[a, "bo"] = sb(f"D_bo{a}", [1, D], scope=st)
                w1 = sb("D_w1", [D, 2 * FFN], scope=st)
                b1 = sb("D_b1", [D, 8], scope=st)
                w2 = sb("D_w2", [D, 4, D], scope=st)
                b2 = sb("D_b2", [1, D], scope=st)
                nw = sb("D_nw", [D, 3, 2 * D], scope=st)
                nb = sb("D_nb", [D, 3, 2], scope=st)
                gb = sb("D_gb", [D, 3, 2, B], scope=st)
                gb4 = sb("D_gb4", [D, 3, 2, U], scope=st)
                qT = sb("D_qT", [D, NB, U * S], scope=st)
                kT = sb("D_kT", [D, NB, U * S], scope=st)
                vv = sb("D_vv", [S, U, NH, W + 1], scope=st)
                o_all = sb("D_o", [S, U, INNER], scope=st)
                loads = [(w1[:], dram["L1_xcond_ff_w1"]),
                         (b1[:], dram["L1_xcond_ff_b1"].rearrange("(c p) -> p c", p=D)),
                         (w2[:], dram["L1_xcond_ff_w2"].rearrange("(c p) n -> p c n", p=D)),
                         (b2[:], dram["L1_xcond_ff_b2"].unsqueeze(0))]
                for a in (1, 2):
                    for n in ("wq", "wk", "wv"):
                        loads.append((wa[a, n][:], dram[f"L1_xcond_attn{a}_{n}"]))
                    loads.append((wa[a, "wo"][:], dram[f"L1_xcond_attn{a}_wo"].rearrange("(c p) n -> p c n", p=D)))
                    loads.append((wa[a, "bo"][:], dram[f"L1_xcond_attn{a}_bo"].unsqueeze(0)))
                for n in range(3):
                    loads.append((nw[:, n, :], dram[f"L1_xcond_norm{n + 1}_w"]))
                    loads.append((nb[:, n, :], dram[f"L1_xcond_norm{n + 1}_b"].rearrange("(c p) -> p c", p=D)))

                with nc.Block() as block:
                    @block.sync
                    def _(sp):
                        for dst, src in loads:
                            sp.dma_start(dst, src, allow_slow_non_contiguous=True).then_inc(sem["loaded"], 16)

                    @block.tensor
                    def _(pe):
                        pe.wait_ge(sem["loaded"], 16 * len(loads))
                        for n in range(3):
                            for c in range(2):
                                last = nc.tensor.matmul(ps[:, 0, (2 * n + c) * B:(2 * n + c + 1) * B], nw[:, n, c * D:(c + 1) * D],
                                                        condT[:], start=True, stop=True)
                        last.then_inc(sem["proj_done"], 1)

                    @block.vector
                    def _(dve):
                        step = Steps(dve, sem["vector_step"])
                        nc.vector.memset(vv[:], 1.0)
                        dve.wait_ge(sem["loaded"], 16 * len(loads))
                        step(nc.vector.tensor_scalar(nb[:, :, 0], nb[:, :, 0], 1.0, None, ALU.add))
                        dve.wait_ge(sem["proj_done"], 1)
                        nc.vector.tensor_tensor(gb[:].rearrange("p n c b -> p (n c) b"),
                                                ps[:, 0, 0:6 * B].rearrange("p (n b) -> p n b", b=B),
                                                nb[:].rearrange("p n c -> p (n c)").unsqueeze(2).broadcast_to([D, 6, B]), ALU.add)
                rest()

                ctxg = sb("D_ctxg", [D, UC], scope=st)
                with nc.Fori(0, NG) as g:
                    with nc.Block() as block:
                        @block.tensor
                        def _(pe):
                            for a in (1, 2):
                                k0 = 32 * (a - 1)
                                keys = S if a == 1 else CL
                                src = xnT if a == 1 else ctxg
                                turn_rows(pe, a - 1, bank=TURN)
                                pe.wait_ge(sem["xnT_ready"], a)
                                for c in range(NB):
                                    bank = job_bank(pe, k0 + c)
                                    nc.tensor.matmul(ps[:, bank, :], wa[a, "wq"][:, c * D:(c + 1) * D], xnT[:],
                                                     start=True, stop=True).then_inc(sem["proj_done"], 1)
                                for c in range(NB):
                                    bank = job_bank(pe, k0 + NB + c)
                                    nc.tensor.matmul(ps[:, bank, 0:U * keys], wa[a, "wk"][:, c * D:(c + 1) * D], src[:, 0:U * keys],
                                                     start=True, stop=True).then_inc(sem["proj_done"], 1)
                                for c in range(2 * U):
                                    bank = job_bank(pe, k0 + 2 * NB + c)
                                    nc.tensor.matmul(ps[0:keys, bank, :], src[:, (c // 2) * keys:(c // 2 + 1) * keys],
                                                     wa[a, "wv"][:, (c % 2) * 512:(c % 2 + 1) * 512],
                                                     start=True, stop=True).then_inc(sem["proj_done"], 1)
                                jobs_read(pe, k0 + 24)
                                attn_tensor(pe, a - 1, keys, True,
                                            lambda h, u: qT[W * (h % 2):W * (h % 2 + 1), h // 2, u * S:(u + 1) * S],
                                            lambda h, u: kT[W * (h % 2):W * (h % 2 + 1), h // 2, u * keys:(u + 1) * keys],
                                            lambda h, u: vv[0:keys, u, h, :])
                                pe.wait_ge(sem["o_normed"], NU * a)
                                for c in range(2 * U):
                                    bank = job_bank(pe, k0 + 24 + c)
                                    for i in range(4):
                                        last = nc.tensor.transpose(ps[:, bank, i * S:(i + 1) * S],
                                                                   o_all[:, c // 2, ((c % 2) * 4 + i) * D:((c % 2) * 4 + i + 1) * D], ident[:])
                                    last.then_inc(sem["proj_done"], 1)
                                jobs_read(pe, k0 + 32)
                                for u in range(U):
                                    for c in range(NB):
                                        nc.tensor.matmul(per(OUT)[:, u, :], qT[:, c, u * S:(u + 1) * S], wa[a, "wo"][:, c, :],
                                                         start=(c == 0), stop=False)
                                    last = nc.tensor.matmul(per(OUT)[:, u, :], ones[0:1, :], wa[a, "bo"][:], start=False, stop=True)
                                last.then_inc(sem["mix_done"], 1)
                            turn_rows(pe, 2, bank=TURN)
                            pe.wait_ge(sem["xnT_ready"], 3)
                            for j in range(4):
                                for c, k in ((4 + j, 64 + 2 * j), (j, 65 + 2 * j)):
                                    bank = job_bank(pe, k)
                                    nc.tensor.matmul(ps[:, bank, :], w1[:, c * D:(c + 1) * D], xnT[:],
                                                     start=True, stop=True).then_inc(sem["proj_done"], 1)
                            jobs_read(pe, 72)
                            for u in range(U):
                                for c in range(4):
                                    nc.tensor.matmul(per(OUT)[:, u, :], kT[:, 4 + c, u * S:(u + 1) * S], w2[:, c, :],
                                                     start=(c == 0), stop=False)
                                last = nc.tensor.matmul(per(OUT)[:, u, :], ones[0:1, :], b2[:], start=False, stop=True)
                            last.then_inc(sem["mix_done"], 1)

                        def empty(eng, k0, a, odd):
                            keys = S if a == 1 else CL
                            for c in range(odd, NB, 2):
                                copy_job(eng, k0 + c, qT[:, c, :], ps[:, (k0 + c) % 4, :])
                            for c in range(odd, NB, 2):
                                copy_job(eng, k0 + NB + c, kT[:, c, 0:U * keys], ps[:, (k0 + NB + c) % 4, 0:U * keys])
                            for c in range(odd, 2 * U, 2):
                                copy_job(eng, k0 + 2 * NB + c, vv[0:keys, c // 2, (c % 2) * 8:(c % 2 + 1) * 8, 0:W],
                                         ps[0:keys, (k0 + 2 * NB + c) % 4, :].rearrange("p (h d) -> p h d", d=W))

                        def empty_turned(eng, k0, odd):
                            for c in range(odd, 2 * U, 2):
                                u, half = c // 2, c % 2
                                copy_job(eng, k0 + 24 + c, qT[:, 4 * half:4 * half + 4, u * S:(u + 1) * S],
                                         ps[:, (k0 + 24 + c) % 4, :].rearrange("p (c t) -> p c t", c=4))

                        @block.scalar
                        def _(act):
                            for a in (1, 2, 3):
                                act.wait_ge(sem["zT_done"], a)
                                if a == 1:
                                    act.wait_ge(sem["table_ready"], 1)
                                for u in range(U):
                                    last = nc.scalar.activation(xnT[:, u * S:(u + 1) * S], ps[:, TURN, u * S:(u + 1) * S], ACT.Identity,
                                                                bias=gb4[:, a - 1, 1, u:u + 1], scale=gb4[:, a - 1, 0, u:u + 1])
                                last.then_inc(sem["xnT_ready"], 1)
                                if a < 3:
                                    k0 = 32 * (a - 1)
                                    empty(act, k0, a, 0)
                                    attn_scalar(act, a - 1, S if a == 1 else CL, W ** -0.5)
                                    empty_turned(act, k0, 0)
                            for j in range(4):
                                act.wait_ge(sem["proj_done"], 64 + 2 * j + 1)
                                nc.scalar.activation(kT[:, j, :], ps[:, (64 + 2 * j) % 4, :], ACT.Gelu, bias=b1[:, 4 + j:5 + j]).then_inc(sem["q_read"], 1)

                        @block.vector
                        def _(dve):
                            step = Steps(dve, sem["vector_step"])
                            nc.vector.tensor_copy(ctxg[:], ctxT[:, bass.ds(g * UC, UC)])
                            nc.vector.tensor_copy(gb4[:].rearrange("p n c u -> p (n c) u"),
                                                  gb[:].rearrange("p n c b -> p (n c) b")[:, :, bass.ds(g * U, U)]).then_inc(sem["table_ready"], 1)
                            step(ln_vector(dve, step, 0, lambda u: x_all[:, g * U + u, :], lambda u: xs[:, u, :]))
                            for a in (1, 2):
                                k0 = 32 * (a - 1)
                                ln_vector(dve, step, a, lambda u: xs[:, u, :]).then_inc(sem["z_ready"], 1)
                                empty(dve, k0, a, 1)
                                attn_vector(dve, step, a - 1, S if a == 1 else CL, True, lambda u: o_all[:, u, :])
                                empty_turned(dve, k0, 1)
                                dve.wait_ge(sem["mix_done"], a)
                                step(nc.vector.tensor_tensor(xs[:], xs[:], per(OUT), ALU.add))
                            ln_vector(dve, step, 3, lambda u: xs[:, u, :]).then_inc(sem["z_ready"], 1)
                            for j in range(4):
                                dve.wait_ge(sem["q_read"], 32 + j + 1)
                                dve.wait_ge(sem["proj_done"], 65 + 2 * j + 1)
                                nc.vector.scalar_tensor_tensor(out=kT[:, 4 + j, :], in0=ps[:, (65 + 2 * j) % 4, :], scalar=b1[:, j:j + 1],
                                                               in1=kT[:, j, :], op0=ALU.add, op1=ALU.mult).then_inc(sem["k_read"], 1)
                            dve.wait_ge(sem["mix_done"], 3)
                            step(nc.vector.tensor_tensor(xs[:], xs[:], per(OUT), ALU.add))
                            xg = x_all[:, bass.ds(g * U, U), :]
                            nc.vector.tensor_tensor(xg, xg, xs[:], ALU.add)

                        @block.gpsimd
                        def _(pool):
                            for r in range(4):
                                ln_pool(pool, r)
                    rest()

        if "D" in SECTIONS:
            stage_block()

        PAD, TAKEN = 3e38, -3e38
        gates = sb("gates", [128, U, EXPERTS + 6])
        gbest = sb("gbest", [128, U, 8])
        gleft = sb("gleft", [128, U, EXPERTS + 6])
        gsum = sb("gsum", [128, U])
        chosen = sb("chosen", [128, U, EXPERTS])

        def route_vector(dve, step, bank, weighted):
            g8 = gates[:, :, 0:EXPERTS]
            over = lambda t: t[:].unsqueeze(2).broadcast_to([128, U, EXPERTS])
            dve.wait_ge(sem["gate_done"], 1)
            step(nc.vector.tensor_reduce(gsum[:], per(bank, EXPERTS), AX.X, ALU.max))
            nc.vector.tensor_tensor(g8, per(bank, EXPERTS), over(gsum), ALU.subtract).then_inc(sem["cand_ready"], 1)
            dve.wait_ge(sem["gate_ready"], 1)
            step(nc.vector.tensor_reduce(gsum[:], g8, AX.X, ALU.add))
            step(nc.vector.reciprocal(gsum[:], gsum[:]))
            step(nc.vector.tensor_tensor(g8, g8, over(gsum), ALU.mult))
            for u in range(U):
                last = nc.vector.max(gbest[:, u, :], gates[:, u, 0:EXPERTS])
            step(last)
            step(nc.vector.memset(gbest[:, :, 2:8], PAD))
            for u in range(U):
                last = nc.vector.match_replace(gleft[:, u, :], gbest[:, u, :], gates[:, u, :], TAKEN)
            step(last)
            if weighted:
                step(nc.vector.scalar_tensor_tensor(out=chosen[:], in0=gleft[:, :, 0:EXPERTS], scalar=0.5 * TAKEN, in1=g8,
                                                    op0=ALU.is_lt, op1=ALU.mult))
            else:
                step(nc.vector.tensor_scalar(chosen[:], gleft[:, :, 0:EXPERTS], 0.5 * TAKEN, None, ALU.is_lt))

        def route_scalar(act):
            act.wait_ge(sem["cand_ready"], 1)
            nc.scalar.activation(gates[:, :, 0:EXPERTS], gates[:, :, 0:EXPERTS], ACT.Exp).then_inc(sem["gate_ready"], 1)

        q_way = nc.dram_tensor("q_way", (D, U * S), F32, kind="Internal").ap()
        k_way = nc.dram_tensor("k_way", (D, U * S), F32, kind="Internal").ap()

        def spread(eng, way, src, dst, cols, ready, spread_to, saved):
            eng.wait_ge(*ready)
            eng.dma_start(way[:, 0:cols], src).then_inc(sem["saved"], 16)
            eng.wait_ge(sem["saved"], 16 * saved)
            for q in range(4):
                eng.dma_start(dst[32 * q:32 * q + HD, :, 0:cols],
                              way[:, 0:cols].rearrange("(g j r) c -> g r j c", g=4, r=HD)[q]).then_inc(spread_to, 16)

        def stage_attn_experts():
            with ExitStack() as st:
                wqkv = sb("E_wqkv", [D, 3 * D], scope=st)
                bqk = sb("E_bqk", [D, 2], scope=st)
                bv = sb("E_bv", [1, D], scope=st)
                wg = sb("E_wg", [D, EXPERTS], scope=st)
                bg = sb("E_bg", [1, EXPERTS], scope=st)
                we = sb("E_we", [D, EXPERTS * D], scope=st)
                be = sb("E_be", [1, EXPERTS * D], scope=st)
                qr = sb("E_qr", [D, U * S], scope=st)
                kr = sb("E_kr", [D, U * S], scope=st)
                q4 = sb("E_q4", [128, 4, U * S], scope=st)
                k4 = sb("E_k4", [128, 4, U * S], scope=st)
                v9 = sb("E_v9", [S, U, NH, HD + 1], scope=st)
                o8 = sb("E_o8", [S, U, D], scope=st)
                moe = sb("E_moe", [S, U, D], scope=st)
                loads = [(wqkv[:], dram["L1_ffn_W_qkv"]),
                         (bqk[:], dram["L1_ffn_b_qkv"][0:2 * D].rearrange("(c p) -> p c", p=D)),
                         (bv[:], dram["L1_ffn_b_qkv"][2 * D:3 * D].unsqueeze(0)),
                         (wg[:], dram["L1_ffn_W_gate"]), (bg[:], dram["L1_ffn_b_gate"].unsqueeze(0)),
                         (we[:].rearrange("d (e f) -> d e f", f=D), dram["L1_ffn_W_experts"].rearrange("e d f -> d e f")),
                         (be[:], dram["L1_ffn_b_experts"].rearrange("e f -> (e f)").unsqueeze(0))]
                with nc.Block() as block:
                    @block.sync
                    def _(sp):
                        for dst, src in loads:
                            sp.dma_start(dst, src, allow_slow_non_contiguous=True).then_inc(sem["loaded"], 16)
                        sp.wait_ge(sem["loaded"], 16 * len(loads))

                    @block.vector
                    def _(dve):
                        nc.vector.memset(v9[:], 1.0)
                        nc.vector.memset(gates[:], PAD)
                rest()

                with nc.Fori(0, NG) as g:
                    with nc.Block() as block:
                        @block.sync
                        def _(sp):
                            spread(sp, q_way, qr[:], q4, U * S, (sem["q_read"], 1), sem["loaded_q"], 1)
                            spread(sp, k_way, kr[:], k4, U * S, (sem["q_read"], 2), sem["loaded_q"], 2)

                        @block.tensor
                        def _(pe):
                            turn_rows(pe, 0, bank=TURN)
                            pe.wait_ge(sem["xnT_ready"], 1)
                            for c in range(2):
                                nc.tensor.matmul(ps[:, TURN + 1 + c, :], wqkv[:, c * D:(c + 1) * D], xnT[:],
                                                 start=True, stop=True).then_inc(sem["q_done"], 1)
                            for u in range(U):
                                nc.tensor.matmul(per(7)[:, u, :], xnT[:, u * S:(u + 1) * S], wqkv[:, 2 * D:3 * D], start=True, stop=False)
                                last = nc.tensor.matmul(per(7)[:, u, :], ones[0:1, :], bv[:], start=False, stop=True)
                            last.then_inc(sem["v_done"], 1)
                            for u in range(U):
                                nc.tensor.matmul(per(TURN, EXPERTS)[:, u, :], xnT[:, u * S:(u + 1) * S], wg[:], start=True, stop=False)
                                last = nc.tensor.matmul(per(TURN, EXPERTS)[:, u, :], ones[0:1, :], bg[:], start=False, stop=True)
                            last.then_inc(sem["gate_done"], 1)
                            for u in range(U):
                                if u >= 2:
                                    pe.wait_ge(sem["expert_ready"], u - 1)
                                for c in range(2):
                                    bank = 2 * (u % 2) + c
                                    nc.tensor.matmul(ps[:, bank, :], xnT[:, u * S:(u + 1) * S], we[:, c * 512:(c + 1) * 512], start=True, stop=False)
                                    last = nc.tensor.matmul(ps[:, bank, :], ones[0:1, :], be[:, c * 512:(c + 1) * 512], start=False, stop=True)
                                last.then_inc(sem["expert_done"], 1)
                            pe.wait_ge(sem["expert_ready"], U)
                            pe.wait_ge(sem["v_read"], 1)
                            pe.wait_ge(sem["q_read"], 2)
                            pe.wait_ge(sem["loaded_q"], 16 * 8)
                            attn_tensor(pe, 0, S, False,
                                        lambda h, u: q4[32 * (h // 4):32 * (h // 4) + HD, h % 4, u * S:(u + 1) * S],
                                        lambda h, u: k4[32 * (h // 4):32 * (h // 4) + HD, h % 4, u * S:(u + 1) * S],
                                        lambda h, u: v9[:, u, h, :])

                        @block.scalar
                        def _(act):
                            act.wait_ge(sem["zT_done"], 1)
                            nc.scalar.activation(xnT[:], ps[:, TURN, :], ACT.Copy).then_inc(sem["xnT_ready"], 1)
                            for c, t in enumerate((qr, kr)):
                                act.wait_ge(sem["q_done"], c + 1)
                                nc.scalar.activation(t[:], ps[:, TURN + 1 + c, :], ACT.Identity, bias=bqk[:, c:c + 1]).then_inc(sem["q_read"], 1)
                            act.wait_ge(sem["v_done"], 1)
                            nc.scalar.activation(v9[:, :, :, 0:HD], per(7).rearrange("p u (h d) -> p u h d", d=HD), ACT.Copy).then_inc(sem["v_read"], 1)
                            route_scalar(act)
                            attn_scalar(act, 0, S, HD ** -0.5)

                        @block.vector
                        def _(dve):
                            step = Steps(dve, sem["vector_step"])
                            ln_vector(dve, step, 0, lambda u: x_all[:, g * U + u, :]).then_inc(sem["z_ready"], 1)
                            route_vector(dve, step, TURN, True)
                            for u in range(U):
                                dve.wait_ge(sem["expert_done"], u + 1)
                                prod = e[:, u % 2, :].rearrange("p (e f) -> p e f", f=D)
                                nc.vector.tensor_tensor(prod, ps[:, 2 * (u % 2):2 * (u % 2) + 2, :].rearrange("p b (e f) -> p (b e) f", f=D),
                                                        chosen[:, u, :].unsqueeze(2).broadcast_to([128, EXPERTS, D]), ALU.mult).then_inc(sem["expert_ready"], 1)
                                dve.wait_ge(sem["expert_ready"], u + 1)
                                last = nc.vector.tensor_reduce(moe[:, u, :], prod.rearrange("p e f -> p f e"), AX.X, ALU.add)
                            step(last)
                            attn_vector(dve, step, 0, S, False, lambda u: o8[:, u, :])
                            dve.wait_ge(sem["o_normed"], NU)
                            step(nc.vector.tensor_tensor(o8[:], o8[:], moe[:], ALU.add))
                            xg = x_all[:, bass.ds(g * U, U), :]
                            nc.vector.tensor_tensor(xg, xg, o8[:], ALU.add)

                        @block.gpsimd
                        def _(pool):
                            ln_pool(pool, 0)
                    rest()

        if "E" in SECTIONS:
            stage_attn_experts()

        def stage_gru():
            CH, CB = 2, B // 2
            RUN = 8
            with ExitStack() as st:
                wT = sb("F_wT", [D, D], scope=st)
                kern_x = sb("F_kern_x", [D, 3 * D], scope=st)
                kern_c = sb("F_kern_c", [D, 3 * D], scope=st)
                recur = sb("F_recur", [D, 3 * D], scope=st)
                bias = sb("F_bias", [D, 3], scope=st)
                encW = sb("F_encW", [D, B * CL], scope=st)
                decT = sb("F_decT", [D, S, B], scope=st)
                gru = sb("F_gru", [D, S, B], scope=st)
                xloc = sb("F_xloc", [D, RUN, B], scope=st)
                hist = sb("F_hist", [D, RUN + 1, B], scope=st)
                sT = sb("F_sT", [CL, CH, CB], scope=st)
                nm = sb("F_nm", [CB, CH], scope=st)
                den = sb("F_den", [CB, CH], scope=st)
                ex = sb("F_ex", [CB, CH, CL], scope=st)
                eT = sb("F_eT", [CL, CH, CB], scope=st)
                cv = sb("F_cv", [D, CH, CB], scope=st)
                zt = sb("F_zt", [D, CH, CB], scope=st)
                rt = sb("F_rt", [D, CH, CB], scope=st)
                cand = sb("F_cand", [D, CH, CB], scope=st)
                t1 = sb("F_t1", [D, CH, CB], scope=st)
                loads = [(wT[:], dram["L2_xcond_W"]), (kern_x[:], dram["L2_xcond_kernel"][0:D, :]),
                         (kern_c[:], dram["L2_xcond_kernel"][D:2 * D, :]), (recur[:], dram["L2_xcond_recurrent_kernel"]),
                         (bias[:], dram["L2_xcond_bias"].rearrange("(c p) -> p c", p=D))]
                CHUNKS = [(s, min(512, B * CL - s)) for s in range(0, B * CL, 512)]
                with nc.Block() as block:
                    @block.sync
                    def _(sp):
                        for dst, src in loads:
                            sp.dma_start(dst, src, allow_slow_non_contiguous=True).then_inc(sem["loaded"], 16)

                    @block.vector
                    def _(dve):
                        nc.vector.tensor_copy(hist[:, RUN, :], condT[:])
                        dve.wait_ge(sem["loaded"], 16 * len(loads))
                        nc.vector.tensor_scalar(bias[:, 0:2], bias[:, 0:2], 0.5, None, ALU.mult)
                        for i, (s, n) in enumerate(CHUNKS):
                            dve.wait_ge(sem["k_done"], i + 1)
                            nc.vector.tensor_copy(encW[:, s:s + n], ps[:, i, 0:n])

                    @block.tensor
                    def _(pe):
                        pe.wait_ge(sem["loaded"], 16 * len(loads))
                        for i, (s, n) in enumerate(CHUNKS):
                            nc.tensor.matmul(ps[:, i, 0:n], wT[:], ctxT[:, s:s + n], start=True, stop=True).then_inc(sem["k_done"], 1)
                rest()

                with nc.Fori(0, NG) as g:
                    with nc.Block() as block:
                        @block.vector
                        def _(dve):
                            step = Steps(dve, sem["vector_step"])
                            ln_vector(dve, step, 0, lambda u: x_all[:, g * U + u, :]).then_inc(sem["z_ready"], 1)
                            dve.wait_ge(sem["zT_done"], 1)
                            nc.vector.tensor_copy(decT[:, :, bass.ds(g * U, U)], per(0, S).rearrange("p u t -> p t u"))

                        @block.gpsimd
                        def _(pool):
                            ln_pool(pool, 0)

                        @block.tensor
                        def _(pe):
                            turn_rows(pe, 0)
                    rest()

                with nc.Fori(0, S // RUN) as n:
                    with nc.Block() as block:
                        chains = [(t, c) for t in range(RUN) for c in range(CH)]
                        mine = lambda c: slice(CB * c, CB * (c + 1))

                        @block.tensor
                        def _(pe):
                            def early(t, c):
                                k = CH * t + c
                                if t == 0:
                                    pe.wait_ge(sem["x_ready"], 1)
                                else:
                                    pe.wait_ge(sem["mix_added"], k - 1)
                                for j in range(CB):
                                    b = CB * c + j
                                    last = nc.tensor.matmul(ps[0:CL, 4 * c, j:j + 1], encW[:, b * CL:(b + 1) * CL], hist[:, t, b:b + 1],
                                                            start=True, stop=True)
                                last.then_inc(sem["scores_done"], 1)
                                gate = lambda i: ps[:, 4 * c + 3, i * CB:(i + 1) * CB]
                                for i in range(3):
                                    nc.tensor.matmul(gate(i), kern_x[:, i * D:(i + 1) * D], xloc[:, t, mine(c)],
                                                     start=(i == 0), stop=False, skip_group_check=True)
                                for i in range(3):
                                    nc.tensor.matmul(gate(i if i < 2 else 3), recur[:, i * D:(i + 1) * D], hist[:, t, mine(c)],
                                                     start=False, stop=(i == 2), skip_group_check=True)

                            def turn_scores(t, c):
                                pe.wait_ge(sem["k_read"], CH * t + c + 1)
                                nc.tensor.transpose(ps[0:CB, 4 * c + 1, 0:CL], sT[:, c, :], ident[0:CL, 0:CL]).then_inc(sem["turned"], 1)

                            def turn_weights(t, c):
                                pe.wait_ge(sem["shifted"], CH * t + c + 1)
                                nc.tensor.transpose(ps[0:CL, 4 * c + 1, 128:128 + CB], ex[:, c, :], ident[0:CB, 0:CB]).then_inc(sem["o_turned"], 1)

                            def attend(t, c):
                                pe.wait_ge(sem["pT_ready"], CH * t + c + 1)
                                for j in range(CB):
                                    last = nc.tensor.matmul(ps[:, 4 * c + 2, j:j + 1], ctx_tm[:, CB * c + j, :], eT[:, c, j:j + 1], start=True, stop=True)
                                last.then_inc(sem["pv_done"], 1)

                            def late(t, c):
                                pe.wait_ge(sem["o_normed"], CH * t + c + 1)
                                for i in range(3):
                                    last = nc.tensor.matmul(ps[:, 4 * c + 3, i * CB:(i + 1) * CB], kern_c[:, i * D:(i + 1) * D], cv[:, c, :],
                                                            start=False, stop=True, skip_group_check=True)
                                last.then_inc(sem["gate_done"], 1)

                            for t in range(RUN):
                                for part in (early, turn_scores, turn_weights, attend, late):
                                    for c in range(CH):
                                        part(t, c)

                        @block.vector
                        def _(dve):
                            step = Steps(dve, sem["vector_step"])
                            nc.vector.tensor_copy(xloc[:], decT[:, bass.ds(n * RUN, RUN), :])
                            nc.vector.tensor_copy(hist[:, 0, :], hist[:, RUN, :]).then_inc(sem["x_ready"], 1)
                            dve.wait_ge(sem["x_ready"], 1)

                            def scores(t, c):
                                dve.wait_ge(sem["scores_done"], CH * t + c + 1)
                                nc.vector.tensor_copy(sT[:, c, :], ps[0:CL, 4 * c, 0:CB]).then_inc(sem["k_read"], 1)

                            def maximum(t, c):
                                dve.wait_ge(sem["turned"], CH * t + c + 1)
                                nc.vector.tensor_reduce(nm[:, c:c + 1], ps[0:CB, 4 * c + 1, 0:CL], AX.X, ALU.max, negate=True).then_inc(sem["cand_ready"], 1)

                            def weights(t, c):
                                dve.wait_ge(sem["exp_done"], CH * t + c + 1)
                                step(nc.vector.reciprocal(den[:, c:c + 1], den[:, c:c + 1]))
                                nc.vector.tensor_scalar(ex[:, c, :], ex[:, c, :], den[:, c:c + 1], None, ALU.mult).then_inc(sem["shifted"], 1)

                            def turned(t, c):
                                dve.wait_ge(sem["o_turned"], CH * t + c + 1)
                                nc.vector.tensor_copy(eT[:, c, :], ps[0:CL, 4 * c + 1, 128:128 + CB]).then_inc(sem["pT_ready"], 1)

                            def attended(t, c):
                                dve.wait_ge(sem["pv_done"], CH * t + c + 1)
                                nc.vector.tensor_copy(cv[:, c, :], ps[:, 4 * c + 2, 0:CB]).then_inc(sem["o_normed"], 1)

                            def candidate(t, c):
                                dve.wait_ge(sem["gate_ready"], 2 * (CH * t + c) + 1)
                                gate = lambda i: ps[:, 4 * c + 3, i * CB:(i + 1) * CB]
                                dve.wait_ge(sem["gate_ready"], 2 * (CH * t + c) + 2)
                                step(nc.vector.scalar_tensor_tensor(out=t1[:, c, :], in0=rt[:, c, :], scalar=1.0, in1=gate(3), op0=ALU.add, op1=ALU.mult))
                                nc.vector.scalar_tensor_tensor(out=t1[:, c, :], in0=t1[:, c, :], scalar=0.5, in1=gate(2), op0=ALU.mult, op1=ALU.add).then_inc(sem["hid_done"], 1)

                            def state(t, c):
                                dve.wait_ge(sem["hid_ready"], CH * t + c + 1)
                                step(nc.vector.tensor_tensor(t1[:, c, :], hist[:, t, mine(c)], cand[:, c, :], ALU.subtract))
                                step(nc.vector.scalar_tensor_tensor(out=t1[:, c, :], in0=zt[:, c, :], scalar=1.0, in1=t1[:, c, :], op0=ALU.add, op1=ALU.mult))
                                nc.vector.scalar_tensor_tensor(out=hist[:, t + 1, mine(c)], in0=t1[:, c, :], scalar=0.5, in1=cand[:, c, :],
                                                               op0=ALU.mult, op1=ALU.add).then_inc(sem["mix_added"], 1)

                            for t in range(RUN):
                                for part in (scores, maximum, weights, turned, attended, candidate, state):
                                    for c in range(CH):
                                        part(t, c)
                            dve.wait_ge(sem["mix_added"], CH * RUN)
                            nc.vector.tensor_copy(gru[:, bass.ds(n * RUN, RUN), :], hist[:, 1:RUN + 1, :])

                        @block.scalar
                        def _(act):
                            def exponentials(t, c):
                                act.wait_ge(sem["cand_ready"], CH * t + c + 1)
                                nc.scalar.activation(ex[:, c, :], ps[0:CB, 4 * c + 1, 0:CL], ACT.Exp, bias=nm[:, c:c + 1],
                                                     accum_out=den[:, c:c + 1]).then_inc(sem["exp_done"], 1)

                            def gates(t, c):
                                act.wait_ge(sem["gate_done"], CH * t + c + 1)
                                for i, dst in ((1, rt), (0, zt)):
                                    nc.scalar.activation(dst[:, c, :], ps[:, 4 * c + 3, i * CB:(i + 1) * CB], ACT.Tanh, bias=bias[:, i:i + 1],
                                                         scale=0.5).then_inc(sem["gate_ready"], 1)

                            def candidates(t, c):
                                act.wait_ge(sem["hid_done"], CH * t + c + 1)
                                nc.scalar.activation(cand[:, c, :], t1[:, c, :], ACT.Tanh, bias=bias[:, 2:3]).then_inc(sem["hid_ready"], 1)

                            for t in range(RUN):
                                for part in (exponentials, gates, candidates):
                                    for c in range(CH):
                                        part(t, c)
                    rest()

                with nc.Block() as block:
                    @block.tensor
                    def _(pe):
                        for i in range(NG):
                            for u in range(U):
                                last = nc.tensor.transpose(ps[:, i, u * D:(u + 1) * D], gru[:, :, i * U + u], ident[:])
                            last.then_inc(sem["turned"], 1)

                    @block.vector
                    def _(dve):
                        for i in range(NG):
                            dve.wait_ge(sem["turned"], i + 1)
                            nc.vector.tensor_tensor(x_all[:, i * U:(i + 1) * U, :], x_all[:, i * U:(i + 1) * U, :], per(i), ALU.add)
                rest()

        if "F" in SECTIONS:
            stage_gru()

        def stage_moe():
            with ExitStack() as st:
                wg = sb("G_wg", [D, EXPERTS], scope=st)
                bg = sb("G_bg", [1, EXPERTS], scope=st)
                w1 = sb("G_w1", [D, EXPERTS, FFN], scope=st)
                b1 = sb("G_b1", [D, EXPERTS, 4], scope=st)
                w2 = sb("G_w2", [D, EXPERTS, 4, D], scope=st)
                b2 = sb("G_b2", [1, EXPERTS, D], scope=st)
                hid = sb("G_hid", [D, 2, 4, U * S], scope=st)
                loads = [(wg[:], dram["L2_ffn_gate_w"]), (bg[:], dram["L2_ffn_gate_b"].unsqueeze(0)),
                         (b2[:], dram["L2_ffn_b2"].unsqueeze(0))]
                for x in range(EXPERTS):
                    loads.append((w1[:, x, :], dram["L2_ffn_w1"][x]))
                    loads.append((b1[:, x, :], dram["L2_ffn_b1"][x].rearrange("(c p) -> p c", p=D)))
                    loads.append((w2[:, x], dram["L2_ffn_w2"][x].rearrange("(c p) n -> p c n", p=D)))
                with nc.Block() as block:
                    @block.sync
                    def _(sp):
                        for dst, src in loads:
                            sp.dma_start(dst, src, allow_slow_non_contiguous=True).then_inc(sem["loaded"], 16)
                        sp.wait_ge(sem["loaded"], 16 * len(loads))

                    @block.vector
                    def _(dve):
                        nc.vector.memset(gates[:], PAD)
                rest()

                with nc.Fori(0, NG) as g:
                    with nc.Block() as block:
                        @block.tensor
                        def _(pe):
                            turn_rows(pe, 0, bank=TURN)
                            pe.wait_ge(sem["xnT_ready"], 1)
                            for u in range(U):
                                nc.tensor.matmul(per(TURN, EXPERTS)[:, u, :], xnT[:, u * S:(u + 1) * S], wg[:], start=True, stop=False)
                                last = nc.tensor.matmul(per(TURN, EXPERTS)[:, u, :], ones[0:1, :], bg[:], start=False, stop=True)
                            last.then_inc(sem["gate_done"], 1)

                            def hidden(x):
                                for c in range(4):
                                    bank = job_bank(pe, 4 * x + c)
                                    nc.tensor.matmul(ps[:, bank, :], w1[:, x, c * D:(c + 1) * D], xnT[:], start=True, stop=True).then_inc(sem["proj_done"], 1)

                            hidden(0)
                            for x in range(EXPERTS):
                                if x + 1 < EXPERTS:
                                    hidden(x + 1)
                                jobs_read(pe, 4 * x + 4)
                                if x >= 2:
                                    pe.wait_ge(sem["mix_added"], x - 1)
                                for u in range(U):
                                    for c in range(4):
                                        nc.tensor.matmul(per(OUT + x % 2)[:, u, :], hid[:, x % 2, c, u * S:(u + 1) * S], w2[:, x, c, :],
                                                         start=(c == 0), stop=False)
                                    last = nc.tensor.matmul(per(OUT + x % 2)[:, u, :], ones[0:1, :], b2[:, x, :], start=False, stop=True)
                                last.then_inc(sem["mix_done"], 1)

                        def relu_job(eng, k):
                            x, c = k // 4, k % 4
                            eng.wait_ge(sem["proj_done"], k + 1)
                            if x >= 2 and c < 2:
                                eng.wait_ge(sem["mix_done"], x - 1)
                            dst, src = hid[:, x % 2, c, :], ps[:, c, :]
                            if k % 2 == 0:
                                nc.scalar.activation(dst, src, ACT.Relu, bias=b1[:, x, c:c + 1]).then_inc(sem["q_read"], 1)
                            else:
                                nc.vector.tensor_scalar(dst, src, b1[:, x, c:c + 1], 0.0, ALU.add, ALU.max).then_inc(sem["k_read"], 1)

                        @block.scalar
                        def _(act):
                            act.wait_ge(sem["zT_done"], 1)
                            nc.scalar.activation(xnT[:], ps[:, TURN, :], ACT.Copy).then_inc(sem["xnT_ready"], 1)
                            route_scalar(act)
                            for k in range(0, 4 * EXPERTS, 2):
                                relu_job(act, k)

                        @block.vector
                        def _(dve):
                            step = Steps(dve, sem["vector_step"])
                            ln_vector(dve, step, 0, lambda u: x_all[:, g * U + u, :]).then_inc(sem["z_ready"], 1)
                            step(nc.vector.tensor_copy(xs[:], x_all[:, bass.ds(g * U, U), :]))
                            route_vector(dve, step, TURN, False)
                            relu_job(dve, 1)
                            relu_job(dve, 3)
                            for x in range(EXPERTS):
                                if x + 1 < EXPERTS:
                                    relu_job(dve, 4 * x + 5)
                                    relu_job(dve, 4 * x + 7)
                                dve.wait_ge(sem["mix_done"], x + 1)
                                for u in range(U):
                                    last = nc.vector.scalar_tensor_tensor(out=xs[:, u, :], in0=per(OUT + x % 2)[:, u, :], scalar=chosen[:, u, x:x + 1],
                                                                          in1=xs[:, u, :], op0=ALU.mult, op1=ALU.add)
                                last.then_inc(sem["mix_added"], 1)
                                dve.wait_ge(sem["mix_added"], x + 1)
                            nc.vector.tensor_copy(x_all[:, bass.ds(g * U, U), :], xs[:])

                        @block.gpsimd
                        def _(pool):
                            ln_pool(pool, 0)
                    rest()

        if "G" in SECTIONS:
            stage_moe()

        def stage_layers():
            R = HD + 1
            NPAIR = 4
            with ExitStack() as st:
                y_all = sb("H_y", [S, B, D], scope=st)
                square = ["q_w", "qs_w", "k_w", "ks_w", "v_w", "cqs_w", "cks_w"]
                w = {n: sb("H_" + n, [D, D], scope=st) for n in square}
                plain = ["so_w", "cq_w", "ck_w", "cv_w", "co_w"]
                w.update({n: sb("H_" + n, [D, D], scope=st) for n in plain})
                f1 = sb("H_f1", [D, FFN], scope=st)
                f1b = sb("H_f1b", [D, 4], scope=st)
                f2 = sb("H_f2", [D, 4, D], scope=st)
                f2b = sb("H_f2b", [1, D], scope=st)
                nw = sb("H_nw", [D, 3, 2 * D], scope=st)
                nb = sb("H_nb", [D, 3, 2], scope=st)
                gb = sb("H_gb", [D, 3, 2, B], scope=st)
                gb4 = sb("H_gb4", [D, 3, 2, U], scope=st)
                cosT = sb("H_cos", [D, S], scope=st)
                sinT = sb("H_sin", [D, S], scope=st)
                ctxg = sb("H_ctxg", [D, UC], scope=st)
                ta = sb("H_ta", [D, 2, U * S], scope=st)
                tb = sb("H_tb", [D, 2, U * S], scope=st)
                rows = sb("H_rows", [D, 2, U * S], scope=st)
                q4 = sb("H_q4", [128, 4, U * S], scope=st)
                k4 = sb("H_k4", [128, 4, U * S], scope=st)
                c4 = sb("H_c4", [128, 4, UC], scope=st)
                v9 = sb("H_v9", [S, U, NH, R], scope=st)
                cv9 = sb("H_cv9", [CL, U, NH, R], scope=st)
                o8 = sb("H_o8", [S, U, D], scope=st)
                hid = sb("H_hid", [D, 4, U * S], scope=st)
                mask_s = sb("H_mask_s", [NG, U * S // 4], mybir.dt.uint32, scope=st)
                mask_c = sb("H_mask_c", [NG, UC // 4], mybir.dt.uint32, scope=st)
                low_s = sb("H_low_s", [NG, U * S], scope=st)
                low_c = sb("H_low_c", [NG, UC], scope=st)
                masks = nc.dram_tensor("masks_way", (NG, U * S), F32, kind="Internal").ap()
                masks_c = nc.dram_tensor("masks_c_way", (NG, UC), F32, kind="Internal").ap()
                ways = [nc.dram_tensor(f"pair_way{p}", (D, U * S), F32, kind="Internal").ap() for p in range(NPAIR)]

                with nc.Block() as block:
                    @block.sync
                    def _(sp):
                        sp.dma_start(cosT[:], dram["cosT"]).then_inc(sem["loaded"], 16)
                        sp.dma_start(sinT[:], dram["sinT"]).then_inc(sem["loaded"], 16)
                        sp.dma_start(mask_s[:], dram["mask_BxS_bf0"].rearrange("(g c) -> g c", g=NG)).then_inc(sem["loaded"], 16)
                        sp.dma_start(mask_c[:], dram["mask_BxS2_bf0"].rearrange("(g c) -> g c", g=NG)).then_inc(sem["loaded"], 16)
                        sp.wait_ge(sem["table_ready"], 2)
                        sp.dma_start(masks, low_s[:]).then_inc(sem["stored"], 16)
                        sp.dma_start(masks_c, low_c[:]).then_inc(sem["stored"], 16)
                        sp.wait_ge(sem["stored"], 32)

                    @block.vector
                    def _(dve):
                        for t in (q4, k4, c4, v9, cv9):
                            nc.vector.memset(t[:], 1.0)
                        dve.wait_ge(sem["loaded"], 64)
                        nc.vector.tensor_scalar(low_s[:], mask_s[:].bitcast(U8), MASKED, None, ALU.mult).then_inc(sem["table_ready"], 1)
                        nc.vector.tensor_scalar(low_c[:], mask_c[:].bitcast(U8), MASKED, None, ALU.mult).then_inc(sem["table_ready"], 1)
                rest()

                with nc.Fori(0, NG) as g:
                    with nc.Block() as block:
                        @block.vector
                        def _(dve):
                            step = Steps(dve, sem["vector_step"])
                            ln_vector(dve, step, 0, lambda u: x_all[:, g * U + u, :], lambda u: y_all[:, g * U + u, :])

                        @block.gpsimd
                        def _(pool):
                            ln_pool(pool, 0)
                    rest()

                def layer_loads(l):
                    one = lambda name, pat, **kw: dram[name][bass.ds(l, 1)].rearrange(pat, **kw)
                    out = [(w[n][:], one("L3_" + n, "a p n -> p (a n)")) for n in square]
                    out += [(w[n][:], one("L3_xcond_" + n, "a p n -> p (a n)")) for n in plain]
                    out += [(f1[:], one("L3_xcond_f1_w", "a p n -> p (a n)")),
                            (f1b[:], one("L3_xcond_f1_b", "a (c p) -> p (a c)", p=D)),
                            (f2[:], one("L3_xcond_f2_w", "a (c p) n -> p (a c) n", p=D)),
                            (f2b[:], one("L3_xcond_f2_b", "a n -> a n"))]
                    for i in range(3):
                        out.append((nw[:, i, :], one(f"L3_xcond_n{i + 1}_w", "a p n -> p (a n)")))
                        out.append((nb[:, i, :], one(f"L3_xcond_n{i + 1}_b", "a (c p) -> p (a c)", p=D)))
                    return out

                with nc.Fori(0, LAYERS) as l:
                    with nc.Block() as block:
                        n_loads = 22

                        @block.sync
                        def _(sp):
                            loads = layer_loads(l)
                            assert len(loads) == n_loads
                            for dst, src in loads:
                                sp.dma_start(dst, src, allow_slow_non_contiguous=True).then_inc(sem["loaded"], 16)

                        @block.tensor
                        def _(pe):
                            pe.wait_ge(sem["loaded"], 16 * n_loads)
                            for n in range(3):
                                for c in range(2):
                                    last = nc.tensor.matmul(ps[:, 0, (2 * n + c) * B:(2 * n + c + 1) * B], nw[:, n, c * D:(c + 1) * D],
                                                            condT[:], start=True, stop=True)
                            last.then_inc(sem["proj_done"], 1)

                        @block.vector
                        def _(dve):
                            step = Steps(dve, sem["vector_step"])
                            dve.wait_ge(sem["loaded"], 16 * n_loads)
                            step(nc.vector.tensor_scalar(nb[:, :, 0], nb[:, :, 0], 1.0, None, ALU.add))
                            dve.wait_ge(sem["proj_done"], 1)
                            nc.vector.tensor_tensor(gb[:].rearrange("p n c b -> p (n c) b"),
                                                    ps[:, 0, 0:6 * B].rearrange("p (n b) -> p n b", b=B),
                                                    nb[:].rearrange("p n c -> p (n c)").unsqueeze(2).broadcast_to([D, 6, B]), ALU.add)
                    rest()

                    with nc.Fori(0, NG) as g:
                        with nc.Block() as block:
                            pair_cols = (UC, U * S, U * S, U * S)
                            pair_to = (c4, q4, k4, q4)
                            pair_banks = ((4, 5), (0, 1), (2, 3), (0, 1))

                            @block.sync
                            def _(sp):
                                for q in range(4):
                                    at = 32 * q + HD
                                    sp.dma_start(k4[at:at + 1, :, :], masks[bass.ds(g, 1), :].unsqueeze(1).broadcast_to([1, 4, U * S])).then_inc(sem["loaded"], 16)
                                    sp.dma_start(c4[at:at + 1, :, :], masks_c[bass.ds(g, 1), :].unsqueeze(1).broadcast_to([1, 4, UC])).then_inc(sem["loaded"], 16)
                                for p in range(NPAIR):
                                    spread(sp, ways[p], rows[:, p % 2, 0:pair_cols[p]], pair_to[p], pair_cols[p],
                                           (sem["table_ready"], p + 1), sem["loaded_q"], p + 1)

                            @block.tensor
                            def _(pe):
                                def pair(p, a, b, src, cols):
                                    for bank, m in zip(pair_banks[p], (a, b)):
                                        last = nc.tensor.matmul(ps[:, bank, 0:cols], w[m][:], src[:, 0:cols], start=True, stop=True)
                                    last.then_inc(sem["q_done"], 1)

                                def outputs(a, m):
                                    pe.wait_ge(sem["o_normed"], NU * a)
                                    for u in range(U):
                                        last = nc.tensor.transpose(ps[:, TURN, u * S:(u + 1) * S], o8[:, u, :], ident[:])
                                    last.then_inc(sem["o_turned"], 1)
                                    pe.wait_ge(sem["oT_ready"], a)
                                    for u in range(U):
                                        last = nc.tensor.matmul(per(OUT)[:, u, :], xnT[:, u * S:(u + 1) * S], w[m][:], start=True, stop=True)
                                    last.then_inc(sem["mix_done"], 1)

                                pe.wait_ge(sem["x_ready"], 1)
                                pair(0, "ck_w", "cks_w", ctxg, UC)
                                for u in range(U):
                                    last = nc.tensor.matmul(per(7)[0:CL, u, :], ctxg[:, u * CL:(u + 1) * CL], w["cv_w"][:], start=True, stop=True)
                                last.then_inc(sem["v_done"], 1)
                                turn_rows(pe, 0, bank=6)
                                pe.wait_ge(sem["xnT_ready"], 1)
                                pair(1, "q_w", "qs_w", xnT, U * S)
                                pair(2, "k_w", "ks_w", xnT, U * S)
                                pe.wait_ge(sem["v_read"], 1)
                                for u in range(U):
                                    last = nc.tensor.matmul(per(7)[:, u, :], xnT[:, u * S:(u + 1) * S], w["v_w"][:], start=True, stop=True)
                                last.then_inc(sem["v_done"], 1)
                                pe.wait_ge(sem["v_read"], 2)
                                pe.wait_ge(sem["rope_done"], 3)
                                pe.wait_ge(sem["loaded"], 16 * 8)
                                pe.wait_ge(sem["loaded_q"], 64 * 3)
                                tile4 = lambda t, n: (lambda h, u: t[32 * (h // 4):32 * (h // 4) + R, h % 4, u * n:(u + 1) * n])
                                attn_tensor(pe, 0, S, False, tile4(q4, S), tile4(k4, S), lambda h, u: v9[:, u, h, :])
                                outputs(1, "so_w")
                                turn_rows(pe, 1, bank=TURN)
                                pe.wait_ge(sem["xnT_ready"], 2)
                                pair(3, "cq_w", "cqs_w", xnT, U * S)
                                pe.wait_ge(sem["rope_done"], 4)
                                pe.wait_ge(sem["loaded_q"], 64 * 4)
                                attn_tensor(pe, 1, CL, False, tile4(q4, S), tile4(c4, CL), lambda h, u: cv9[:, u, h, :])
                                outputs(2, "co_w")
                                turn_rows(pe, 2, bank=TURN)
                                pe.wait_ge(sem["xnT_ready"], 3)
                                for c in range(4):
                                    nc.tensor.matmul(ps[:, c, :], f1[:, c * D:(c + 1) * D], xnT[:], start=True, stop=True).then_inc(sem["hid_done"], 1)
                                pe.wait_ge(sem["hid_ready"], 4)
                                for u in range(U):
                                    for c in range(4):
                                        nc.tensor.matmul(per(OUT)[:, u, :], hid[:, c, u * S:(u + 1) * S], f2[:, c, :], start=(c == 0), stop=False)
                                    last = nc.tensor.matmul(per(OUT)[:, u, :], ones[0:1, :], f2b[:], start=False, stop=True)
                                last.then_inc(sem["mix_done"], 1)

                            @block.scalar
                            def _(act):
                                def affine(a, bank):
                                    act.wait_ge(sem["zT_done"], a + 1)
                                    for u in range(U):
                                        last = nc.scalar.activation(xnT[:, u * S:(u + 1) * S], ps[:, bank, u * S:(u + 1) * S], ACT.Identity,
                                                                    bias=gb4[:, a, 1, u:u + 1], scale=gb4[:, a, 0, u:u + 1])
                                    last.then_inc(sem["xnT_ready"], 1)

                                def outputs(a):
                                    act.wait_ge(sem["o_turned"], a)
                                    nc.scalar.activation(xnT[:], ps[:, TURN, :], ACT.Copy).then_inc(sem["oT_ready"], 1)

                                act.wait_ge(sem["v_done"], 1)
                                nc.scalar.activation(cv9[:, :, :, 0:HD], per(7)[0:CL].rearrange("p u (h d) -> p u h d", d=HD), ACT.Copy).then_inc(sem["v_read"], 1)
                                act.wait_ge(sem["x_ready"], 2)
                                affine(0, 6)
                                act.wait_ge(sem["v_done"], 2)
                                nc.scalar.activation(v9[:, :, :, 0:HD], per(7).rearrange("p u (h d) -> p u h d", d=HD), ACT.Copy).then_inc(sem["v_read"], 1)
                                attn_scalar(act, 0, S, HD ** -0.5)
                                outputs(1)
                                affine(1, TURN)
                                attn_scalar(act, 1, CL, HD ** -0.5)
                                outputs(2)
                                affine(2, TURN)
                                for c in range(4):
                                    act.wait_ge(sem["hid_done"], c + 1)
                                    nc.scalar.activation(hid[:, c, :], ps[:, c, :], ACT.Gelu, bias=f1b[:, c:c + 1]).then_inc(sem["hid_ready"], 1)

                            @block.vector
                            def _(dve):
                                step = Steps(dve, sem["vector_step"])

                                def rotate(p):
                                    n = CL if p == 0 else S
                                    dve.wait_ge(sem["q_done"], p + 1)
                                    if p >= 2:
                                        dve.wait_ge(sem["table_ready"], p - 1)
                                    for bank, table, t in zip(pair_banks[p], (cosT, sinT), (ta, tb)):
                                        last = nc.vector.tensor_tensor(t[:, p % 2, 0:U * n].rearrange("p (u t) -> p u t", u=U), per(bank, n),
                                                                       table[:, 0:n].unsqueeze(1).broadcast_to([D, U, n]), ALU.mult)
                                    last.then_inc(sem["rope_done"], 1)

                                nc.vector.tensor_copy(ctxg[:], ctxT[:, bass.ds(g * UC, UC)]).then_inc(sem["x_ready"], 1)
                                nc.vector.tensor_copy(gb4[:].rearrange("p n c u -> p (n c) u"),
                                                      gb[:].rearrange("p n c b -> p (n c) b")[:, :, bass.ds(g * U, U)]).then_inc(sem["x_ready"], 1)
                                step(nc.vector.tensor_copy(xs[:], y_all[:, bass.ds(g * U, U), :]))
                                ln_vector(dve, step, 0, lambda u: xs[:, u, :]).then_inc(sem["z_ready"], 1)
                                for p in range(3):
                                    rotate(p)
                                attn_vector(dve, step, 0, S, False, lambda u: o8[:, u, :])
                                dve.wait_ge(sem["mix_done"], 1)
                                step(nc.vector.tensor_tensor(xs[:], xs[:], per(OUT), ALU.add))
                                ln_vector(dve, step, 1, lambda u: xs[:, u, :]).then_inc(sem["z_ready"], 1)
                                rotate(3)
                                attn_vector(dve, step, 1, CL, False, lambda u: o8[:, u, :])
                                dve.wait_ge(sem["mix_done"], 2)
                                step(nc.vector.tensor_tensor(xs[:], xs[:], per(OUT), ALU.add))
                                ln_vector(dve, step, 2, lambda u: xs[:, u, :]).then_inc(sem["z_ready"], 1)
                                dve.wait_ge(sem["mix_done"], 3)
                                nc.vector.tensor_tensor(y_all[:, bass.ds(g * U, U), :], xs[:], per(OUT), ALU.add)

                            @block.gpsimd
                            def _(pool):
                                def add_pair(p):
                                    pool.wait_ge(sem["rope_done"], p + 1)
                                    if p >= 2:
                                        pool.wait_ge(sem["saved"], 16 * (p - 1))
                                    at = (slice(None), p % 2, slice(0, pair_cols[p]))
                                    nc.gpsimd.tensor_tensor(rows[at], ta[at], tb[at], ALU.add).then_inc(sem["table_ready"], 1)

                                ln_pool(pool, 0)
                                for p in range(3):
                                    add_pair(p)
                                ln_pool(pool, 1)
                                add_pair(3)
                                ln_pool(pool, 2)
                        rest()

                with nc.Block() as block:
                    @block.vector
                    def _(dve):
                        nc.vector.tensor_tensor(x_all[:], x_all[:], y_all[:], ALU.add)
                rest()

        if "H" in SECTIONS:
            stage_layers()

        def stage_ternary():
            with ExitStack() as st:
                wfc = sb("I_wfc", [D, FFN], scope=st)
                wpj = sb("I_wpj", [D, FFN], scope=st)
                neg = sb("I_neg", [D, FFN], scope=st)
                lnw = sb("I_lnw", [D, 4], scope=st)
                lnb = sb("I_lnb", [D, 4], scope=st)
                mag = sb("I_mag", [D, 2], scope=st)
                thr = sb("I_thr", [D, 2], scope=st)
                nthr = sb("I_nthr", [D, 2], scope=st)
                hid = sb("I_hid", [S, U, FFN], scope=st)
                hidT = sb("I_hidT", [D, 4, U * S], scope=st)
                loads = [(wfc[:], dram["L3_ffn_W_fc"]),
                         (wpj[:].rearrange("p (c n) -> p c n", c=4), dram["L3_ffn_W_proj"].rearrange("(c p) n -> p c n", p=D)),
                         (lnw[:], dram["L3_ffn_ln_w"].rearrange("(c p) -> p c", p=D)),
                         (lnb[:], dram["L3_ffn_ln_b"].rearrange("(c p) -> p c", p=D))]
                with nc.Block() as block:
                    @block.sync
                    def _(sp):
                        for dst, src in loads:
                            sp.dma_start(dst, src, allow_slow_non_contiguous=True).then_inc(sem["loaded"], 16)

                    @block.vector
                    def _(dve):
                        step = Steps(dve, sem["vector_step"])
                        dve.wait_ge(sem["loaded"], 16 * len(loads))
                        nc.vector.tensor_reduce(mag[:, 0:1], wfc[:], AX.X, ALU.add, apply_absolute_value=True)
                        nc.vector.tensor_reduce(mag[:, 1:2], wpj[:], AX.X, ALU.add, apply_absolute_value=True).then_inc(sem["z_ready"], 1)
                        dve.wait_ge(sem["zT_done"], 1)
                        step(nc.vector.tensor_scalar(thr[:], ps[:, 0, 0:2], 1.0 / (D * FFN), 1e-6, ALU.mult, ALU.add))
                        step(nc.vector.tensor_scalar(thr[:], thr[:], 0.5, None, ALU.mult))
                        step(nc.vector.tensor_scalar(nthr[:], thr[:], -1.0, None, ALU.mult))
                        for i, w in enumerate((wfc, wpj)):
                            step(nc.vector.tensor_scalar(neg[:], w[:], nthr[:, i:i + 1], None, ALU.is_lt))
                            step(nc.vector.scalar_tensor_tensor(out=w[:], in0=w[:], scalar=thr[:, i:i + 1], in1=neg[:],
                                                                op0=ALU.is_gt, op1=ALU.subtract))

                    @block.tensor
                    def _(pe):
                        pe.wait_ge(sem["z_ready"], 1)
                        nc.tensor.matmul(ps[:, 0, 0:2], ones[:], mag[:], start=True, stop=True).then_inc(sem["zT_done"], 1)
                rest()

                with nc.Fori(0, NG) as g:
                    with nc.Block() as block:
                        @block.tensor
                        def _(pe):
                            turn_rows(pe, 0, bank=TURN)
                            pe.wait_ge(sem["xnT_ready"], 1)
                            for u in range(U):
                                nc.tensor.matmul(ps[:, u, :], xnT[:, u * S:(u + 1) * S], wfc[:], start=True, stop=True).then_inc(sem["hid_done"], 1)
                            pe.wait_ge(sem["z_ready"], 2)
                            for c in range(4):
                                for u in range(U):
                                    last = nc.tensor.transpose(ps[:, c, u * S:(u + 1) * S], hid[:, u, c * D:(c + 1) * D], ident[:])
                                last.then_inc(sem["turned"], 1)
                            pe.wait_ge(sem["pT_ready"], 4)
                            for u in range(U):
                                for c in range(4):
                                    last = nc.tensor.matmul(per(OUT)[:, u, :], hidT[:, c, u * S:(u + 1) * S], wpj[:, c * D:(c + 1) * D],
                                                            start=(c == 0), stop=(c == 3))
                            last.then_inc(sem["mix_done"], 1)

                        @block.scalar
                        def _(act):
                            act.wait_ge(sem["zT_done"], 1)
                            nc.scalar.activation(xnT[:], ps[:, TURN, :], ACT.Copy).then_inc(sem["xnT_ready"], 1)
                            for u in range(U):
                                act.wait_ge(sem["hid_done"], u + 1)
                                last = nc.scalar.activation(hid[:, u, :], ps[:, u, :], ACT.Gelu).then_inc(sem["hid_ready"], 1)
                            for c in range(4):
                                act.wait_ge(sem["turned"], c + 1)
                                nc.scalar.activation(hidT[:, c, :], ps[:, c, :], ACT.Identity, bias=lnb[:, c:c + 1],
                                                     scale=lnw[:, c:c + 1]).then_inc(sem["pT_ready"], 1)

                        @block.vector
                        def _(dve):
                            step = Steps(dve, sem["vector_step"])
                            ln_vector(dve, step, 0, lambda u: x_all[:, g * U + u, :]).then_inc(sem["z_ready"], 1)
                            dve.wait_ge(sem["hid_ready"], U)
                            ln_vector(dve, step, 1, lambda u: hid[:, u, :], lambda u: hid[:, u, :]).then_inc(sem["z_ready"], 1)
                            dve.wait_ge(sem["mix_done"], 1)
                            xg = x_all[:, bass.ds(g * U, U), :]
                            nc.vector.tensor_tensor(xg, xg, per(OUT), ALU.add)

                        @block.gpsimd
                        def _(pool):
                            ln_pool(pool, 0)
                            ln_pool(pool, 1)
                    rest()

        if "I" in SECTIONS:
            stage_ternary()

        with nc.Block() as block:
            @block.sync
            def _(sp):
                sp.dma_start(out.rearrange("b t d -> t b d"), x_all[:]).then_inc(sem["stored"], 16)
                sp.wait_ge(sem["stored"], 16)


_TRANSPOSED = ["L0_ffn_expert_down", "L2_xcond_W", "L3_ffn_W_fc", "L3_ffn_W_proj"]


def kernel(**inputs):
    import concourse.bacc as _bacc
    from concourse.bass_utils import run_bass_kernel_spmd as _run

    f32 = np.float32
    arrays = {}
    for name, a in inputs.items():
        a = np.asarray(a)
        if a.dtype == np.bool_:
            a = np.ascontiguousarray(a).reshape(-1).view(np.uint32)
        arrays[name] = a
    for name in _TRANSPOSED:
        arrays[name] = arrays[name].T
    arrays["condT"] = arrays["cond_1024"].T
    for name in ("n1_w", "n2_w", "n3_w", "qkv_w", "so_w", "cq_w", "ck_w", "cv_w", "co_w", "f1_w", "f2_w"):
        arrays["L3_xcond_" + name] = arrays["L3_xcond_" + name].transpose(0, 2, 1)
    swap = np.arange(D).reshape(NH, 2, HD // 2)[:, ::-1, :].reshape(-1)
    qkv = arrays["L3_xcond_qkv_w"]
    arrays["L3_q_w"], arrays["L3_k_w"], arrays["L3_v_w"] = qkv[:, :, 0:D], qkv[:, :, D:2 * D], qkv[:, :, 2 * D:]
    arrays["L3_qs_w"] = arrays["L3_q_w"][:, :, swap]
    arrays["L3_ks_w"] = arrays["L3_k_w"][:, :, swap]
    arrays["L3_cqs_w"] = arrays["L3_xcond_cq_w"][:, :, swap]
    arrays["L3_cks_w"] = arrays["L3_xcond_ck_w"][:, :, swap]
    arrays["ident"] = np.eye(128, dtype=f32)
    half = HD // 2
    inv = (1.0 / 10000.0 ** (np.arange(half, dtype=f32) / f32(half))).astype(f32)
    ang = np.arange(S, dtype=f32)[:, None] * inv
    cos = np.cos(ang).astype(f32).T
    sin = np.sin(ang).astype(f32).T
    arrays["cosT"] = np.tile(np.concatenate([cos, cos]), (NH, 1))
    arrays["sinT"] = np.tile(np.concatenate([-sin, sin]), (NH, 1))
    rows = np.arange(D) // 16
    arrays["block_mask"] = (rows[:, None] == np.arange(8)[None, :]).astype(f32)

    nc = _bacc.Bacc("TRN2", target_bir_lowering=False, num_devices=1)
    dram, given = {}, {}
    for name, a in arrays.items():
        a = np.ascontiguousarray(a)
        given["in_" + name] = a
        dram[name] = nc.dram_tensor("in_" + name, a.shape, mybir.dt.from_np(a.dtype), kind="ExternalInput").ap()
    out = nc.dram_tensor("out_x", (B, S, D), F32, kind="ExternalOutput").ap()
    build(nc, dram, out)
    r = _run(nc, [given], core_ids=[0])
    return r.results[0]["out_x"]
```

```python
from contextlib import ExitStack

import numpy as np

import concourse.bass as bass
from concourse import mybir

SECTIONS = "ACDEFGHI"

F32 = mybir.dt.float32
U8 = mybir.dt.uint8
BF16 = mybir.dt.bfloat16
F16 = mybir.dt.float16
ALU = mybir.AluOpType
ACT = mybir.ActivationFunctionType
AX = mybir.AxisListType

B = 32
S = 128
D = 128
CL = 77
U = 4
NG = B // U
UC = U * CL
NH = 16
HD = D // NH
HL = 8
NU = U * NH // HL
SCORE, TURN, OUT = 0, 4, 6
LN_EPS = 1e-5
MASKED = -1e30
LAYERS = 6
FFN = 512
EXPERTS = 8

SIGNALS = [
    "loaded", "loaded_q", "stored", "vector_step", "scalar_step", "pool_step",
    "var_ready", "rstd_ready", "z_ready", "zT_done", "xnT_ready",
    "scores_done", "shifted", "exp_done", "turned", "pT_ready", "pv_done", "o_normed",
    "proj_done", "proj_read", "k_done", "k_read", "v_done", "v_read", "q_done", "q_read",
    "rope_done", "spread", "o_turned", "oT_ready", "mix_done", "mix_added",
    "hid_done", "hid_ready", "ffn_done", "ffn_added", "gate_done", "gate_ready",
    "upd_done", "upd_ready", "expert_done", "expert_ready", "x_ready", "gram_done",
    "rest_ready", "masked_a", "masked_v", "saved", "table_ready", "outer_ready", "cand_ready",
]


class Steps:

    def __init__(self, eng, sem):
        self.eng, self.sem, self.n = eng, sem, 0

    def __call__(self, ins):
        ins.then_inc(self.sem, 1)
        self.n += 1
        self.eng.wait_ge(self.sem, self.n)


def build(nc, dram, out):
    with ExitStack() as ctx:
        def sb(name, shape, dt=F32, scope=ctx):
            return scope.enter_context(nc.sbuf_tensor(name, shape, dt))

        sem = {name: ctx.enter_context(nc.semaphore(name)) for name in SIGNALS}
        numbers = sorted(s.num for s in sem.values())
        all_signals = range(numbers[0], numbers[-1] + 1)
        assert len(numbers) == len(all_signals)

        def rest():
            nc.sync.sem_clear(all_signals)
            nc.all_engine_barrier()

        x_all = sb("x_all", [S, B, D])
        ctx_tm = sb("ctx_tm", [CL, B, D])
        ctxT = sb("ctxT", [D, B * CL])
        condT = sb("condT", [D, B])
        ident = sb("ident", [128, 128])
        ones = sb("ones", [128, 128])
        neghalf = sb("neghalf", [128, 64])
        zn = sb("zn", [128, U, D + 1])
        stats = sb("stats", [128, U, 6])
        mv = sb("mv", [128, U, 2])
        veps = sb("veps", [128, U])
        rstd = sb("rstd", [128, U])
        xnT = sb("xnT", [D, U * S])
        xs = sb("xs", [S, U, D])
        e = sb("e", [128, 2, HL * S])
        pT = sb("pT", [128, 2, HL, S])
        ph = pT[:].rearrange("p b h s -> p (b h s)")[:, 0:HL * S].bitcast(F16).rearrange("p (b h s) -> p b h s", b=2, h=HL)
        pl = pT[:].rearrange("p b h s -> p (b h s)")[:, HL * S:2 * HL * S].bitcast(F16).rearrange("p (b h s) -> p b h s", b=2, h=HL)
        mx = sb("mx", [128, 2, HL])
        rec = sb("rec", [128, 2, HL])
        ones_b = sb("ones_b", [1, 128], BF16)
        osum = sb("osum", [128, 2, HL, HD + 1])
        ps = ctx.enter_context(nc.psum_tensor("ps", [128, 8, 512], F32))

        def per(bank, n=D):
            return ps[:, bank, 0:U * n].rearrange("p (u d) -> p u d", u=U)

        def ln_vector(dve, step, r, src, dst=None, rows=128, n=U):
            dst = dst or (lambda u: zn[0:rows, u, 0:D])
            for u in range(n):
                last = nc.vector.bn_stats(stats[0:rows, u, :], src(u))
            step(last)
            for u in range(n):
                last = nc.vector.bn_aggr(mv[0:rows, u, :], stats[0:rows, u, :])
            step(last)
            nc.vector.tensor_scalar(veps[0:rows, 0:n], mv[0:rows, 0:n, 1], LN_EPS, None, ALU.add).then_inc(sem["var_ready"], 1)
            dve.wait_ge(sem["rstd_ready"], r + 1)
            for u in range(n):
                last = nc.vector.tensor_scalar(dst(u), src(u), mv[0:rows, u, 0:1], rstd[0:rows, u:u + 1],
                                               ALU.subtract, ALU.mult)
            return last

        def ln_pool(pool, r, rows=128, n=U):
            pool.wait_ge(sem["var_ready"], r + 1)
            nc.gpsimd.tensor_tensor(rstd[0:rows, 0:n], veps[0:rows, 0:n], neghalf[0:rows, 0:n],
                                    ALU.pow).then_inc(sem["rstd_ready"], 1)

        def turn_rows(pe, r, bank=0, rows=128):
            pe.wait_ge(sem["z_ready"], r + 1)
            for u in range(U):
                last = nc.tensor.transpose(ps[:, bank, u * rows:(u + 1) * rows], zn[0:rows, u, 0:D],
                                           ident[0:rows, 0:rows])
            last.then_inc(sem["zT_done"], 1)

        def slot_head(i, wide):
            return 2 * (i % 4) + i // 4 if wide else i

        def attn_tensor(pe, a, keys, wide, q_of, k_of, v_of):
            hd = D // 2 if wide else HD

            def scores(n):
                u, half = n // 2, n % 2
                if n >= 2:
                    pe.wait_ge(sem["shifted"], NU * a + n - 1)
                for slot in range(4):
                    for bank in range(2):
                        h = HL * half + slot_head(4 * bank + slot, wide)
                        last = nc.tensor.matmul(ps[:, SCORE + 2 * half + bank, slot * S:slot * S + keys],
                                                q_of(h, u), k_of(h, u), start=True, stop=True)
                last.then_inc(sem["scores_done"], 1)

            def turn(n):
                N = NU * a + n
                pe.wait_ge(sem["exp_done"], N + 1)
                if N >= 1:
                    pe.wait_ge(sem["pT_ready"], 2 * N)
                for i in range(HL):
                    last = nc.tensor.transpose(ps[0:keys, TURN + i // 4, (i % 4) * S:(i % 4 + 1) * S],
                                               e[:, n % 2, i * keys:(i + 1) * keys], ident[:, :])
                    if i % 4 == 3:
                        last.then_inc(sem["turned"], 1)

            def values(n):
                N, u, half = NU * a + n, n // 2, n % 2
                pe.wait_ge(sem["pT_ready"], 2 * N + 2)
                back = 1 if wide else 2
                if N >= back:
                    pe.wait_ge(sem["o_normed"], N + 1 - back)
                for i in range(HL):
                    hl = slot_head(i, wide)
                    last = nc.tensor.matmul(out_place(n, hl, wide), pT[0:keys, n % 2, i, :],
                                            v_of(HL * half + hl, u), start=True, stop=True)
                last.then_inc(sem["pv_done"], 1)

            scores(0)
            scores(1)
            for n in range(NU):
                turn(n)
                if n + 2 < NU:
                    scores(n + 2)
                values(n)

        def out_place(n, hl, wide):
            w = (D // 2 if wide else HD) + 1
            if wide:
                return ps[:, OUT + hl // 4, (hl % 4) * w:(hl % 4 + 1) * w]
            return ps[:, OUT + n % 2, hl * w:(hl + 1) * w]

        def attn_vector(dve, step, a, keys, wide, o_of):
            w = (D // 2 if wide else HD) + 1

            def shift(n):
                N, half = NU * a + n, n % 2
                view = ps[:, SCORE + 2 * half:SCORE + 2 * half + 2, :].rearrange(
                    "p b (s k) -> p (b s) k", s=4)[:, :, 0:keys]
                dve.wait_ge(sem["scores_done"], N + 1)
                m = mx[:, n % 2, :]
                step(nc.vector.tensor_reduce(m, view, AX.X, ALU.max))
                if N >= 2:
                    dve.wait_ge(sem["turned"], 2 * N - 2)
                nc.vector.tensor_tensor(
                    e[:, n % 2, 0:HL * keys].rearrange("p (h k) -> p h k", h=HL), view,
                    m.unsqueeze(2).broadcast_to([128, HL, keys]), ALU.subtract).then_inc(sem["shifted"], 1)

            def norm(n):
                N, u, half = NU * a + n, n // 2, n % 2
                dve.wait_ge(sem["pv_done"], N + 1)
                if wide:
                    p = ps[:, OUT:OUT + 2, 0:4 * w].rearrange("p b (h d) -> p b h d", d=w)
                    r = rec[:, n % 2, :].rearrange("p (b h) -> p b h", b=2)
                    step(nc.vector.reciprocal(r, p[:, :, :, w - 1]))
                    nc.vector.tensor_tensor(
                        o_of(u)[:, HL * half * (w - 1):HL * (half + 1) * (w - 1)].rearrange(
                            "p (b h d) -> p b h d", b=2, d=w - 1), p[:, :, :, 0:w - 1],
                        r.unsqueeze(3).broadcast_to([128, 2, 4, w - 1]), ALU.mult).then_inc(sem["o_normed"], 1)
                else:
                    p = ps[:, OUT + n % 2, 0:HL * w].rearrange("p (h d) -> p h d", d=w)
                    step(nc.vector.reciprocal(rec[:, n % 2, :], p[:, :, w - 1]))
                    nc.vector.tensor_tensor(
                        o_of(u)[:, HL * half * HD:HL * (half + 1) * HD].rearrange("p (h d) -> p h d", d=HD),
                        p[:, :, 0:HD], rec[:, n % 2, :].unsqueeze(2).broadcast_to([128, HL, HD]),
                        ALU.mult).then_inc(sem["o_normed"], 1)

            for n in range(NU):
                shift(n)
                if n >= 2:
                    norm(n - 2)
            norm(NU - 2)
            norm(NU - 1)

        def attn_scalar(act, a, keys, scale):
            def exponential(n):
                act.wait_ge(sem["shifted"], NU * a + n + 1)
                nc.scalar.activation(e[:, n % 2, 0:HL * keys], e[:, n % 2, 0:HL * keys], ACT.Exp,
                                     scale=scale).then_inc(sem["exp_done"], 1)

            exponential(0)
            for n in range(NU):
                N = NU * a + n
                if n + 1 < NU:
                    exponential(n + 1)
                if N >= 2:
                    act.wait_ge(sem["pv_done"], N - 1)
                for b in range(2):
                    act.wait_ge(sem["turned"], 2 * N + b + 1)
                    nc.scalar.activation(pT[0:keys, n % 2, 4 * b:4 * b + 4, :],
                                         ps[0:keys, TURN + b, :].rearrange("p (h s) -> p h s", h=4),
                                         ACT.Copy).then_inc(sem["pT_ready"], 1)

        HP = HD + 1

        def masked_by_vector(h):
            return h % 8 < 5

        def mask_queries(eng, a, src, qm, blocks):
            for h in range(NH):
                if eng == "vector" and masked_by_vector(h):
                    nc.vector.tensor_scalar(qm[:, h, :], src, blocks[:, h:h + 1], None, ALU.mult).then_inc(sem["masked_v"], 1)
                if eng == "scalar" and not masked_by_vector(h):
                    nc.scalar.activation(qm[:, h, :], src, ACT.Copy, scale=blocks[:, h:h + 1]).then_inc(sem["masked_a"], 1)

        def small_tensor(pe, a, keys, qm, kT, vp, low=None):
            def scores(n):
                u, half = n // 2, n % 2
                if n >= 2:
                    pe.wait_ge(sem["shifted"], NU * a + n - 1)
                if n < 2:
                    pe.wait_ge(sem["masked_v"], 10 * a + 5 * (n + 1))
                    pe.wait_ge(sem["masked_a"], 6 * a + 3 * (n + 1))
                for c in range(2):
                    bank = SCORE + 2 * half + c
                    if low is not None:
                        nc.tensor.matmul(ps[:, bank, :].rearrange("p (s k) -> p s k", s=4)[:, :, 0:keys], ones_b[0:1, :],
                                         low[0:1, u * keys:(u + 1) * keys].unsqueeze(1).broadcast_to([1, 4, keys]),
                                         start=True, stop=False, skip_group_check=True)
                    for slot in range(4):
                        h = HL * half + 4 * c + slot
                        last = nc.tensor.matmul(ps[:, bank, slot * S:slot * S + keys], qm[:, h, u * S:(u + 1) * S],
                                                kT[:, u * keys:(u + 1) * keys], start=(low is None), stop=True,
                                                skip_group_check=True)
                last.then_inc(sem["scores_done"], 1)

            def turn(n):
                N = NU * a + n
                pe.wait_ge(sem["exp_done"], N + 1)
                if N >= 1:
                    pe.wait_ge(sem["rest_ready"], 2 * N)
                for i in range(HL):
                    last = nc.tensor.transpose(ps[0:keys, TURN + i // 4, (i % 4) * S:(i % 4 + 1) * S],
                                               e[:, n % 2, i * keys:(i + 1) * keys], ident[:, :])
                    if i % 4 == 3:
                        last.then_inc(sem["turned"], 1)

            def values(n):
                N, u, half = NU * a + n, n // 2, n % 2
                if N >= 2:
                    pe.wait_ge(sem["o_normed"], N - 1)
                for i in range(HL):
                    if i % 4 == 0:
                        pe.wait_ge(sem["rest_ready"], 2 * N + i // 4 + 1)
                    at = ps[:, OUT + n % 2, i * 3 * HP:(i + 1) * 3 * HP]
                    v = vp[0:keys, u, HL * half + i, :]
                    nc.tensor.matmul(at, ph[0:keys, n % 2, i, :], v, start=True, stop=False, skip_group_check=True)
                    last = nc.tensor.matmul(at[:, 0:2 * HP], pl[0:keys, n % 2, i, :], v[:, 0:2 * HP], start=False, stop=True,
                                            skip_group_check=True)
                last.then_inc(sem["pv_done"], 1)

            scores(0)
            scores(1)
            for n in range(NU):
                turn(n)
                if n + 2 < NU:
                    scores(n + 2)
                values(n)

        def small_vector(dve, step, a, keys, o_of):
            def shift(n):
                N, half = NU * a + n, n % 2
                view = ps[:, SCORE + 2 * half:SCORE + 2 * half + 2, :].rearrange(
                    "p b (s k) -> p (b s) k", s=4)[:, :, 0:keys]
                dve.wait_ge(sem["scores_done"], N + 1)
                m = mx[:, n % 2, :]
                step(nc.vector.tensor_reduce(m, view, AX.X, ALU.max))
                if N >= 2:
                    dve.wait_ge(sem["turned"], 2 * N - 2)
                nc.vector.tensor_tensor(
                    e[:, n % 2, 0:HL * keys].rearrange("p (h k) -> p h k", h=HL), view,
                    m.unsqueeze(2).broadcast_to([128, HL, keys]), ALU.subtract).then_inc(sem["shifted"], 1)

            def rest_of(n):
                N = NU * a + n
                if N >= 2:
                    dve.wait_ge(sem["pv_done"], N - 1)
                for b in range(2):
                    dve.wait_ge(sem["pT_ready"], 2 * N + b + 1)
                    nc.vector.tensor_tensor(pl[0:keys, n % 2, 4 * b:4 * b + 4, :],
                                            ps[0:keys, TURN + b, :].rearrange("p (h s) -> p h s", h=4),
                                            ph[0:keys, n % 2, 4 * b:4 * b + 4, :], ALU.subtract).then_inc(sem["rest_ready"], 1)

            def norm(n):
                N, u, half = NU * a + n, n // 2, n % 2
                dve.wait_ge(sem["pv_done"], N + 1)
                p = ps[:, OUT + n % 2, 0:HL * 3 * HP].rearrange("p (h c d) -> p h d c", c=3, d=HP)
                step(nc.vector.tensor_reduce(osum[:, n % 2], p, AX.X, ALU.add))
                step(nc.vector.reciprocal(rec[:, n % 2, :], osum[:, n % 2, :, HD]))
                nc.vector.tensor_tensor(
                    o_of(u)[:, HL * half * HD:HL * (half + 1) * HD].rearrange("p (h d) -> p h d", d=HD),
                    osum[:, n % 2, :, 0:HD], rec[:, n % 2, :].unsqueeze(2).broadcast_to([128, HL, HD]),
                    ALU.mult).then_inc(sem["o_normed"], 1)

            for n in range(NU):
                shift(n)
                if n >= 1:
                    rest_of(n - 1)
                if n >= 2:
                    norm(n - 2)
            rest_of(NU - 1)
            norm(NU - 2)
            norm(NU - 1)

        def small_scalar(act, a, keys, scale):
            def exponential(n):
                act.wait_ge(sem["shifted"], NU * a + n + 1)
                nc.scalar.activation(e[:, n % 2, 0:HL * keys], e[:, n % 2, 0:HL * keys], ACT.Exp,
                                     scale=scale).then_inc(sem["exp_done"], 1)

            exponential(0)
            for n in range(NU):
                N = NU * a + n
                if n + 1 < NU:
                    exponential(n + 1)
                if N >= 2:
                    act.wait_ge(sem["pv_done"], N - 1)
                for b in range(2):
                    act.wait_ge(sem["turned"], 2 * N + b + 1)
                    nc.scalar.activation(ph[0:keys, n % 2, 4 * b:4 * b + 4, :],
                                         ps[0:keys, TURN + b, :].rearrange("p (h s) -> p h s", h=4),
                                         ACT.Copy).then_inc(sem["pT_ready"], 1)

        def split(step, src, part, rest_):
            step(nc.vector.tensor_copy(part(0), src))
            nc.vector.tensor_tensor(rest_, src, part(0), ALU.subtract)
            step(nc.vector.tensor_tensor(part(1), src, part(0), ALU.subtract))
            return nc.vector.tensor_tensor(part(2), rest_, part(1), ALU.subtract)

        def split_values(step, bank, vp, rows):
            return split(step, per(bank)[0:rows].rearrange("p u (h d) -> p u h d", d=HD),
                         lambda i: vp[0:rows, :, :, i * HP:i * HP + HD],
                         vrest[0:rows].rearrange("p u (h d) -> p u h d", d=HD))

        def set_ones(vp):
            nc.vector.memset(vp[:], 0.0)
            return nc.vector.memset(vp[:, :, :, HD:HP], 1.0)

        with nc.Block() as block:
            @block.sync
            def _(sp):
                sp.dma_start(ident[:], dram["ident"]).then_inc(sem["loaded"], 16)
                sp.dma_start(ctx_tm[:], dram["ctx_1024"].rearrange("b t d -> t b d")).then_inc(sem["loaded"], 16)
                sp.dma_start(x_all[:], dram["x"].rearrange("b t d -> t b d")).then_inc(sem["loaded_q"], 16)
                sp.dma_start(condT[:], dram["condT"]).then_inc(sem["loaded_q"], 16)
                sp.wait_ge(sem["loaded_q"], 32)

            @block.vector
            def _(dve):
                nc.vector.memset(ones[:], 1.0)
                nc.vector.memset(neghalf[:], -0.5)
                nc.vector.memset(ones_b[:], 1.0)
                nc.vector.memset(zn[:], 1.0)
                for b in range(B):
                    if b % U == U - 1:
                        g = b // U
                        dve.wait_ge(sem["zT_done"], g + 1)
                        nc.vector.tensor_copy(ctxT[:, g * UC:(g + 1) * UC],
                                              ps[:, g % 2, 0:UC]).then_inc(sem["xnT_ready"], 1)

            @block.tensor
            def _(pe):
                pe.wait_ge(sem["loaded"], 32)
                for g in range(NG):
                    if g >= 2:
                        pe.wait_ge(sem["xnT_ready"], g - 1)
                    for u in range(U):
                        last = nc.tensor.transpose(ps[:, g % 2, u * CL:(u + 1) * CL], ctx_tm[:, g * U + u, :],
                                                   ident[0:CL, 0:CL])
                    last.then_inc(sem["zT_done"], 1)
        rest()

        gram = sb("gram", [D, D + 1])
        def stage_slots():
            with ExitStack() as st:
                names = ["wk", "wv", "wq", "wu", "w1", "w2"]
                w = {n: sb("A_" + n, [D, D], scope=st) for n in names}
                cols = ["lnkv_g", "lnkv_b", "lnq_g", "lnq_b", "lnm_g", "lnm_b", "bk", "bv", "bq", "b1"]
                col = {n: sb("A_c_" + n, [D, 1], scope=st) for n in cols}
                wide = ["q_mu", "q_logsig", "lnp_g", "lnp_b"]
                row = {n: sb("A_r_" + n, [128, D], scope=st) for n in wide}
                bu = sb("A_bu", [1, D], scope=st)
                b2 = sb("A_b2", [1, D], scope=st)
                cond_bc = sb("A_cond", [128, B * D], scope=st)
                cT = sb("A_cT", [D, UC], scope=st)
                kT = sb("A_kT", [D, UC], scope=st)
                qT = sb("A_qT", [D, U * S], scope=st)
                v1 = sb("A_v1", [CL, U, D + 1], scope=st)
                attn = sb("A_attn", [CL, U, S], scope=st)
                am = sb("A_am", [CL, U], scope=st)
                ar = sb("A_ar", [CL, U], scope=st)
                ur = sb("A_ur", [128, U], scope=st)
                n_loads = len(names) + len(cols) + len(wide) + 3

                with nc.Block() as block:
                    @block.sync
                    def _(sp):
                        for n in names:
                            sp.dma_start(w[n][:], dram["L0_xcond_" + n]).then_inc(sem["loaded"], 16)
                        for n in cols:
                            sp.dma_start(col[n][:], dram["L0_xcond_" + n].unsqueeze(1)).then_inc(sem["loaded"], 16)
                        for n in wide:
                            src = dram["L0_xcond_" + n]
                            src = src.rearrange("a b d -> (a b d)") if n.startswith("q_") else src
                            sp.dma_start(row[n][:], src.partition_broadcast(128)).then_inc(sem["loaded"], 16)
                        sp.dma_start(bu[:], dram["L0_xcond_bu"].unsqueeze(0)).then_inc(sem["loaded"], 16)
                        sp.dma_start(b2[:], dram["L0_xcond_b2"].unsqueeze(0)).then_inc(sem["loaded"], 16)
                        sp.dma_start(cond_bc[:], dram["cond_1024"].rearrange("b d -> (b d)").partition_broadcast(128)).then_inc(sem["loaded"], 16)
                        sp.wait_ge(sem["loaded"], 16 * n_loads)

                    @block.scalar
                    def _(act):
                        act.wait_ge(sem["loaded"], 16 * n_loads)
                        nc.scalar.activation(row["q_logsig"][:], row["q_logsig"][:], ACT.Exp)

                    @block.vector
                    def _(dve):
                        nc.vector.memset(v1[:], 1.0)
                        nc.vector.memset(gram[:], 0.0)
                rest()

                def over(t):
                    return t[:].unsqueeze(1).broadcast_to([128, U, D])

                with nc.Fori(0, NG) as g:
                    with nc.Block() as block:
                        @block.vector
                        def _(dve):
                            step = Steps(dve, sem["vector_step"])
                            ln_vector(dve, step, 0, lambda u: ctx_tm[:, g * U + u, :], rows=CL).then_inc(sem["z_ready"], 1)
                            dve.wait_ge(sem["zT_done"], 1)
                            step(ln_vector(dve, step, 1, lambda u: x_all[:, g * U + u, :]))
                            step(nc.vector.tensor_tensor(xs[:], zn[:, :, 0:D], over(row["q_logsig"]), ALU.mult))
                            step(nc.vector.tensor_tensor(xs[:], xs[:], over(row["q_mu"]), ALU.add))
                            dve.wait_ge(sem["v_done"], 1)
                            nc.vector.tensor_copy(v1[:, :, 0:D], per(2)[0:CL]).then_inc(sem["v_read"], 1)
                            for it in range(3):
                                ln_vector(dve, step, 3 * it + 2, lambda u: xs[:, u, :]).then_inc(sem["z_ready"], 1)
                                dve.wait_ge(sem["scores_done"], it + 1)
                                step(nc.vector.tensor_reduce(am[:], per(2)[0:CL], AX.X, ALU.max))
                                nc.vector.tensor_tensor(attn[:], per(2)[0:CL], am[:].unsqueeze(2).broadcast_to([CL, U, S]),
                                                        ALU.subtract).then_inc(sem["shifted"], 1)
                                dve.wait_ge(sem["exp_done"], it + 1)
                                step(nc.vector.tensor_reduce(ar[:], attn[:], AX.X, ALU.add))
                                step(nc.vector.reciprocal(ar[:], ar[:]))
                                step(nc.vector.tensor_tensor(attn[:], attn[:], ar[:].unsqueeze(2).broadcast_to([CL, U, S]), ALU.mult))
                                nc.vector.tensor_scalar(attn[:], attn[:], 1e-8, None, ALU.add).then_inc(sem["upd_ready"], 1)
                                dve.wait_ge(sem["upd_done"], it + 1)
                                up = ps[:, 3:5, 0:2 * (D + 1)].rearrange("p b (u d) -> p b u d", u=2)
                                ur4 = ur[:].rearrange("p (b u) -> p b u", b=2)
                                step(nc.vector.reciprocal(ur4, up[:, :, :, D]))
                                nc.vector.tensor_tensor(zn[:, :, 0:D].rearrange("p (b u) d -> p b u d", b=2), up[:, :, :, 0:D],
                                                        ur4.unsqueeze(3).broadcast_to([128, 2, 2, D]), ALU.mult).then_inc(sem["o_normed"], 1)
                                dve.wait_ge(sem["mix_done"], it + 1)
                                step(nc.vector.tensor_tensor(xs[:], xs[:], per(5), ALU.add))
                                ln_vector(dve, step, 3 * it + 3, lambda u: xs[:, u, :]).then_inc(sem["z_ready"], 1)
                                dve.wait_ge(sem["ffn_done"], it + 1)
                                step(nc.vector.tensor_tensor(xs[:], xs[:], per(5), ALU.add))
                                step(nc.vector.tensor_tensor(xs[:].rearrange("p u d -> p (u d)"), xs[:].rearrange("p u d -> p (u d)"),
                                                             cond_bc[:, bass.ds(g * U * D, U * D)], ALU.add))
                                step(ln_vector(dve, step, 3 * it + 4, lambda u: xs[:, u, :]))
                                step(nc.vector.tensor_tensor(xs[:], zn[:, :, 0:D], over(row["lnp_g"]), ALU.mult))
                                step(nc.vector.tensor_tensor(xs[:], xs[:], over(row["lnp_b"]), ALU.add))
                            xg = x_all[:, bass.ds(g * U, U), :]
                            step(nc.vector.tensor_tensor(xg, xg, xs[:], ALU.add))
                            ln_vector(dve, step, 11, lambda u: x_all[:, g * U + u, :]).then_inc(sem["x_ready"], 1)
                            dve.wait_ge(sem["gram_done"], 1)
                            nc.vector.tensor_tensor(gram[:], gram[:], ps[:, 6, 0:D + 1], ALU.add)

                        @block.gpsimd
                        def _(pool):
                            ln_pool(pool, 0, rows=CL)
                            for r in range(1, 12):
                                ln_pool(pool, r)

                        @block.scalar
                        def _(act):
                            act.wait_ge(sem["zT_done"], 1)
                            nc.scalar.activation(cT[:], ps[:, 0, 0:UC], ACT.Identity, bias=col["lnkv_b"][:],
                                                 scale=col["lnkv_g"][:]).then_inc(sem["xnT_ready"], 1)
                            act.wait_ge(sem["k_done"], 1)
                            nc.scalar.activation(kT[:], ps[:, 1, 0:UC], ACT.Identity, bias=col["bk"][:]).then_inc(sem["k_read"], 1)
                            for it in range(3):
                                act.wait_ge(sem["zT_done"], 2 * it + 2)
                                nc.scalar.activation(xnT[:], ps[:, 0, :], ACT.Identity, bias=col["lnq_b"][:],
                                                     scale=col["lnq_g"][:]).then_inc(sem["xnT_ready"], 1)
                                act.wait_ge(sem["q_done"], it + 1)
                                nc.scalar.activation(qT[:], ps[:, 1, :], ACT.Identity, bias=col["bq"][:]).then_inc(sem["q_read"], 1)
                                act.wait_ge(sem["shifted"], it + 1)
                                nc.scalar.activation(attn[:], attn[:], ACT.Exp, scale=float(D) ** 0.5).then_inc(sem["exp_done"], 1)
                                act.wait_ge(sem["o_turned"], it + 1)
                                nc.scalar.activation(xnT[:], ps[:, 0, :], ACT.Identity, bias=col["bv"][:]).then_inc(sem["oT_ready"], 1)
                                act.wait_ge(sem["zT_done"], 2 * it + 3)
                                nc.scalar.activation(xnT[:], ps[:, 0, :], ACT.Identity, bias=col["lnm_b"][:],
                                                     scale=col["lnm_g"][:]).then_inc(sem["xnT_ready"], 1)
                                act.wait_ge(sem["hid_done"], it + 1)
                                nc.scalar.activation(qT[:], ps[:, 1, :], ACT.Gelu, bias=col["b1"][:]).then_inc(sem["hid_ready"], 1)

                        @block.tensor
                        def _(pe):
                            turn_rows(pe, 0, rows=CL)
                            pe.wait_ge(sem["xnT_ready"], 1)
                            nc.tensor.matmul(ps[:, 1, 0:UC], w["wk"][:], cT[:], start=True, stop=True).then_inc(sem["k_done"], 1)
                            for u in range(U):
                                last = nc.tensor.matmul(ps[0:CL, 2, u * D:(u + 1) * D], cT[:, u * CL:(u + 1) * CL], w["wv"][:],
                                                        start=True, stop=True)
                            last.then_inc(sem["v_done"], 1)
                            pe.wait_ge(sem["k_read"], 1)
                            pe.wait_ge(sem["v_read"], 1)
                            for it in range(3):
                                turn_rows(pe, 2 * it + 1)
                                pe.wait_ge(sem["xnT_ready"], 2 * it + 2)
                                nc.tensor.matmul(ps[:, 1, :], w["wq"][:], xnT[:], start=True, stop=True).then_inc(sem["q_done"], 1)
                                pe.wait_ge(sem["q_read"], it + 1)
                                for u in range(U):
                                    last = nc.tensor.matmul(ps[0:CL, 2, u * S:(u + 1) * S], kT[:, u * CL:(u + 1) * CL],
                                                            qT[:, u * S:(u + 1) * S], start=True, stop=True)
                                last.then_inc(sem["scores_done"], 1)
                                pe.wait_ge(sem["upd_ready"], it + 1)
                                for u in range(U):
                                    last = nc.tensor.matmul(ps[:, 3 + u // 2, (u % 2) * (D + 1):(u % 2 + 1) * (D + 1)],
                                                            attn[:, u, :], v1[:, u, :], start=True, stop=True)
                                last.then_inc(sem["upd_done"], 1)
                                pe.wait_ge(sem["o_normed"], it + 1)
                                for u in range(U):
                                    last = nc.tensor.transpose(ps[:, 0, u * S:(u + 1) * S], zn[:, u, 0:D], ident[:])
                                last.then_inc(sem["o_turned"], 1)
                                pe.wait_ge(sem["oT_ready"], it + 1)
                                for u in range(U):
                                    nc.tensor.matmul(per(5)[:, u, :], xnT[:, u * S:(u + 1) * S], w["wu"][:], start=True, stop=False)
                                    last = nc.tensor.matmul(per(5)[:, u, :], ones[0:1, :], bu[:], start=False, stop=True)
                                last.then_inc(sem["mix_done"], 1)
                                turn_rows(pe, 2 * it + 2)
                                pe.wait_ge(sem["xnT_ready"], 2 * it + 3)
                                nc.tensor.matmul(ps[:, 1, :], w["w1"][:], xnT[:], start=True, stop=True).then_inc(sem["hid_done"], 1)
                                pe.wait_ge(sem["hid_ready"], it + 1)
                                for u in range(U):
                                    nc.tensor.matmul(per(5)[:, u, :], qT[:, u * S:(u + 1) * S], w["w2"][:], start=True, stop=False)
                                    last = nc.tensor.matmul(per(5)[:, u, :], ones[0:1, :], b2[:], start=False, stop=True)
                                last.then_inc(sem["ffn_done"], 1)
                            pe.wait_ge(sem["x_ready"], 1)
                            for u in range(U):
                                last = nc.tensor.matmul(ps[:, 6, 0:D + 1], zn[:, u, 0:D], zn[:, u, :], start=(u == 0), stop=(u == U - 1))
                            last.then_inc(sem["gram_done"], 1)
                    rest()

        if "A" in SECTIONS or "C" in SECTIONS:
            stage_slots()

        def stage_product_keys():
            QH, KEYS, HALF, TOP, E = 8, 32, 16, 4, D
            QD = 2 * HALF
            NQ = QH * QD
            CELLS = 2 * QH
            PAD, TAKEN = 3e38, -3e38
            with ExitStack() as st:
                wq = sb("C_wq", [D, NQ], scope=st)
                bq = sb("C_bq", [128, NQ], scope=st)
                gamma = sb("C_gamma", [128, QD], scope=st)
                beta = sb("C_beta", [128, QD], scope=st)
                keys = sb("C_keys", [KEYS, 2, HALF], scope=st)
                ksq = sb("C_ksq", [KEYS, 2, HALF], scope=st)
                kn2 = sb("C_kn2", [KEYS, 2], scope=st)
                keys4 = sb("C_keys4", [KEYS, 4, QD], scope=st)
                kblk = sb("C_kblk", [128, 8, KEYS], scope=st)
                blocks = sb("C_blocks", [128, 8], scope=st)
                keysT = sb("C_keysT", [128, KEYS], scope=st)
                down = sb("C_down", [D, E], scope=st)
                up = sb("C_up", [E, D], scope=st)
                mean_h = sb("C_mean_h", [128, D], scope=st)
                prod = sb("C_prod", [128, NQ], scope=st)
                mean_q = sb("C_mean_q", [128, NQ], scope=st)
                var_q = sb("C_var_q", [128, NQ], scope=st)
                m_r = sb("C_m_r", [128, QD], scope=st)
                v_r = sb("C_v_r", [128, QD], scope=st)
                a_r = sb("C_a_r", [128, QD], scope=st)
                wT = sb("C_wT", [128, 2 * NQ], scope=st)
                wkey = sb("C_wkey", [D, 2 * NQ], scope=st)
                bkey = sb("C_bkey", [1, 2 * NQ], scope=st)
                sq = sb("C_sq", [128, 2, NQ], scope=st)
                n2 = sb("C_n2", [128, 2, CELLS], scope=st)
                rn = sb("C_rn", [128, 2, CELLS], scope=st)
                cand = sb("C_cand", [128, 2, CELLS, KEYS + TOP], scope=st)
                best = sb("C_best", [128, 2, CELLS, 8], scope=st)
                left = sb("C_left", [128, CELLS, KEYS + TOP], scope=st)
                ex = sb("C_ex", [128, 2, CELLS, KEYS], scope=st)
                z = sb("C_z", [128, CELLS], scope=st)
                tail = sb("C_tail", [128, 2], scope=st)
                outer = sb("C_outer", [128, 2, QH, 4, KEYS], scope=st)
                coef = sb("C_coef", [128, E], scope=st)
                act_g = sb("C_act", [128, U, E], scope=st)
                yT = sb("C_yT", [E, U * S], scope=st)

                with nc.Block() as block:
                    @block.sync
                    def _(sp):
                        pairs = [(wq[:], dram["L0_ffn_Wq"]), (bq[:], dram["L0_ffn_bq"].partition_broadcast(128)),
                                 (gamma[:], dram["L0_ffn_bn_gamma"].partition_broadcast(128)),
                                 (beta[:], dram["L0_ffn_bn_beta"].partition_broadcast(128)),
                                 (keys[:, 0, :], dram["L0_ffn_sub_key0"]), (keys[:, 1, :], dram["L0_ffn_sub_key1"]),
                                 (down[:], dram["L0_ffn_expert_down"]), (up[:], dram["L0_ffn_expert_up"]),
                                 (blocks[:], dram["block_mask"])]
                        for dst, src in pairs:
                            sp.dma_start(dst, src).then_inc(sem["loaded"], 16)

                    @block.vector
                    def _(dve):
                        step = Steps(dve, sem["vector_step"])
                        heads = lambda t: t[:].rearrange("p (h r) -> p h r", h=QH)
                        over_h = lambda t: t[:].unsqueeze(1).broadcast_to([128, QH, QD])
                        nc.vector.memset(cand[:], PAD)
                        step(nc.vector.tensor_scalar(gram[:], gram[:], 1.0 / (B * S), None, ALU.mult))
                        nc.vector.tensor_scalar(mean_h[:], ones[:], gram[:, D:D + 1], None, ALU.mult).then_inc(sem["x_ready"], 1)
                        dve.wait_ge(sem["loaded"], 16 * 9)
                        dve.wait_ge(sem["q_done"], 1)
                        step(nc.vector.tensor_copy(mean_q[:], ps[:, 1, 0:NQ]))
                        nc.vector.tensor_tensor(prod[:], ps[:, 0, 0:NQ], wq[:], ALU.mult).then_inc(sem["upd_ready"], 1)
                        dve.wait_ge(sem["upd_done"], 1)
                        step(nc.vector.tensor_tensor(var_q[:], mean_q[:], mean_q[:], ALU.mult))
                        step(nc.vector.tensor_tensor(var_q[:], ps[:, 2, 0:NQ], var_q[:], ALU.subtract))
                        step(nc.vector.tensor_tensor(mean_q[:], mean_q[:], bq[:], ALU.add))
                        step(nc.vector.tensor_reduce(m_r[:], mean_q[:].rearrange("p (h r) -> p r h", h=QH), AX.X, ALU.add))
                        step(nc.vector.tensor_scalar(m_r[:], m_r[:], 1.0 / QH, None, ALU.mult))
                        step(nc.vector.tensor_tensor(heads(prod), heads(mean_q), over_h(m_r), ALU.subtract))
                        step(nc.vector.tensor_tensor(prod[:], prod[:], prod[:], ALU.mult))
                        step(nc.vector.tensor_tensor(var_q[:], var_q[:], prod[:], ALU.add))
                        step(nc.vector.tensor_reduce(v_r[:], var_q[:].rearrange("p (h r) -> p r h", h=QH), AX.X, ALU.add))
                        step(nc.vector.tensor_scalar(v_r[:], v_r[:], 1.0 / QH, 1e-5, ALU.mult, ALU.add))
                        step(nc.vector.tensor_tensor(ksq[:], keys[:], keys[:], ALU.mult))
                        step(nc.vector.tensor_reduce(kn2[:], ksq[:], AX.X, ALU.add))
                        nc.vector.tensor_scalar(kn2[:], kn2[:], 1e-24, None, ALU.max).then_inc(sem["var_ready"], 1)
                        dve.wait_ge(sem["rstd_ready"], 2)
                        step(nc.vector.tensor_tensor(a_r[:], a_r[:], gamma[:], ALU.mult))
                        step(nc.vector.tensor_tensor(m_r[:], m_r[:], a_r[:], ALU.mult))
                        step(nc.vector.tensor_tensor(m_r[:], beta[:], m_r[:], ALU.subtract))
                        step(nc.vector.tensor_tensor(heads(wq), heads(wq), over_h(a_r), ALU.mult))
                        step(nc.vector.tensor_tensor(heads(bq), heads(bq), over_h(a_r), ALU.mult))
                        step(nc.vector.tensor_tensor(heads(bq), heads(bq), over_h(m_r), ALU.add))
                        step(nc.vector.tensor_tensor(keys[:], keys[:], kn2[:].unsqueeze(2).broadcast_to([KEYS, 2, HALF]), ALU.mult))
                        nc.vector.tensor_copy(keys4[:], keys[:].rearrange("p a r -> p (a r)").unsqueeze(1).broadcast_to([KEYS, 4, QD])).then_inc(sem["z_ready"], 1)
                        dve.wait_ge(sem["zT_done"], 1)
                        step(nc.vector.tensor_copy(keysT[:], ps[:, 3, 0:KEYS]))
                        nc.vector.tensor_copy(wT[:], ps[:, 4, :])
                        nc.vector.tensor_tensor(kblk[:], keysT[:].unsqueeze(1).broadcast_to([128, 8, KEYS]),
                                                blocks[:].unsqueeze(2).broadcast_to([128, 8, KEYS]), ALU.mult).then_inc(sem["table_ready"], 1)
                        dve.wait_ge(sem["k_done"], 1)
                        nc.vector.tensor_copy(wkey[:], ps[:, 5, :])
                        nc.vector.tensor_copy(bkey[:], ps[0:1, 6, :])

                    @block.gpsimd
                    def _(pool):
                        pool.wait_ge(sem["var_ready"], 1)
                        nc.gpsimd.tensor_tensor(a_r[:], v_r[:], neghalf[:, 0:QD], ALU.pow).then_inc(sem["rstd_ready"], 1)
                        nc.gpsimd.tensor_tensor(kn2[:], kn2[:], neghalf[0:KEYS, 0:2], ALU.pow).then_inc(sem["rstd_ready"], 1)

                    @block.tensor
                    def _(pe):
                        pe.wait_ge(sem["loaded"], 16 * 9)
                        pe.wait_ge(sem["x_ready"], 1)
                        nc.tensor.matmul(ps[:, 0, 0:NQ], gram[:, 0:D], wq[:], start=True, stop=True)
                        nc.tensor.matmul(ps[:, 1, 0:NQ], mean_h[:], wq[:], start=True, stop=True).then_inc(sem["q_done"], 1)
                        pe.wait_ge(sem["upd_ready"], 1)
                        nc.tensor.matmul(ps[:, 2, 0:NQ], ones[:], prod[:], start=True, stop=True).then_inc(sem["upd_done"], 1)
                        pe.wait_ge(sem["z_ready"], 1)
                        nc.tensor.transpose(ps[:, 3, 0:KEYS], keys4[:].rearrange("p a r -> p (a r)"), ident[0:KEYS, 0:KEYS])
                        for c in range(2):
                            nc.tensor.transpose(ps[:, 4, c * 128:(c + 1) * 128], wq[:, c * 128:(c + 1) * 128], ident[:])
                            last = nc.tensor.transpose(ps[:, 4, NQ + c * 128:NQ + (c + 1) * 128], bq[:, c * 128:(c + 1) * 128], ident[:])
                        last.then_inc(sem["zT_done"], 1)
                        pe.wait_ge(sem["table_ready"], 1)
                        kb = kblk[:].rearrange("p a k -> p (a k)")
                        for c in range(2):
                            nc.tensor.matmul(ps[:, 5, c * NQ:(c + 1) * NQ], wT[:, c * 128:(c + 1) * 128], kb, start=True, stop=True)
                            last = nc.tensor.matmul(ps[:, 6, c * NQ:(c + 1) * NQ], wT[:, NQ + c * 128:NQ + (c + 1) * 128], kb, start=True, stop=True)
                        last.then_inc(sem["k_done"], 1)
                rest()

                with nc.Fori(0, NG) as g:
                    with nc.Block() as block:
                        @block.vector
                        def _(dve):
                            step = Steps(dve, sem["vector_step"])
                            ln_vector(dve, step, 0, lambda u: x_all[:, g * U + u, :]).then_inc(sem["z_ready"], 1)

                            def select(u):
                                b = u % 2
                                dve.wait_ge(sem["q_read"], u + 1)
                                step(nc.vector.tensor_reduce(n2[:, b, :], sq[:, b, :].rearrange("p (c r) -> p c r", r=HALF), AX.X, ALU.add))
                                nc.vector.tensor_scalar(n2[:, b, :], n2[:, b, :], 1e-24, None, ALU.max).then_inc(sem["var_ready"], 1)
                                dve.wait_ge(sem["rstd_ready"], u + 2)
                                nc.vector.tensor_tensor(cand[:, b, :, 0:KEYS], ps[:, b, :].rearrange("p (c k) -> p c k", k=KEYS),
                                                        rn[:, b, :].unsqueeze(2).broadcast_to([128, CELLS, KEYS]), ALU.mult).then_inc(sem["cand_ready"], 1)
                                dve.wait_ge(sem["cand_ready"], u + 1)
                                for c in range(CELLS):
                                    last = nc.vector.max(best[:, b, c, :], cand[:, b, c, 0:KEYS])
                                step(last)
                                step(nc.vector.memset(best[:, b, :, TOP:8], PAD))
                                for c in range(CELLS):
                                    last = nc.vector.match_replace(left[:, c, :], best[:, b, c, :], cand[:, b, c, :], TAKEN)
                                step(last)
                                dve.wait_ge(sem["exp_done"], u + 1)
                                step(nc.vector.scalar_tensor_tensor(out=ex[:, b], in0=left[:, :, 0:KEYS], scalar=0.5 * TAKEN, in1=ex[:, b],
                                                                    op0=ALU.is_lt, op1=ALU.mult))
                                step(nc.vector.tensor_reduce(z[:], ex[:, b], AX.X, ALU.add))
                                step(nc.vector.reciprocal(z[:], z[:]))
                                nc.vector.tensor_tensor(ex[:, b], ex[:, b], z[:].unsqueeze(2).broadcast_to([128, CELLS, KEYS]),
                                                        ALU.mult).then_inc(sem["shifted"], 1)
                                dve.wait_ge(sem["shifted"], u + 1)
                                first = ex[:, b].rearrange("p (h a) k -> p h a k", a=2)[:, :, 0, 4:KEYS]
                                nc.vector.tensor_reduce(tail[:, b:b + 1], first, AX.XY, ALU.add)

                            def weigh(u):
                                b = u % 2
                                dve.wait_ge(sem["outer_ready"], u + 1)
                                step(nc.vector.tensor_reduce(coef[:], outer[:, b].rearrange("p h i k -> p (i k) h"), AX.X, ALU.add))
                                step(nc.vector.tensor_tensor(coef[:, E - 1:E], coef[:, E - 1:E], tail[:, b:b + 1], ALU.add))
                                if u == 0:
                                    dve.wait_ge(sem["hid_ready"], 1)
                                nc.vector.tensor_tensor(xs[:, u, :], act_g[:, u, :], coef[:], ALU.mult).then_inc(sem["expert_ready"], 1)
                                dve.wait_ge(sem["expert_ready"], u + 1)

                            for u in range(U):
                                select(u)
                                if u:
                                    weigh(u - 1)
                            weigh(U - 1)
                            dve.wait_ge(sem["mix_done"], 1)
                            xg = x_all[:, bass.ds(g * U, U), :]
                            nc.vector.tensor_tensor(xg, xg, per(6), ALU.add)

                        @block.gpsimd
                        def _(pool):
                            ln_pool(pool, 0)
                            for u in range(U):
                                b = u % 2
                                pool.wait_ge(sem["var_ready"], u + 2)
                                if u >= 2:
                                    pool.wait_ge(sem["cand_ready"], u - 1)
                                nc.gpsimd.tensor_tensor(rn[:, b, :], n2[:, b, :], neghalf[:, 0:CELLS], ALU.pow).then_inc(sem["rstd_ready"], 1)
                                pool.wait_ge(sem["shifted"], u + 1)
                                if u >= 2:
                                    pool.wait_ge(sem["expert_ready"], u - 1)
                                halves = ex[:, b].rearrange("p (h a) k -> p h a k", a=2)
                                for i in range(4):
                                    last = nc.gpsimd.tensor_tensor(outer[:, b, :, i, :], halves[:, :, 0, i:i + 1].broadcast_to([128, QH, KEYS]),
                                                                   halves[:, :, 1, :], ALU.mult)
                                last.then_inc(sem["outer_ready"], 1)

                        @block.scalar
                        def _(act):
                            act.wait_ge(sem["zT_done"], 1)
                            nc.scalar.activation(xnT[:], ps[:, 4, :], ACT.Copy).then_inc(sem["xnT_ready"], 1)
                            act.wait_ge(sem["hid_done"], 1)
                            nc.scalar.activation(act_g[:], per(7), ACT.Gelu).then_inc(sem["hid_ready"], 1)
                            for u in range(U):
                                b = u % 2
                                act.wait_ge(sem["scores_done"], u + 1)
                                nc.scalar.activation(sq[:, b, :], ps[:, 2 + b, 0:NQ], ACT.Square).then_inc(sem["q_read"], 1)
                                act.wait_ge(sem["cand_ready"], u + 1)
                                if u >= 2:
                                    act.wait_ge(sem["outer_ready"], u - 1)
                                nc.scalar.activation(ex[:, b], cand[:, b, :, 0:KEYS], ACT.Exp).then_inc(sem["exp_done"], 1)
                            act.wait_ge(sem["o_turned"], 1)
                            nc.scalar.activation(yT[:], ps[:, 5, :], ACT.Copy).then_inc(sem["oT_ready"], 1)

                        @block.tensor
                        def _(pe):
                            turn_rows(pe, 0, bank=4)
                            pe.wait_ge(sem["xnT_ready"], 1)
                            for u in range(U):
                                last = nc.tensor.matmul(per(7)[:, u, :], xnT[:, u * S:(u + 1) * S], down[:], start=True, stop=True)
                            last.then_inc(sem["hid_done"], 1)
                            for u in range(U):
                                b, z_u = u % 2, xnT[:, u * S:(u + 1) * S]
                                if u >= 2:
                                    pe.wait_ge(sem["cand_ready"], u - 1)
                                    pe.wait_ge(sem["q_read"], u - 1)
                                nc.tensor.matmul(ps[:, b, :], z_u, wkey[:], start=True, stop=False)
                                nc.tensor.matmul(ps[:, b, :], ones[0:1, :], bkey[:], start=False, stop=True)
                                nc.tensor.matmul(ps[:, 2 + b, 0:NQ], z_u, wq[:], start=True, stop=False)
                                nc.tensor.matmul(ps[:, 2 + b, 0:NQ], ones[0:1, :], bq[0:1, :], start=False, stop=True).then_inc(sem["scores_done"], 1)
                            pe.wait_ge(sem["expert_ready"], U)
                            for u in range(U):
                                last = nc.tensor.transpose(ps[:, 5, u * S:(u + 1) * S], xs[:, u, :], ident[:])
                            last.then_inc(sem["o_turned"], 1)
                            pe.wait_ge(sem["oT_ready"], 1)
                            for u in range(U):
                                last = nc.tensor.matmul(per(6)[:, u, :], yT[:, u * S:(u + 1) * S], up[:], start=True, stop=True)
                            last.then_inc(sem["mix_done"], 1)
                    rest()

        if "C" in SECTIONS:
            stage_product_keys()

        def wait_all(eng, names, value):
            for n in names:
                eng.wait_ge(sem[n], value)

        def job_bank(pe, k):
            if k >= 4:
                pe.wait_ge(sem["q_read" if k % 2 == 0 else "k_read"], (k - 4) // 2 + 1)
            return k % 4

        def jobs_read(pe, n):
            pe.wait_ge(sem["q_read"], n // 2)
            pe.wait_ge(sem["k_read"], n // 2)

        def copy_job(eng, k, dst, src):
            eng.wait_ge(sem["proj_done"], k + 1)
            if k % 2 == 0:
                nc.scalar.activation(dst, src, ACT.Copy).then_inc(sem["q_read"], 1)
            else:
                nc.vector.tensor_copy(dst, src).then_inc(sem["k_read"], 1)

        def stage_block():
            W, INNER, NB = D // 2, NH * D // 2, NH // 2
            with ExitStack() as st:
                wa = {}
                for a in (1, 2):
                    for n in ("wq", "wk", "wv"):
                        wa[a, n] = sb(f"D_{n}{a}", [D, INNER], scope=st)
                    wa[a, "wo"] = sb(f"D_wo{a}", [D, NB, D], scope=st)
                    wa[a, "bo"] = sb(f"D_bo{a}", [1, D], scope=st)
                w1 = sb("D_w1", [D, 2 * FFN], scope=st)
                b1 = sb("D_b1", [D, 8], scope=st)
                w2 = sb("D_w2", [D, 4, D], scope=st)
                b2 = sb("D_b2", [1, D], scope=st)
                nw = sb("D_nw", [D, 3, 2 * D], scope=st)
                nb = sb("D_nb", [D, 3, 2], scope=st)
                gb = sb("D_gb", [D, 3, 2, B], scope=st)
                gb4 = sb("D_gb4", [D, 3, 2, U], scope=st)
                qT = sb("D_qT", [D, NB, U * S], scope=st)
                kT = sb("D_kT", [D, NB, U * S], scope=st)
                vv = sb("D_vv", [S, U, NH, W + 1], scope=st)
                o_all = sb("D_o", [S, U, INNER], scope=st)
                loads = [(w1[:], dram["L1_xcond_ff_w1"]),
                         (b1[:], dram["L1_xcond_ff_b1"].rearrange("(c p) -> p c", p=D)),
                         (w2[:], dram["L1_xcond_ff_w2"].rearrange("(c p) n -> p c n", p=D)),
                         (b2[:], dram["L1_xcond_ff_b2"].unsqueeze(0))]
                for a in (1, 2):
                    for n in ("wq", "wk", "wv"):
                        loads.append((wa[a, n][:], dram[f"L1_xcond_attn{a}_{n}"]))
                    loads.append((wa[a, "wo"][:], dram[f"L1_xcond_attn{a}_wo"].rearrange("(c p) n -> p c n", p=D)))
                    loads.append((wa[a, "bo"][:], dram[f"L1_xcond_attn{a}_bo"].unsqueeze(0)))
                for n in range(3):
                    loads.append((nw[:, n, :], dram[f"L1_xcond_norm{n + 1}_w"]))
                    loads.append((nb[:, n, :], dram[f"L1_xcond_norm{n + 1}_b"].rearrange("(c p) -> p c", p=D)))

                with nc.Block() as block:
                    @block.sync
                    def _(sp):
                        for dst, src in loads:
                            sp.dma_start(dst, src, allow_slow_non_contiguous=True).then_inc(sem["loaded"], 16)

                    @block.tensor
                    def _(pe):
                        pe.wait_ge(sem["loaded"], 16 * len(loads))
                        for n in range(3):
                            for c in range(2):
                                last = nc.tensor.matmul(ps[:, 0, (2 * n + c) * B:(2 * n + c + 1) * B], nw[:, n, c * D:(c + 1) * D],
                                                        condT[:], start=True, stop=True)
                        last.then_inc(sem["proj_done"], 1)

                    @block.vector
                    def _(dve):
                        step = Steps(dve, sem["vector_step"])
                        nc.vector.memset(vv[:], 1.0)
                        dve.wait_ge(sem["loaded"], 16 * len(loads))
                        step(nc.vector.tensor_scalar(nb[:, :, 0], nb[:, :, 0], 1.0, None, ALU.add))
                        dve.wait_ge(sem["proj_done"], 1)
                        nc.vector.tensor_tensor(gb[:].rearrange("p n c b -> p (n c) b"),
                                                ps[:, 0, 0:6 * B].rearrange("p (n b) -> p n b", b=B),
                                                nb[:].rearrange("p n c -> p (n c)").unsqueeze(2).broadcast_to([D, 6, B]), ALU.add)
                rest()

                ctxg = sb("D_ctxg", [D, UC], scope=st)
                with nc.Fori(0, NG) as g:
                    with nc.Block() as block:
                        @block.tensor
                        def _(pe):
                            for a in (1, 2):
                                k0 = 32 * (a - 1)
                                keys = S if a == 1 else CL
                                src = xnT if a == 1 else ctxg
                                turn_rows(pe, a - 1, bank=TURN)
                                pe.wait_ge(sem["xnT_ready"], a)
                                for c in range(NB):
                                    bank = job_bank(pe, k0 + c)
                                    nc.tensor.matmul(ps[:, bank, :], wa[a, "wq"][:, c * D:(c + 1) * D], xnT[:],
                                                     start=True, stop=True).then_inc(sem["proj_done"], 1)
                                for c in range(NB):
                                    bank = job_bank(pe, k0 + NB + c)
                                    nc.tensor.matmul(ps[:, bank, 0:U * keys], wa[a, "wk"][:, c * D:(c + 1) * D], src[:, 0:U * keys],
                                                     start=True, stop=True).then_inc(sem["proj_done"], 1)
                                for c in range(2 * U):
                                    bank = job_bank(pe, k0 + 2 * NB + c)
                                    nc.tensor.matmul(ps[0:keys, bank, :], src[:, (c // 2) * keys:(c // 2 + 1) * keys],
                                                     wa[a, "wv"][:, (c % 2) * 512:(c % 2 + 1) * 512],
                                                     start=True, stop=True).then_inc(sem["proj_done"], 1)
                                jobs_read(pe, k0 + 24)
                                attn_tensor(pe, a - 1, keys, True,
                                            lambda h, u: qT[W * (h % 2):W * (h % 2 + 1), h // 2, u * S:(u + 1) * S],
                                            lambda h, u: kT[W * (h % 2):W * (h % 2 + 1), h // 2, u * keys:(u + 1) * keys],
                                            lambda h, u: vv[0:keys, u, h, :])
                                pe.wait_ge(sem["o_normed"], NU * a)
                                for c in range(2 * U):
                                    bank = job_bank(pe, k0 + 24 + c)
                                    for i in range(4):
                                        last = nc.tensor.transpose(ps[:, bank, i * S:(i + 1) * S],
                                                                   o_all[:, c // 2, ((c % 2) * 4 + i) * D:((c % 2) * 4 + i + 1) * D], ident[:])
                                    last.then_inc(sem["proj_done"], 1)
                                jobs_read(pe, k0 + 32)
                                for u in range(U):
                                    for c in range(NB):
                                        nc.tensor.matmul(per(OUT)[:, u, :], qT[:, c, u * S:(u + 1) * S], wa[a, "wo"][:, c, :],
                                                         start=(c == 0), stop=False)
                                    last = nc.tensor.matmul(per(OUT)[:, u, :], ones[0:1, :], wa[a, "bo"][:], start=False, stop=True)
                                last.then_inc(sem["mix_done"], 1)
                            turn_rows(pe, 2, bank=TURN)
                            pe.wait_ge(sem["xnT_ready"], 3)
                            for j in range(4):
                                for c, k in ((4 + j, 64 + 2 * j), (j, 65 + 2 * j)):
                                    bank = job_bank(pe, k)
                                    nc.tensor.matmul(ps[:, bank, :], w1[:, c * D:(c + 1) * D], xnT[:],
                                                     start=True, stop=True).then_inc(sem["proj_done"], 1)
                            jobs_read(pe, 72)
                            for u in range(U):
                                for c in range(4):
                                    nc.tensor.matmul(per(OUT)[:, u, :], kT[:, 4 + c, u * S:(u + 1) * S], w2[:, c, :],
                                                     start=(c == 0), stop=False)
                                last = nc.tensor.matmul(per(OUT)[:, u, :], ones[0:1, :], b2[:], start=False, stop=True)
                            last.then_inc(sem["mix_done"], 1)

                        def empty(eng, k0, a, odd):
                            keys = S if a == 1 else CL
                            for c in range(odd, NB, 2):
                                copy_job(eng, k0 + c, qT[:, c, :], ps[:, (k0 + c) % 4, :])
                            for c in range(odd, NB, 2):
                                copy_job(eng, k0 + NB + c, kT[:, c, 0:U * keys], ps[:, (k0 + NB + c) % 4, 0:U * keys])
                            for c in range(odd, 2 * U, 2):
                                copy_job(eng, k0 + 2 * NB + c, vv[0:keys, c // 2, (c % 2) * 8:(c % 2 + 1) * 8, 0:W],
                                         ps[0:keys, (k0 + 2 * NB + c) % 4, :].rearrange("p (h d) -> p h d", d=W))

                        def empty_turned(eng, k0, odd):
                            for c in range(odd, 2 * U, 2):
                                u, half = c // 2, c % 2
                                copy_job(eng, k0 + 24 + c, qT[:, 4 * half:4 * half + 4, u * S:(u + 1) * S],
                                         ps[:, (k0 + 24 + c) % 4, :].rearrange("p (c t) -> p c t", c=4))

                        @block.scalar
                        def _(act):
                            for a in (1, 2, 3):
                                act.wait_ge(sem["zT_done"], a)
                                if a == 1:
                                    act.wait_ge(sem["table_ready"], 1)
                                for u in range(U):
                                    last = nc.scalar.activation(xnT[:, u * S:(u + 1) * S], ps[:, TURN, u * S:(u + 1) * S], ACT.Identity,
                                                                bias=gb4[:, a - 1, 1, u:u + 1], scale=gb4[:, a - 1, 0, u:u + 1])
                                last.then_inc(sem["xnT_ready"], 1)
                                if a < 3:
                                    k0 = 32 * (a - 1)
                                    empty(act, k0, a, 0)
                                    attn_scalar(act, a - 1, S if a == 1 else CL, W ** -0.5)
                                    empty_turned(act, k0, 0)
                            for j in range(4):
                                act.wait_ge(sem["proj_done"], 64 + 2 * j + 1)
                                nc.scalar.activation(kT[:, j, :], ps[:, (64 + 2 * j) % 4, :], ACT.Gelu, bias=b1[:, 4 + j:5 + j]).then_inc(sem["q_read"], 1)

                        @block.vector
                        def _(dve):
                            step = Steps(dve, sem["vector_step"])
                            nc.vector.tensor_copy(ctxg[:], ctxT[:, bass.ds(g * UC, UC)])
                            nc.vector.tensor_copy(gb4[:].rearrange("p n c u -> p (n c) u"),
                                                  gb[:].rearrange("p n c b -> p (n c) b")[:, :, bass.ds(g * U, U)]).then_inc(sem["table_ready"], 1)
                            step(ln_vector(dve, step, 0, lambda u: x_all[:, g * U + u, :], lambda u: xs[:, u, :]))
                            for a in (1, 2):
                                k0 = 32 * (a - 1)
                                ln_vector(dve, step, a, lambda u: xs[:, u, :]).then_inc(sem["z_ready"], 1)
                                empty(dve, k0, a, 1)
                                attn_vector(dve, step, a - 1, S if a == 1 else CL, True, lambda u: o_all[:, u, :])
                                empty_turned(dve, k0, 1)
                                dve.wait_ge(sem["mix_done"], a)
                                step(nc.vector.tensor_tensor(xs[:], xs[:], per(OUT), ALU.add))
                            ln_vector(dve, step, 3, lambda u: xs[:, u, :]).then_inc(sem["z_ready"], 1)
                            for j in range(4):
                                dve.wait_ge(sem["q_read"], 32 + j + 1)
                                dve.wait_ge(sem["proj_done"], 65 + 2 * j + 1)
                                nc.vector.scalar_tensor_tensor(out=kT[:, 4 + j, :], in0=ps[:, (65 + 2 * j) % 4, :], scalar=b1[:, j:j + 1],
                                                               in1=kT[:, j, :], op0=ALU.add, op1=ALU.mult).then_inc(sem["k_read"], 1)
                            dve.wait_ge(sem["mix_done"], 3)
                            step(nc.vector.tensor_tensor(xs[:], xs[:], per(OUT), ALU.add))
                            xg = x_all[:, bass.ds(g * U, U), :]
                            nc.vector.tensor_tensor(xg, xg, xs[:], ALU.add)

                        @block.gpsimd
                        def _(pool):
                            for r in range(4):
                                ln_pool(pool, r)
                    rest()

        if "D" in SECTIONS:
            stage_block()

        vrest = sb("vrest", [S, U, D])
        PAD, TAKEN = 3e38, -3e38
        gates = sb("gates", [128, U, EXPERTS + 6])
        gbest = sb("gbest", [128, U, 8])
        gleft = sb("gleft", [128, U, EXPERTS + 6])
        gsum = sb("gsum", [128, U])
        chosen = sb("chosen", [128, U, EXPERTS])

        def route_vector(dve, step, bank, weighted):
            g8 = gates[:, :, 0:EXPERTS]
            over = lambda t: t[:].unsqueeze(2).broadcast_to([128, U, EXPERTS])
            dve.wait_ge(sem["gate_done"], 1)
            step(nc.vector.tensor_reduce(gsum[:], per(bank, EXPERTS), AX.X, ALU.max))
            nc.vector.tensor_tensor(g8, per(bank, EXPERTS), over(gsum), ALU.subtract).then_inc(sem["cand_ready"], 1)
            dve.wait_ge(sem["gate_ready"], 1)
            step(nc.vector.tensor_reduce(gsum[:], g8, AX.X, ALU.add))
            step(nc.vector.reciprocal(gsum[:], gsum[:]))
            step(nc.vector.tensor_tensor(g8, g8, over(gsum), ALU.mult))
            for u in range(U):
                last = nc.vector.max(gbest[:, u, :], gates[:, u, 0:EXPERTS])
            step(last)
            step(nc.vector.memset(gbest[:, :, 2:8], PAD))
            for u in range(U):
                last = nc.vector.match_replace(gleft[:, u, :], gbest[:, u, :], gates[:, u, :], TAKEN)
            step(last)
            if weighted:
                step(nc.vector.scalar_tensor_tensor(out=chosen[:], in0=gleft[:, :, 0:EXPERTS], scalar=0.5 * TAKEN, in1=g8,
                                                    op0=ALU.is_lt, op1=ALU.mult))
            else:
                step(nc.vector.tensor_scalar(chosen[:], gleft[:, :, 0:EXPERTS], 0.5 * TAKEN, None, ALU.is_lt))

        def route_scalar(act):
            act.wait_ge(sem["cand_ready"], 1)
            nc.scalar.activation(gates[:, :, 0:EXPERTS], gates[:, :, 0:EXPERTS], ACT.Exp).then_inc(sem["gate_ready"], 1)

        def stage_attn_experts():
            with ExitStack() as st:
                wqkv = sb("E_wqkv", [D, 3 * D], scope=st)
                bqk = sb("E_bqk", [D, 2], scope=st)
                bv = sb("E_bv", [1, D], scope=st)
                wg = sb("E_wg", [D, EXPERTS], scope=st)
                bg = sb("E_bg", [1, EXPERTS], scope=st)
                we = sb("E_we", [D, EXPERTS * D], scope=st)
                be = sb("E_be", [1, EXPERTS * D], scope=st)
                qr = sb("E_qr", [D, U * S], scope=st)
                kr = sb("E_kr", [D, U * S], scope=st)
                qm = sb("E_qm", [D, NH, U * S], scope=st)
                heads = sb("E_heads", [D, NH], scope=st)
                vp = sb("E_vp", [S, U, NH, 3 * HP], BF16, scope=st)
                o8 = sb("E_o8", [S, U, D], scope=st)
                moe = sb("E_moe", [S, U, D], scope=st)
                loads = [(heads[:], dram["head_mask"]), (wqkv[:], dram["L1_ffn_W_qkv"]),
                         (bqk[:], dram["L1_ffn_b_qkv"][0:2 * D].rearrange("(c p) -> p c", p=D)),
                         (bv[:], dram["L1_ffn_b_qkv"][2 * D:3 * D].unsqueeze(0)),
                         (wg[:], dram["L1_ffn_W_gate"]), (bg[:], dram["L1_ffn_b_gate"].unsqueeze(0)),
                         (we[:].rearrange("d (e f) -> d e f", f=D), dram["L1_ffn_W_experts"].rearrange("e d f -> d e f")),
                         (be[:], dram["L1_ffn_b_experts"].rearrange("e f -> (e f)").unsqueeze(0))]
                with nc.Block() as block:
                    @block.sync
                    def _(sp):
                        for dst, src in loads:
                            sp.dma_start(dst, src, allow_slow_non_contiguous=True).then_inc(sem["loaded"], 16)
                        sp.wait_ge(sem["loaded"], 16 * len(loads))

                    @block.vector
                    def _(dve):
                        Steps(dve, sem["vector_step"])(nc.vector.memset(vp[:], 0.0))
                        nc.vector.memset(vp[:, :, :, HD:HP], 1.0)
                        nc.vector.memset(gates[:], PAD)
                rest()

                with nc.Fori(0, NG) as g:
                    with nc.Block() as block:
                        @block.tensor
                        def _(pe):
                            turn_rows(pe, 0, bank=TURN)
                            pe.wait_ge(sem["xnT_ready"], 1)
                            for c in range(2):
                                nc.tensor.matmul(ps[:, TURN + 1 + c, :], wqkv[:, c * D:(c + 1) * D], xnT[:],
                                                 start=True, stop=True).then_inc(sem["q_done"], 1)
                            for u in range(U):
                                nc.tensor.matmul(per(7)[:, u, :], xnT[:, u * S:(u + 1) * S], wqkv[:, 2 * D:3 * D], start=True, stop=False)
                                last = nc.tensor.matmul(per(7)[:, u, :], ones[0:1, :], bv[:], start=False, stop=True)
                            last.then_inc(sem["v_done"], 1)
                            for u in range(U):
                                nc.tensor.matmul(per(TURN, EXPERTS)[:, u, :], xnT[:, u * S:(u + 1) * S], wg[:], start=True, stop=False)
                                last = nc.tensor.matmul(per(TURN, EXPERTS)[:, u, :], ones[0:1, :], bg[:], start=False, stop=True)
                            last.then_inc(sem["gate_done"], 1)
                            for u in range(U):
                                if u >= 2:
                                    pe.wait_ge(sem["expert_ready"], u - 1)
                                for c in range(2):
                                    bank = 2 * (u % 2) + c
                                    nc.tensor.matmul(ps[:, bank, :], xnT[:, u * S:(u + 1) * S], we[:, c * 512:(c + 1) * 512], start=True, stop=False)
                                    last = nc.tensor.matmul(ps[:, bank, :], ones[0:1, :], be[:, c * 512:(c + 1) * 512], start=False, stop=True)
                                last.then_inc(sem["expert_done"], 1)
                            pe.wait_ge(sem["expert_ready"], U)
                            pe.wait_ge(sem["v_read"], 1)
                            pe.wait_ge(sem["q_read"], 2)
                            small_tensor(pe, 0, S, qm, kr, vp)

                        @block.scalar
                        def _(act):
                            act.wait_ge(sem["zT_done"], 1)
                            nc.scalar.activation(xnT[:], ps[:, TURN, :], ACT.Copy).then_inc(sem["xnT_ready"], 1)
                            for c, t in enumerate((qr, kr)):
                                act.wait_ge(sem["q_done"], c + 1)
                                nc.scalar.activation(t[:], ps[:, TURN + 1 + c, :], ACT.Identity, bias=bqk[:, c:c + 1]).then_inc(sem["q_read"], 1)
                            act.wait_ge(sem["q_read"], 1)
                            mask_queries("scalar", 0, qr[:], qm, heads)
                            route_scalar(act)
                            small_scalar(act, 0, S, HD ** -0.5)

                        @block.vector
                        def _(dve):
                            step = Steps(dve, sem["vector_step"])
                            ln_vector(dve, step, 0, lambda u: x_all[:, g * U + u, :]).then_inc(sem["z_ready"], 1)
                            dve.wait_ge(sem["q_read"], 1)
                            mask_queries("vector", 0, qr[:], qm, heads)
                            dve.wait_ge(sem["v_done"], 1)
                            split_values(step, 7, vp, S).then_inc(sem["v_read"], 1)
                            route_vector(dve, step, TURN, True)
                            for u in range(U):
                                dve.wait_ge(sem["expert_done"], u + 1)
                                prod = e[:, u % 2, :].rearrange("p (e f) -> p e f", f=D)
                                nc.vector.tensor_tensor(prod, ps[:, 2 * (u % 2):2 * (u % 2) + 2, :].rearrange("p b (e f) -> p (b e) f", f=D),
                                                        chosen[:, u, :].unsqueeze(2).broadcast_to([128, EXPERTS, D]), ALU.mult).then_inc(sem["expert_ready"], 1)
                                dve.wait_ge(sem["expert_ready"], u + 1)
                                last = nc.vector.tensor_reduce(moe[:, u, :], prod.rearrange("p e f -> p f e"), AX.X, ALU.add)
                            step(last)
                            small_vector(dve, step, 0, S, lambda u: o8[:, u, :])
                            dve.wait_ge(sem["o_normed"], NU)
                            step(nc.vector.tensor_tensor(o8[:], o8[:], moe[:], ALU.add))
                            xg = x_all[:, bass.ds(g * U, U), :]
                            nc.vector.tensor_tensor(xg, xg, o8[:], ALU.add)

                        @block.gpsimd
                        def _(pool):
                            ln_pool(pool, 0)
                    rest()

        if "E" in SECTIONS:
            stage_attn_experts()

        def stage_gru():
            CH, CB = 2, B // 2
            RUN = 16
            with ExitStack() as st:
                wT = sb("F_wT", [D, D], scope=st)
                gate_w = {n: sb("F_" + n, [D, 3 * D], scope=st) for n in ("x", "c", "h")}
                gate_p = {n: sb("F_p" + n, [D, 3, 3 * D], BF16, scope=st) for n in ("x", "c", "h")}
                bias = sb("F_bias", [D, 3], scope=st)
                encW = sb("F_encW", [D, 3, B, 128], BF16, scope=st)
                ctxp = sb("F_ctxp", [CL, 3, B, D], BF16, scope=st)
                decT = sb("F_decT", [D, 3, S, B], BF16, scope=st)
                spare = sb("F_spare", [128, 2, U * D], scope=st)
                gru = sb("F_gru", [D, S, B], scope=st)
                xloc = sb("F_xloc", [D, 3, RUN, B], BF16, scope=st)
                hp = sb("F_hp", [D, B, 3], BF16, scope=st)
                hist = sb("F_hist", [D, RUN + 1, B], scope=st)
                sT = sb("F_sT", [CL, CH, CB], scope=st)
                nm = sb("F_nm", [CB, CH], scope=st)
                den = sb("F_den", [D, CH, CB], scope=st)
                keep = sb("F_keep", [D, CH, CB], scope=st)
                ones16 = sb("F_ones16", [128, 128], F16, scope=st)
                ex = sb("F_ex", [CB, CH, CL], scope=st)
                eT = sb("F_eT", [CL, CH, CB, 2], F16, scope=st)
                cv = sb("F_cv", [D, CH, CB], scope=st)
                cvp = sb("F_cvp", [D, CH, CB, 3], BF16, scope=st)
                left = sb("F_left", [D, CH, CB], scope=st)
                zt = sb("F_zt", [D, CH, CB], scope=st)
                rt = sb("F_rt", [D, CH, CB], scope=st)
                cand = sb("F_cand", [D, CH, CB], scope=st)
                t1 = sb("F_t1", [D, CH, CB], scope=st)
                loads = [(wT[:], dram["L2_xcond_W"]), (gate_w["x"][:], dram["L2_xcond_kernel"][0:D, :]),
                         (gate_w["c"][:], dram["L2_xcond_kernel"][D:2 * D, :]), (gate_w["h"][:], dram["L2_xcond_recurrent_kernel"]),
                         (bias[:], dram["L2_xcond_bias"].rearrange("(c p) -> p c", p=D))]
                SCALE = 1024.0
                PRODUCTS = [(0, 0), (0, 1), (0, 2), (1, 0), (1, 1), (2, 0)]

                def parts(step, made, src, part, rest_):
                    step(nc.vector.tensor_tensor(part(0), made[0], made[1], made[2]))
                    nc.vector.tensor_tensor(rest_, src, part(0), ALU.subtract)
                    step(nc.vector.tensor_tensor(part(1), src, part(0), ALU.subtract))
                    return nc.vector.tensor_tensor(part(2), rest_, part(1), ALU.subtract)

                with nc.Block() as block:
                    @block.sync
                    def _(sp):
                        for dst, src in loads:
                            sp.dma_start(dst, src, allow_slow_non_contiguous=True).then_inc(sem["loaded"], 16)

                    @block.vector
                    def _(dve):
                        step = Steps(dve, sem["vector_step"])
                        nc.vector.tensor_copy(hist[:, RUN, :], condT[:])
                        nc.vector.memset(encW[:], 0.0)
                        nc.vector.memset(ones16[:], 1.0)
                        step(split(step, condT[:], lambda i: hp[:, :, i], spare[:, 0, 0:B]))
                        dve.wait_ge(sem["loaded"], 16 * len(loads))
                        nc.vector.tensor_scalar(bias[:, 0:2], bias[:, 0:2], 0.5, None, ALU.mult)
                        for n in ("x", "c", "h"):
                            step(split(step, gate_w[n][:], lambda i: gate_p[n][:, i, :], spare[:, 0, 0:3 * D]))
                        for g in range(NG):
                            mine = slice(g * U, (g + 1) * U)
                            step(split(step, ctx_tm[:, mine, :], lambda i: ctxp[:, i, mine, :],
                                       spare[0:CL, 0, :].rearrange("p (u d) -> p u d", u=U)))
                            dve.wait_ge(sem["k_done"], g + 1)
                            step(split(step, per(g, CL), lambda i: encW[:, i, mine, 0:CL],
                                       spare[:, 0, 0:UC].rearrange("p (u k) -> p u k", u=U)))

                    @block.tensor
                    def _(pe):
                        pe.wait_ge(sem["loaded"], 16 * len(loads))
                        for g in range(NG):
                            nc.tensor.matmul(ps[:, g, 0:UC], wT[:], ctxT[:, g * UC:(g + 1) * UC], start=True, stop=True).then_inc(sem["k_done"], 1)
                rest()

                with nc.Fori(0, NG) as g:
                    with nc.Block() as block:
                        @block.vector
                        def _(dve):
                            step = Steps(dve, sem["vector_step"])
                            ln_vector(dve, step, 0, lambda u: x_all[:, g * U + u, :]).then_inc(sem["z_ready"], 1)
                            dve.wait_ge(sem["zT_done"], 1)
                            tok = per(0, S).rearrange("p u t -> p t u")
                            split(step, tok, lambda i: decT[:, i, :, bass.ds(g * U, U)],
                                  spare[:, 0, :].rearrange("p (t u) -> p t u", u=U))

                        @block.gpsimd
                        def _(pool):
                            ln_pool(pool, 0)

                        @block.tensor
                        def _(pe):
                            turn_rows(pe, 0)
                    rest()

                with nc.Fori(0, S // RUN) as n:
                    with nc.Block() as block:
                        mine = lambda c: slice(CB * c, CB * (c + 1))

                        @block.tensor
                        def _(pe):
                            def score(t, c):
                                k = CH * t + c
                                if t == 0:
                                    pe.wait_ge(sem["x_ready"], 1)
                                else:
                                    pe.wait_ge(sem["mix_added"], k - 1)
                                for j in range(CB):
                                    b = CB * c + j
                                    for i in range(3):
                                        last = nc.tensor.matmul(ps[:, 4 * c, 3 * j:3 * j + 3 - i], encW[:, i, b, :], hp[:, b, 0:3 - i],
                                                                start=(i == 0), stop=(i == 2), skip_group_check=True)
                                last.then_inc(sem["scores_done"], 1)

                            def early(t, c):
                                gate = lambda i: ps[:, 4 * c + 3, i * CB:(i + 1) * CB]
                                for i in range(3):
                                    for a, b in PRODUCTS:
                                        nc.tensor.matmul(gate(i), gate_p["x"][:, a, i * D:(i + 1) * D], xloc[:, b, t, mine(c)],
                                                         start=(i == 0 and a + b == 0), stop=False, skip_group_check=True)
                                for i in range(3):
                                    for a, b in PRODUCTS:
                                        nc.tensor.matmul(gate(i if i < 2 else 3), gate_p["h"][:, a, i * D:(i + 1) * D], hp[:, mine(c), b],
                                                         start=False, stop=(i == 2 and a == 2), skip_group_check=True)

                            def turn_scores(t, c):
                                pe.wait_ge(sem["k_read"], CH * t + c + 1)
                                nc.tensor.transpose(ps[0:CB, 4 * c + 1, 0:CL], sT[:, c, :], ident[0:CL, 0:CL]).then_inc(sem["turned"], 1)

                            def turn_weights(t, c):
                                pe.wait_ge(sem["exp_done"], CH * t + c + 1)
                                nc.tensor.transpose(ps[0:CL, 4 * c + 1, 128:128 + CB], ex[:, c, :], ident[0:CB, 0:CB]).then_inc(sem["o_turned"], 1)

                            def attend(t, c):
                                pe.wait_ge(sem["pT_ready"], CH * t + c + 1)
                                nc.tensor.matmul(ps[:, 4 * c + 2, 128:128 + 2 * CB], ones16[0:CL, :], eT[:, c].rearrange("p j i -> p (j i)"),
                                                 start=True, stop=True, skip_group_check=True)
                                for j in range(CB):
                                    for i in range(3):
                                        m = 2 if i < 2 else 1
                                        last = nc.tensor.matmul(ps[:, 4 * c + 2, 2 * j:2 * j + m], ctxp[:, i, CB * c + j, :], eT[:, c, j, 0:m],
                                                                start=(i == 0), stop=(i == 2), skip_group_check=True)
                                last.then_inc(sem["pv_done"], 1)

                            def late(t, c):
                                pe.wait_ge(sem["o_normed"], CH * t + c + 1)
                                for i in range(3):
                                    for a, b in PRODUCTS:
                                        last = nc.tensor.matmul(ps[:, 4 * c + 3, i * CB:(i + 1) * CB], gate_p["c"][:, a, i * D:(i + 1) * D], cvp[:, c, :, b],
                                                                start=False, stop=(a == 2), skip_group_check=True)
                                last.then_inc(sem["gate_done"], 1)

                            for t in range(RUN):
                                for part in (score, turn_scores, early, turn_weights, attend, late):
                                    for c in range(CH):
                                        part(t, c)

                        @block.vector
                        def _(dve):
                            step = Steps(dve, sem["vector_step"])
                            nc.vector.tensor_copy(xloc[:], decT[:, :, bass.ds(n * RUN, RUN), :])
                            nc.vector.tensor_copy(hist[:, 0, :], hist[:, RUN, :]).then_inc(sem["x_ready"], 1)
                            dve.wait_ge(sem["x_ready"], 1)

                            def scores(t, c):
                                dve.wait_ge(sem["scores_done"], CH * t + c + 1)
                                nc.vector.tensor_reduce(sT[:, c, :], ps[0:CL, 4 * c, 0:3 * CB].rearrange("p (j i) -> p j i", i=3), AX.X, ALU.add).then_inc(sem["k_read"], 1)

                            def maximum(t, c):
                                dve.wait_ge(sem["turned"], CH * t + c + 1)
                                nc.vector.tensor_reduce(nm[:, c:c + 1], ps[0:CB, 4 * c + 1, 0:CL], AX.X, ALU.max, negate=True).then_inc(sem["cand_ready"], 1)

                            def turned(t, c):
                                dve.wait_ge(sem["o_turned"], CH * t + c + 1)
                                src = ps[0:CL, 4 * c + 1, 128:128 + CB]
                                step(nc.vector.tensor_scalar(eT[:, c, :, 0], src, SCALE, None, ALU.mult))
                                nc.vector.scalar_tensor_tensor(out=eT[:, c, :, 1], in0=src, scalar=SCALE, in1=eT[:, c, :, 0],
                                                               op0=ALU.mult, op1=ALU.subtract).then_inc(sem["pT_ready"], 1)

                            def attended(t, c):
                                dve.wait_ge(sem["pv_done"], CH * t + c + 1)
                                nc.vector.tensor_reduce(den[:, c, :], ps[:, 4 * c + 2, 128:128 + 2 * CB].rearrange("p (j i) -> p j i", i=2), AX.X, ALU.add)
                                step(nc.vector.tensor_reduce(t1[:, c, :], ps[:, 4 * c + 2, 0:2 * CB].rearrange("p (j i) -> p j i", i=2), AX.X, ALU.add))
                                step(nc.vector.reciprocal(den[:, c, :], den[:, c, :]))
                                nc.vector.tensor_tensor(cv[:, c, :], t1[:, c, :], den[:, c, :], ALU.mult)
                                parts(step, (t1[:, c, :], den[:, c, :], ALU.mult), cv[:, c, :], lambda i: cvp[:, c, :, i],
                                      left[:, c, :]).then_inc(sem["o_normed"], 1)

                            def candidate(t, c):
                                dve.wait_ge(sem["gate_ready"], 2 * (CH * t + c) + 1)
                                gate = lambda i: ps[:, 4 * c + 3, i * CB:(i + 1) * CB]
                                dve.wait_ge(sem["gate_ready"], 2 * (CH * t + c) + 2)
                                step(nc.vector.scalar_tensor_tensor(out=t1[:, c, :], in0=rt[:, c, :], scalar=1.0, in1=gate(3), op0=ALU.add, op1=ALU.mult))
                                nc.vector.scalar_tensor_tensor(out=t1[:, c, :], in0=t1[:, c, :], scalar=0.5, in1=gate(2), op0=ALU.mult, op1=ALU.add).then_inc(sem["hid_done"], 1)

                            def blend(t, c):
                                nc.vector.tensor_scalar(keep[:, c, :], zt[:, c, :], 0.5, 0.5, ALU.mult, ALU.add)
                                step(nc.vector.tensor_scalar(zt[:, c, :], zt[:, c, :], -0.5, 0.5, ALU.mult, ALU.add))
                                step(nc.vector.tensor_tensor(keep[:, c, :], keep[:, c, :], hist[:, t, mine(c)], ALU.mult))

                            def state(t, c):
                                dve.wait_ge(sem["hid_ready"], CH * t + c + 1)
                                step(nc.vector.tensor_tensor(t1[:, c, :], zt[:, c, :], cand[:, c, :], ALU.mult))
                                new = hist[:, t + 1, mine(c)]
                                nc.vector.tensor_tensor(new, t1[:, c, :], keep[:, c, :], ALU.add)
                                parts(step, (t1[:, c, :], keep[:, c, :], ALU.add), new, lambda i: hp[:, mine(c), i],
                                      left[:, c, :]).then_inc(sem["mix_added"], 1)

                            for t in range(RUN):
                                for part in (scores, maximum, turned, attended, candidate, blend, state):
                                    for c in range(CH):
                                        part(t, c)
                            dve.wait_ge(sem["mix_added"], CH * RUN)
                            nc.vector.tensor_copy(gru[:, bass.ds(n * RUN, RUN), :], hist[:, 1:RUN + 1, :])

                        @block.scalar
                        def _(act):
                            def exponentials(t, c):
                                act.wait_ge(sem["cand_ready"], CH * t + c + 1)
                                nc.scalar.activation(ex[:, c, :], ps[0:CB, 4 * c + 1, 0:CL], ACT.Exp, bias=nm[:, c:c + 1]).then_inc(sem["exp_done"], 1)

                            def gates(t, c):
                                act.wait_ge(sem["gate_done"], CH * t + c + 1)
                                for i, dst in ((1, rt), (0, zt)):
                                    nc.scalar.activation(dst[:, c, :], ps[:, 4 * c + 3, i * CB:(i + 1) * CB], ACT.Tanh, bias=bias[:, i:i + 1],
                                                         scale=0.5).then_inc(sem["gate_ready"], 1)

                            def candidates(t, c):
                                act.wait_ge(sem["hid_done"], CH * t + c + 1)
                                nc.scalar.activation(cand[:, c, :], t1[:, c, :], ACT.Tanh, bias=bias[:, 2:3]).then_inc(sem["hid_ready"], 1)

                            for t in range(RUN):
                                for part in (exponentials, gates, candidates):
                                    for c in range(CH):
                                        part(t, c)
                    rest()

                with nc.Block() as block:
                    @block.tensor
                    def _(pe):
                        for i in range(NG):
                            for u in range(U):
                                last = nc.tensor.transpose(ps[:, i, u * D:(u + 1) * D], gru[:, :, i * U + u], ident[:])
                            last.then_inc(sem["turned"], 1)

                    @block.vector
                    def _(dve):
                        for i in range(NG):
                            dve.wait_ge(sem["turned"], i + 1)
                            nc.vector.tensor_tensor(x_all[:, i * U:(i + 1) * U, :], x_all[:, i * U:(i + 1) * U, :], per(i), ALU.add)
                rest()

        if "F" in SECTIONS:
            stage_gru()

        def stage_moe():
            with ExitStack() as st:
                wg = sb("G_wg", [D, EXPERTS], scope=st)
                bg = sb("G_bg", [1, EXPERTS], scope=st)
                w1 = sb("G_w1", [D, EXPERTS, FFN], scope=st)
                b1 = sb("G_b1", [D, EXPERTS, 4], scope=st)
                w2 = sb("G_w2", [D, EXPERTS, 4, D], scope=st)
                b2 = sb("G_b2", [1, EXPERTS, D], scope=st)
                hid = sb("G_hid", [D, 2, 4, U * S], scope=st)
                loads = [(wg[:], dram["L2_ffn_gate_w"]), (bg[:], dram["L2_ffn_gate_b"].unsqueeze(0)),
                         (b2[:], dram["L2_ffn_b2"].unsqueeze(0))]
                for x in range(EXPERTS):
                    loads.append((w1[:, x, :], dram["L2_ffn_w1"][x]))
                    loads.append((b1[:, x, :], dram["L2_ffn_b1"][x].rearrange("(c p) -> p c", p=D)))
                    loads.append((w2[:, x], dram["L2_ffn_w2"][x].rearrange("(c p) n -> p c n", p=D)))
                with nc.Block() as block:
                    @block.sync
                    def _(sp):
                        for dst, src in loads:
                            sp.dma_start(dst, src, allow_slow_non_contiguous=True).then_inc(sem["loaded"], 16)
                        sp.wait_ge(sem["loaded"], 16 * len(loads))

                    @block.vector
                    def _(dve):
                        nc.vector.memset(gates[:], PAD)
                rest()

                with nc.Fori(0, NG) as g:
                    with nc.Block() as block:
                        @block.tensor
                        def _(pe):
                            turn_rows(pe, 0, bank=TURN)
                            pe.wait_ge(sem["xnT_ready"], 1)
                            for u in range(U):
                                nc.tensor.matmul(per(TURN, EXPERTS)[:, u, :], xnT[:, u * S:(u + 1) * S], wg[:], start=True, stop=False)
                                last = nc.tensor.matmul(per(TURN, EXPERTS)[:, u, :], ones[0:1, :], bg[:], start=False, stop=True)
                            last.then_inc(sem["gate_done"], 1)

                            def hidden(x):
                                for c in range(4):
                                    bank = job_bank(pe, 4 * x + c)
                                    nc.tensor.matmul(ps[:, bank, :], w1[:, x, c * D:(c + 1) * D], xnT[:], start=True, stop=True).then_inc(sem["proj_done"], 1)

                            hidden(0)
                            for x in range(EXPERTS):
                                if x + 1 < EXPERTS:
                                    hidden(x + 1)
                                jobs_read(pe, 4 * x + 4)
                                if x >= 2:
                                    pe.wait_ge(sem["mix_added"], x - 1)
                                for u in range(U):
                                    for c in range(4):
                                        nc.tensor.matmul(per(OUT + x % 2)[:, u, :], hid[:, x % 2, c, u * S:(u + 1) * S], w2[:, x, c, :],
                                                         start=(c == 0), stop=False)
                                    last = nc.tensor.matmul(per(OUT + x % 2)[:, u, :], ones[0:1, :], b2[:, x, :], start=False, stop=True)
                                last.then_inc(sem["mix_done"], 1)

                        def relu_job(eng, k):
                            x, c = k // 4, k % 4
                            eng.wait_ge(sem["proj_done"], k + 1)
                            if x >= 2 and c < 2:
                                eng.wait_ge(sem["mix_done"], x - 1)
                            dst, src = hid[:, x % 2, c, :], ps[:, c, :]
                            if k % 2 == 0:
                                nc.scalar.activation(dst, src, ACT.Relu, bias=b1[:, x, c:c + 1]).then_inc(sem["q_read"], 1)
                            else:
                                nc.vector.tensor_scalar(dst, src, b1[:, x, c:c + 1], 0.0, ALU.add, ALU.max).then_inc(sem["k_read"], 1)

                        @block.scalar
                        def _(act):
                            act.wait_ge(sem["zT_done"], 1)
                            nc.scalar.activation(xnT[:], ps[:, TURN, :], ACT.Copy).then_inc(sem["xnT_ready"], 1)
                            route_scalar(act)
                            for k in range(0, 4 * EXPERTS, 2):
                                relu_job(act, k)

                        @block.vector
                        def _(dve):
                            step = Steps(dve, sem["vector_step"])
                            ln_vector(dve, step, 0, lambda u: x_all[:, g * U + u, :]).then_inc(sem["z_ready"], 1)
                            step(nc.vector.tensor_copy(xs[:], x_all[:, bass.ds(g * U, U), :]))
                            route_vector(dve, step, TURN, False)
                            relu_job(dve, 1)
                            relu_job(dve, 3)
                            for x in range(EXPERTS):
                                if x + 1 < EXPERTS:
                                    relu_job(dve, 4 * x + 5)
                                    relu_job(dve, 4 * x + 7)
                                dve.wait_ge(sem["mix_done"], x + 1)
                                for u in range(U):
                                    last = nc.vector.scalar_tensor_tensor(out=xs[:, u, :], in0=per(OUT + x % 2)[:, u, :], scalar=chosen[:, u, x:x + 1],
                                                                          in1=xs[:, u, :], op0=ALU.mult, op1=ALU.add)
                                last.then_inc(sem["mix_added"], 1)
                                dve.wait_ge(sem["mix_added"], x + 1)
                            nc.vector.tensor_copy(x_all[:, bass.ds(g * U, U), :], xs[:])

                        @block.gpsimd
                        def _(pool):
                            ln_pool(pool, 0)
                    rest()

        if "G" in SECTIONS:
            stage_moe()

        def stage_layers():
            NPAIR = 4
            with ExitStack() as st:
                y_all = sb("H_y", [S, B, D], scope=st)
                square = ["q_w", "qs_w", "k_w", "ks_w", "v_w", "cqs_w", "cks_w"]
                w = {n: sb("H_" + n, [D, D], scope=st) for n in square}
                plain = ["so_w", "cq_w", "ck_w", "cv_w", "co_w"]
                w.update({n: sb("H_" + n, [D, D], scope=st) for n in plain})
                f1 = sb("H_f1", [D, FFN], scope=st)
                f1b = sb("H_f1b", [D, 4], scope=st)
                f2 = sb("H_f2", [D, 4, D], scope=st)
                f2b = sb("H_f2b", [1, D], scope=st)
                nw = sb("H_nw", [D, 3, 2 * D], scope=st)
                nb = sb("H_nb", [D, 3, 2], scope=st)
                gb = sb("H_gb", [D, 3, 2, B], scope=st)
                gb4 = sb("H_gb4", [D, 3, 2, U], scope=st)
                cosT = sb("H_cos", [D, S], scope=st)
                sinT = sb("H_sin", [D, S], scope=st)
                ctxg = sb("H_ctxg", [D, UC], scope=st)
                ta = sb("H_ta", [D, 2, U * S], scope=st)
                tb = sb("H_tb", [D, 2, U * S], scope=st)
                qr = sb("H_qr", [D, U * S], scope=st)
                kr = sb("H_kr", [D, U * S], scope=st)
                cr = sb("H_cr", [D, UC], scope=st)
                qm = sb("H_qm", [D, NH, U * S], scope=st)
                heads = sb("H_heads", [D, NH], scope=st)
                vp = sb("H_vp", [S, U, NH, 3 * HP], BF16, scope=st)
                cvp = sb("H_cvp", [CL, U, NH, 3 * HP], BF16, scope=st)
                o8 = sb("H_o8", [S, U, D], scope=st)
                hid = sb("H_hid", [D, 4, U * S], scope=st)
                mask_s = sb("H_mask_s", [1, B * S // 4], mybir.dt.uint32, scope=st)
                mask_c = sb("H_mask_c", [1, B * CL // 4], mybir.dt.uint32, scope=st)
                low_s = sb("H_low_s", [1, B * S], BF16, scope=st)
                low_c = sb("H_low_c", [1, B * CL], BF16, scope=st)
                low4 = sb("H_low4", [1, U * S], BF16, scope=st)
                low4c = sb("H_low4c", [1, UC], BF16, scope=st)

                with nc.Block() as block:
                    @block.sync
                    def _(sp):
                        sp.dma_start(cosT[:], dram["cosT"]).then_inc(sem["loaded"], 16)
                        sp.dma_start(sinT[:], dram["sinT"]).then_inc(sem["loaded"], 16)
                        sp.dma_start(heads[:], dram["head_mask"]).then_inc(sem["loaded"], 16)
                        sp.dma_start(mask_s[:], dram["mask_BxS_bf0"].unsqueeze(0)).then_inc(sem["loaded"], 16)
                        sp.dma_start(mask_c[:], dram["mask_BxS2_bf0"].unsqueeze(0)).then_inc(sem["loaded"], 16)

                    @block.vector
                    def _(dve):
                        step = Steps(dve, sem["vector_step"])
                        for t in (vp, cvp):
                            step(nc.vector.memset(t[:], 0.0))
                            nc.vector.memset(t[:, :, :, HD:HP], 1.0)
                        dve.wait_ge(sem["loaded"], 80)
                        nc.vector.tensor_scalar(low_s[:], mask_s[:].bitcast(U8), MASKED, None, ALU.mult)
                        nc.vector.tensor_scalar(low_c[:], mask_c[:].bitcast(U8), MASKED, None, ALU.mult)
                rest()

                with nc.Fori(0, NG) as g:
                    with nc.Block() as block:
                        @block.vector
                        def _(dve):
                            step = Steps(dve, sem["vector_step"])
                            ln_vector(dve, step, 0, lambda u: x_all[:, g * U + u, :], lambda u: y_all[:, g * U + u, :])

                        @block.gpsimd
                        def _(pool):
                            ln_pool(pool, 0)
                    rest()

                def layer_loads(l):
                    one = lambda name, pat, **kw: dram[name][bass.ds(l, 1)].rearrange(pat, **kw)
                    out = [(w[n][:], one("L3_" + n, "a p n -> p (a n)")) for n in square]
                    out += [(w[n][:], one("L3_xcond_" + n, "a p n -> p (a n)")) for n in plain]
                    out += [(f1[:], one("L3_xcond_f1_w", "a p n -> p (a n)")),
                            (f1b[:], one("L3_xcond_f1_b", "a (c p) -> p (a c)", p=D)),
                            (f2[:], one("L3_xcond_f2_w", "a (c p) n -> p (a c) n", p=D)),
                            (f2b[:], one("L3_xcond_f2_b", "a n -> a n"))]
                    for i in range(3):
                        out.append((nw[:, i, :], one(f"L3_xcond_n{i + 1}_w", "a p n -> p (a n)")))
                        out.append((nb[:, i, :], one(f"L3_xcond_n{i + 1}_b", "a (c p) -> p (a c)", p=D)))
                    return out

                with nc.Fori(0, LAYERS) as l:
                    with nc.Block() as block:
                        n_loads = 22

                        @block.sync
                        def _(sp):
                            loads = layer_loads(l)
                            assert len(loads) == n_loads
                            for dst, src in loads:
                                sp.dma_start(dst, src, allow_slow_non_contiguous=True).then_inc(sem["loaded"], 16)

                        @block.tensor
                        def _(pe):
                            pe.wait_ge(sem["loaded"], 16 * n_loads)
                            for n in range(3):
                                for c in range(2):
                                    last = nc.tensor.matmul(ps[:, 0, (2 * n + c) * B:(2 * n + c + 1) * B], nw[:, n, c * D:(c + 1) * D],
                                                            condT[:], start=True, stop=True)
                            last.then_inc(sem["proj_done"], 1)

                        @block.vector
                        def _(dve):
                            step = Steps(dve, sem["vector_step"])
                            dve.wait_ge(sem["loaded"], 16 * n_loads)
                            step(nc.vector.tensor_scalar(nb[:, :, 0], nb[:, :, 0], 1.0, None, ALU.add))
                            dve.wait_ge(sem["proj_done"], 1)
                            nc.vector.tensor_tensor(gb[:].rearrange("p n c b -> p (n c) b"),
                                                    ps[:, 0, 0:6 * B].rearrange("p (n b) -> p n b", b=B),
                                                    nb[:].rearrange("p n c -> p (n c)").unsqueeze(2).broadcast_to([D, 6, B]), ALU.add)
                    rest()

                    with nc.Fori(0, NG) as g:
                        with nc.Block() as block:
                            pair_cols = (UC, U * S, U * S, U * S)
                            pair_to = (cr, qr, kr, qr)
                            pair_banks = ((4, 5), (0, 1), (2, 3), (0, 1))

                            @block.tensor
                            def _(pe):
                                def pair(p, a, b, src, cols):
                                    for bank, m in zip(pair_banks[p], (a, b)):
                                        last = nc.tensor.matmul(ps[:, bank, 0:cols], w[m][:], src[:, 0:cols], start=True, stop=True)
                                    last.then_inc(sem["q_done"], 1)

                                def outputs(a, m):
                                    pe.wait_ge(sem["o_normed"], NU * a)
                                    for u in range(U):
                                        last = nc.tensor.transpose(ps[:, TURN, u * S:(u + 1) * S], o8[:, u, :], ident[:])
                                    last.then_inc(sem["o_turned"], 1)
                                    pe.wait_ge(sem["oT_ready"], a)
                                    for u in range(U):
                                        last = nc.tensor.matmul(per(OUT)[:, u, :], xnT[:, u * S:(u + 1) * S], w[m][:], start=True, stop=True)
                                    last.then_inc(sem["mix_done"], 1)

                                pe.wait_ge(sem["x_ready"], 1)
                                pair(0, "ck_w", "cks_w", ctxg, UC)
                                for u in range(U):
                                    last = nc.tensor.matmul(per(7)[0:CL, u, :], ctxg[:, u * CL:(u + 1) * CL], w["cv_w"][:], start=True, stop=True)
                                last.then_inc(sem["v_done"], 1)
                                turn_rows(pe, 0, bank=6)
                                pe.wait_ge(sem["xnT_ready"], 1)
                                pair(1, "q_w", "qs_w", xnT, U * S)
                                pair(2, "k_w", "ks_w", xnT, U * S)
                                pe.wait_ge(sem["v_read"], 1)
                                for u in range(U):
                                    last = nc.tensor.matmul(per(7)[:, u, :], xnT[:, u * S:(u + 1) * S], w["v_w"][:], start=True, stop=True)
                                last.then_inc(sem["v_done"], 1)
                                pe.wait_ge(sem["v_read"], 2)
                                pe.wait_ge(sem["rope_done"], 3)
                                pe.wait_ge(sem["table_ready"], 3)
                                small_tensor(pe, 0, S, qm, kr, vp, low4)
                                outputs(1, "so_w")
                                turn_rows(pe, 1, bank=TURN)
                                pe.wait_ge(sem["xnT_ready"], 2)
                                pair(3, "cq_w", "cqs_w", xnT, U * S)
                                pe.wait_ge(sem["rope_done"], 4)
                                small_tensor(pe, 1, CL, qm, cr, cvp, low4c)
                                outputs(2, "co_w")
                                turn_rows(pe, 2, bank=TURN)
                                pe.wait_ge(sem["xnT_ready"], 3)
                                for c in range(4):
                                    nc.tensor.matmul(ps[:, c, :], f1[:, c * D:(c + 1) * D], xnT[:], start=True, stop=True).then_inc(sem["hid_done"], 1)
                                pe.wait_ge(sem["hid_ready"], 4)
                                for u in range(U):
                                    for c in range(4):
                                        nc.tensor.matmul(per(OUT)[:, u, :], hid[:, c, u * S:(u + 1) * S], f2[:, c, :], start=(c == 0), stop=False)
                                    last = nc.tensor.matmul(per(OUT)[:, u, :], ones[0:1, :], f2b[:], start=False, stop=True)
                                last.then_inc(sem["mix_done"], 1)

                            @block.scalar
                            def _(act):
                                def affine(a, bank):
                                    act.wait_ge(sem["zT_done"], a + 1)
                                    for u in range(U):
                                        last = nc.scalar.activation(xnT[:, u * S:(u + 1) * S], ps[:, bank, u * S:(u + 1) * S], ACT.Identity,
                                                                    bias=gb4[:, a, 1, u:u + 1], scale=gb4[:, a, 0, u:u + 1])
                                    last.then_inc(sem["xnT_ready"], 1)

                                def outputs(a):
                                    act.wait_ge(sem["o_turned"], a)
                                    nc.scalar.activation(xnT[:], ps[:, TURN, :], ACT.Copy).then_inc(sem["oT_ready"], 1)

                                act.wait_ge(sem["x_ready"], 2)
                                affine(0, 6)
                                act.wait_ge(sem["table_ready"], 2)
                                mask_queries("scalar", 0, qr[:], qm, heads)
                                small_scalar(act, 0, S, HD ** -0.5)
                                outputs(1)
                                affine(1, TURN)
                                act.wait_ge(sem["table_ready"], 4)
                                mask_queries("scalar", 1, qr[:], qm, heads)
                                small_scalar(act, 1, CL, HD ** -0.5)
                                outputs(2)
                                affine(2, TURN)
                                for c in range(4):
                                    act.wait_ge(sem["hid_done"], c + 1)
                                    nc.scalar.activation(hid[:, c, :], ps[:, c, :], ACT.Gelu, bias=f1b[:, c:c + 1]).then_inc(sem["hid_ready"], 1)

                            @block.vector
                            def _(dve):
                                step = Steps(dve, sem["vector_step"])

                                def rotate(p):
                                    n = CL if p == 0 else S
                                    dve.wait_ge(sem["q_done"], p + 1)
                                    if p >= 2:
                                        dve.wait_ge(sem["table_ready"], p - 1)
                                    for bank, table, t in zip(pair_banks[p], (cosT, sinT), (ta, tb)):
                                        last = nc.vector.tensor_tensor(t[:, p % 2, 0:U * n].rearrange("p (u t) -> p u t", u=U), per(bank, n),
                                                                       table[:, 0:n].unsqueeze(1).broadcast_to([D, U, n]), ALU.mult)
                                    last.then_inc(sem["rope_done"], 1)

                                nc.vector.tensor_copy(low4[:], low_s[:, bass.ds(g * U * S, U * S)])
                                nc.vector.tensor_copy(low4c[:], low_c[:, bass.ds(g * UC, UC)])
                                nc.vector.tensor_copy(ctxg[:], ctxT[:, bass.ds(g * UC, UC)]).then_inc(sem["x_ready"], 1)
                                nc.vector.tensor_copy(gb4[:].rearrange("p n c u -> p (n c) u"),
                                                      gb[:].rearrange("p n c b -> p (n c) b")[:, :, bass.ds(g * U, U)]).then_inc(sem["x_ready"], 1)
                                step(nc.vector.tensor_copy(xs[:], y_all[:, bass.ds(g * U, U), :]))
                                ln_vector(dve, step, 0, lambda u: xs[:, u, :]).then_inc(sem["z_ready"], 1)
                                for p in range(3):
                                    rotate(p)
                                    if p == 0:
                                        dve.wait_ge(sem["v_done"], 1)
                                        split_values(step, 7, cvp, CL).then_inc(sem["v_read"], 1)
                                dve.wait_ge(sem["table_ready"], 2)
                                mask_queries("vector", 0, qr[:], qm, heads)
                                dve.wait_ge(sem["v_done"], 2)
                                split_values(step, 7, vp, S).then_inc(sem["v_read"], 1)
                                small_vector(dve, step, 0, S, lambda u: o8[:, u, :])
                                dve.wait_ge(sem["mix_done"], 1)
                                step(nc.vector.tensor_tensor(xs[:], xs[:], per(OUT), ALU.add))
                                ln_vector(dve, step, 1, lambda u: xs[:, u, :]).then_inc(sem["z_ready"], 1)
                                rotate(3)
                                dve.wait_ge(sem["table_ready"], 4)
                                mask_queries("vector", 1, qr[:], qm, heads)
                                small_vector(dve, step, 1, CL, lambda u: o8[:, u, :])
                                dve.wait_ge(sem["mix_done"], 2)
                                step(nc.vector.tensor_tensor(xs[:], xs[:], per(OUT), ALU.add))
                                ln_vector(dve, step, 2, lambda u: xs[:, u, :]).then_inc(sem["z_ready"], 1)
                                dve.wait_ge(sem["mix_done"], 3)
                                nc.vector.tensor_tensor(y_all[:, bass.ds(g * U, U), :], xs[:], per(OUT), ALU.add)

                            @block.gpsimd
                            def _(pool):
                                def add_pair(p):
                                    pool.wait_ge(sem["rope_done"], p + 1)
                                    at = (slice(None), p % 2, slice(0, pair_cols[p]))
                                    nc.gpsimd.tensor_tensor(pair_to[p][:], ta[at], tb[at], ALU.add).then_inc(sem["table_ready"], 1)

                                ln_pool(pool, 0)
                                for p in range(3):
                                    add_pair(p)
                                ln_pool(pool, 1)
                                add_pair(3)
                                ln_pool(pool, 2)
                        rest()

                with nc.Block() as block:
                    @block.vector
                    def _(dve):
                        nc.vector.tensor_tensor(x_all[:], x_all[:], y_all[:], ALU.add)
                rest()

        if "H" in SECTIONS:
            stage_layers()

        def stage_ternary():
            with ExitStack() as st:
                wfc = sb("I_wfc", [D, FFN], scope=st)
                wpj = sb("I_wpj", [D, FFN], scope=st)
                neg = sb("I_neg", [D, FFN], scope=st)
                lnw = sb("I_lnw", [D, 4], scope=st)
                lnb = sb("I_lnb", [D, 4], scope=st)
                mag = sb("I_mag", [D, 2], scope=st)
                thr = sb("I_thr", [D, 2], scope=st)
                nthr = sb("I_nthr", [D, 2], scope=st)
                hid = sb("I_hid", [S, U, FFN], scope=st)
                hidT = sb("I_hidT", [D, 4, U * S], scope=st)
                loads = [(wfc[:], dram["L3_ffn_W_fc"]),
                         (wpj[:].rearrange("p (c n) -> p c n", c=4), dram["L3_ffn_W_proj"].rearrange("(c p) n -> p c n", p=D)),
                         (lnw[:], dram["L3_ffn_ln_w"].rearrange("(c p) -> p c", p=D)),
                         (lnb[:], dram["L3_ffn_ln_b"].rearrange("(c p) -> p c", p=D))]
                with nc.Block() as block:
                    @block.sync
                    def _(sp):
                        for dst, src in loads:
                            sp.dma_start(dst, src, allow_slow_non_contiguous=True).then_inc(sem["loaded"], 16)

                    @block.vector
                    def _(dve):
                        step = Steps(dve, sem["vector_step"])
                        dve.wait_ge(sem["loaded"], 16 * len(loads))
                        nc.vector.tensor_reduce(mag[:, 0:1], wfc[:], AX.X, ALU.add, apply_absolute_value=True)
                        nc.vector.tensor_reduce(mag[:, 1:2], wpj[:], AX.X, ALU.add, apply_absolute_value=True).then_inc(sem["z_ready"], 1)
                        dve.wait_ge(sem["zT_done"], 1)
                        step(nc.vector.tensor_scalar(thr[:], ps[:, 0, 0:2], 1.0 / (D * FFN), 1e-6, ALU.mult, ALU.add))
                        step(nc.vector.tensor_scalar(thr[:], thr[:], 0.5, None, ALU.mult))
                        step(nc.vector.tensor_scalar(nthr[:], thr[:], -1.0, None, ALU.mult))
                        for i, w in enumerate((wfc, wpj)):
                            step(nc.vector.tensor_scalar(neg[:], w[:], nthr[:, i:i + 1], None, ALU.is_lt))
                            step(nc.vector.scalar_tensor_tensor(out=w[:], in0=w[:], scalar=thr[:, i:i + 1], in1=neg[:],
                                                                op0=ALU.is_gt, op1=ALU.subtract))

                    @block.tensor
                    def _(pe):
                        pe.wait_ge(sem["z_ready"], 1)
                        nc.tensor.matmul(ps[:, 0, 0:2], ones[:], mag[:], start=True, stop=True).then_inc(sem["zT_done"], 1)
                rest()

                with nc.Fori(0, NG) as g:
                    with nc.Block() as block:
                        @block.tensor
                        def _(pe):
                            turn_rows(pe, 0, bank=TURN)
                            pe.wait_ge(sem["xnT_ready"], 1)
                            for u in range(U):
                                nc.tensor.matmul(ps[:, u, :], xnT[:, u * S:(u + 1) * S], wfc[:], start=True, stop=True).then_inc(sem["hid_done"], 1)
                            pe.wait_ge(sem["z_ready"], 2)
                            for c in range(4):
                                for u in range(U):
                                    last = nc.tensor.transpose(ps[:, c, u * S:(u + 1) * S], hid[:, u, c * D:(c + 1) * D], ident[:])
                                last.then_inc(sem["turned"], 1)
                            pe.wait_ge(sem["pT_ready"], 4)
                            for u in range(U):
                                for c in range(4):
                                    last = nc.tensor.matmul(per(OUT)[:, u, :], hidT[:, c, u * S:(u + 1) * S], wpj[:, c * D:(c + 1) * D],
                                                            start=(c == 0), stop=(c == 3))
                            last.then_inc(sem["mix_done"], 1)

                        @block.scalar
                        def _(act):
                            act.wait_ge(sem["zT_done"], 1)
                            nc.scalar.activation(xnT[:], ps[:, TURN, :], ACT.Copy).then_inc(sem["xnT_ready"], 1)
                            for u in range(U):
                                act.wait_ge(sem["hid_done"], u + 1)
                                last = nc.scalar.activation(hid[:, u, :], ps[:, u, :], ACT.Gelu).then_inc(sem["hid_ready"], 1)
                            for c in range(4):
                                act.wait_ge(sem["turned"], c + 1)
                                nc.scalar.activation(hidT[:, c, :], ps[:, c, :], ACT.Identity, bias=lnb[:, c:c + 1],
                                                     scale=lnw[:, c:c + 1]).then_inc(sem["pT_ready"], 1)

                        @block.vector
                        def _(dve):
                            step = Steps(dve, sem["vector_step"])
                            ln_vector(dve, step, 0, lambda u: x_all[:, g * U + u, :]).then_inc(sem["z_ready"], 1)
                            dve.wait_ge(sem["hid_ready"], U)
                            ln_vector(dve, step, 1, lambda u: hid[:, u, :], lambda u: hid[:, u, :]).then_inc(sem["z_ready"], 1)
                            dve.wait_ge(sem["mix_done"], 1)
                            xg = x_all[:, bass.ds(g * U, U), :]
                            nc.vector.tensor_tensor(xg, xg, per(OUT), ALU.add)

                        @block.gpsimd
                        def _(pool):
                            ln_pool(pool, 0)
                            ln_pool(pool, 1)
                    rest()

        if "I" in SECTIONS:
            stage_ternary()

        with nc.Block() as block:
            @block.sync
            def _(sp):
                sp.dma_start(out.rearrange("b t d -> t b d"), x_all[:]).then_inc(sem["stored"], 16)
                sp.wait_ge(sem["stored"], 16)


_TRANSPOSED = ["L0_ffn_expert_down", "L2_xcond_W", "L3_ffn_W_fc", "L3_ffn_W_proj"]


def kernel(**inputs):
    import concourse.bacc as _bacc
    from concourse.bass_utils import run_bass_kernel_spmd as _run

    f32 = np.float32
    arrays = {}
    for name, a in inputs.items():
        a = np.asarray(a)
        if a.dtype == np.bool_:
            a = np.ascontiguousarray(a).reshape(-1).view(np.uint32)
        arrays[name] = a
    for name in _TRANSPOSED:
        arrays[name] = arrays[name].T
    arrays["condT"] = arrays["cond_1024"].T
    for name in ("n1_w", "n2_w", "n3_w", "qkv_w", "so_w", "cq_w", "ck_w", "cv_w", "co_w", "f1_w", "f2_w"):
        arrays["L3_xcond_" + name] = arrays["L3_xcond_" + name].transpose(0, 2, 1)
    swap = np.arange(D).reshape(NH, 2, HD // 2)[:, ::-1, :].reshape(-1)
    qkv = arrays["L3_xcond_qkv_w"]
    arrays["L3_q_w"], arrays["L3_k_w"], arrays["L3_v_w"] = qkv[:, :, 0:D], qkv[:, :, D:2 * D], qkv[:, :, 2 * D:]
    arrays["L3_qs_w"] = arrays["L3_q_w"][:, :, swap]
    arrays["L3_ks_w"] = arrays["L3_k_w"][:, :, swap]
    arrays["L3_cqs_w"] = arrays["L3_xcond_cq_w"][:, :, swap]
    arrays["L3_cks_w"] = arrays["L3_xcond_ck_w"][:, :, swap]
    arrays["ident"] = np.eye(128, dtype=f32)
    half = HD // 2
    inv = (1.0 / 10000.0 ** (np.arange(half, dtype=f32) / f32(half))).astype(f32)
    ang = np.arange(S, dtype=f32)[:, None] * inv
    cos = np.cos(ang).astype(f32).T
    sin = np.sin(ang).astype(f32).T
    arrays["cosT"] = np.tile(np.concatenate([cos, cos]), (NH, 1))
    arrays["sinT"] = np.tile(np.concatenate([-sin, sin]), (NH, 1))
    rows = np.arange(D) // 16
    arrays["head_mask"] = np.repeat(np.eye(NH, dtype=f32), HD, axis=0)
    arrays["block_mask"] = (rows[:, None] == np.arange(8)[None, :]).astype(f32)

    nc = _bacc.Bacc("TRN2", target_bir_lowering=False, num_devices=1)
    dram, given = {}, {}
    for name, a in arrays.items():
        a = np.ascontiguousarray(a)
        given["in_" + name] = a
        dram[name] = nc.dram_tensor("in_" + name, a.shape, mybir.dt.from_np(a.dtype), kind="ExternalInput").ap()
    out = nc.dram_tensor("out_x", (B, S, D), F32, kind="ExternalOutput").ap()
    build(nc, dram, out)
    r = _run(nc, [given], core_ids=[0])
    return r.results[0]["out_x"]
```

```python
from contextlib import ExitStack

import numpy as np

import concourse.bass as bass
from concourse import mybir

SECTIONS = "ACDEFGHI"

F32 = mybir.dt.float32
U8 = mybir.dt.uint8
BF16 = mybir.dt.bfloat16
F16 = mybir.dt.float16
ALU = mybir.AluOpType
ACT = mybir.ActivationFunctionType
AX = mybir.AxisListType

B = 32
S = 128
D = 128
CL = 77
U = 4
NG = B // U
UC = U * CL
NH = 16
HD = D // NH
HL = 8
NU = U * NH // HL
SCORE, TURN, OUT = 0, 4, 6
LN_EPS = 1e-5
MASKED = -1e30
LAYERS = 6
FFN = 512
EXPERTS = 8

SIGNALS = [
    "loaded", "loaded_q", "stored", "vector_step", "scalar_step", "var_ready", "rstd_ready", "z_ready",
    "zT_done", "xnT_ready", "scores_done", "shifted", "exp_done", "turned", "pT_ready", "pv_done",
    "o_normed", "proj_done", "k_done", "k_read", "v_done", "v_read", "q_done", "q_read", "rope_done",
    "o_turned", "oT_ready", "mix_done", "mix_added", "hid_done", "hid_ready", "ffn_done", "gate_done",
    "gate_ready", "upd_done", "upd_ready", "expert_done", "expert_ready", "x_ready", "gram_done",
    "rest_ready", "peaks_ready", "low_ready", "masked_a", "masked_v", "table_ready", "outer_ready",
    "cand_ready",
]


class Steps:

    def __init__(self, eng, sem):
        self.eng, self.sem, self.n = eng, sem, 0

    def __call__(self, ins):
        ins.then_inc(self.sem, 1)
        self.n += 1
        self.eng.wait_ge(self.sem, self.n)


def build(nc, dram, out):
    with ExitStack() as ctx:
        def sb(name, shape, dt=F32, scope=ctx):
            return scope.enter_context(nc.sbuf_tensor(name, shape, dt))

        sem = {name: ctx.enter_context(nc.semaphore(name)) for name in SIGNALS}
        numbers = sorted(s.num for s in sem.values())
        all_signals = range(numbers[0], numbers[-1] + 1)
        assert len(numbers) == len(all_signals)

        def rest():
            nc.sync.sem_clear(all_signals)
            nc.all_engine_barrier()

        x_all = sb("x_all", [S, B, D])
        ctx_tm = sb("ctx_tm", [CL, B, D])
        ctxT = sb("ctxT", [D, B * CL])
        condT = sb("condT", [D, B])
        ident = sb("ident", [128, 128])
        ones = sb("ones", [128, 128])
        neghalf = sb("neghalf", [128, 64])
        zn = sb("zn", [128, U, D + 1])
        stats = sb("stats", [128, U, 6])
        mv = sb("mv", [128, U, 2])
        veps = sb("veps", [128, U])
        rstd = sb("rstd", [128, U])
        xnT = sb("xnT", [D, U * S])
        xs = sb("xs", [S, U, D])
        e = sb("e", [128, 2, HL * S])
        pT = sb("pT", [128, 2, HL, S])
        ph = pT[:].rearrange("p b h s -> p (b h s)")[:, 0:HL * S].bitcast(F16).rearrange("p (b h s) -> p b h s", b=2, h=HL)
        pl = pT[:].rearrange("p b h s -> p (b h s)")[:, HL * S:2 * HL * S].bitcast(F16).rearrange("p (b h s) -> p b h s", b=2, h=HL)
        mx = sb("mx", [128, 2, HL])
        rec = sb("rec", [128, 2, HL])
        ones_b = sb("ones_b", [1, 128], BF16)
        osum = sb("osum", [128, 2, HL, HD + 1])
        ps = ctx.enter_context(nc.psum_tensor("ps", [128, 8, 512], F32))

        def per(bank, n=D):
            return ps[:, bank, 0:U * n].rearrange("p (u d) -> p u d", u=U)

        def ln_vector(dve, step, r, src, dst=None, rows=128, n=U):
            dst = dst or (lambda u: zn[0:rows, u, 0:D])
            for u in range(n):
                last = nc.vector.bn_stats(stats[0:rows, u, :], src(u))
            step(last)
            for u in range(n):
                last = nc.vector.bn_aggr(mv[0:rows, u, :], stats[0:rows, u, :])
            step(last)
            nc.vector.tensor_scalar(veps[0:rows, 0:n], mv[0:rows, 0:n, 1], LN_EPS, None, ALU.add).then_inc(sem["var_ready"], 1)
            dve.wait_ge(sem["rstd_ready"], r + 1)
            for u in range(n):
                last = nc.vector.tensor_scalar(dst(u), src(u), mv[0:rows, u, 0:1], rstd[0:rows, u:u + 1],
                                               ALU.subtract, ALU.mult)
            return last

        def ln_pool(pool, r, rows=128, n=U):
            pool.wait_ge(sem["var_ready"], r + 1)
            nc.gpsimd.tensor_tensor(rstd[0:rows, 0:n], veps[0:rows, 0:n], neghalf[0:rows, 0:n],
                                    ALU.pow).then_inc(sem["rstd_ready"], 1)

        def turn_rows(pe, r, bank=0, rows=128):
            pe.wait_ge(sem["z_ready"], r + 1)
            for u in range(U):
                last = nc.tensor.transpose(ps[:, bank, u * rows:(u + 1) * rows], zn[0:rows, u, 0:D],
                                           ident[0:rows, 0:rows])
            last.then_inc(sem["zT_done"], 1)

        WIDE = D // 2

        def attn_tensor(pe, a, keys, q_of, k_of, v_of):
            def scores(n):
                u, half = n // 2, n % 2
                if n >= 2:
                    pe.wait_ge(sem["shifted"], NU * a + n - 1)
                for i in range(HL):
                    last = nc.tensor.matmul(ps[:, SCORE + 2 * half + i // 4, (i % 4) * S:(i % 4 + 1) * S],
                                            q_of(HL * half + i, u), k_of(HL * half + i, u), start=True, stop=True)
                last.then_inc(sem["scores_done"], 1)

            def turn(n):
                N = NU * a + n
                pe.wait_ge(sem["exp_done"], N + 1)
                if N >= 1:
                    pe.wait_ge(sem["pT_ready"], 2 * N)
                for i in range(HL):
                    last = nc.tensor.transpose(ps[0:keys, TURN + i // 4, (i % 4) * S:(i % 4 + 1) * S],
                                               e[:, n % 2, i * keys:(i + 1) * keys], ident[:, :])
                    if i % 4 == 3:
                        last.then_inc(sem["turned"], 1)

            def values(n):
                N, u, half = NU * a + n, n // 2, n % 2
                pe.wait_ge(sem["pT_ready"], 2 * N + 2)
                if N >= 1:
                    pe.wait_ge(sem["o_normed"], N)
                for i in range(HL):
                    last = nc.tensor.matmul(ps[:, OUT + i // 4, (i % 4) * S:(i % 4 + 1) * S], pT[0:keys, n % 2, i, :],
                                            v_of(HL * half + i, u), start=True, stop=True)
                last.then_inc(sem["pv_done"], 1)

            scores(0)
            scores(1)
            for n in range(NU):
                turn(n)
                if n + 2 < NU:
                    scores(n + 2)
                values(n)

        def attn_vector(dve, step, a, keys, o_of):
            def shift(n):
                N, half = NU * a + n, n % 2
                view = ps[:, SCORE + 2 * half:SCORE + 2 * half + 2, :].rearrange(
                    "p b (s k) -> p (b s) k", s=4)[:, :, 0:keys]
                dve.wait_ge(sem["scores_done"], N + 1)
                m = mx[:, n % 2, :]
                step(nc.vector.tensor_reduce(m, view, AX.X, ALU.max))
                if N >= 2:
                    dve.wait_ge(sem["turned"], 2 * N - 2)
                nc.vector.tensor_tensor(
                    e[:, n % 2, 0:HL * keys].rearrange("p (h k) -> p h k", h=HL), view,
                    m.unsqueeze(2).broadcast_to([128, HL, keys]), ALU.subtract).then_inc(sem["shifted"], 1)

            def norm(n):
                N, u, half = NU * a + n, n // 2, n % 2
                dve.wait_ge(sem["pv_done"], N + 1)
                p = ps[:, OUT:OUT + 2, :].rearrange("p b (h d) -> p (b h) d", d=S)
                step(nc.vector.reciprocal(rec[:, n % 2, :], p[:, :, WIDE]))
                nc.vector.tensor_tensor(
                    o_of(u)[:, HL * half * WIDE:HL * (half + 1) * WIDE].rearrange("p (h d) -> p h d", d=WIDE),
                    p[:, :, 0:WIDE], rec[:, n % 2, :].unsqueeze(2).broadcast_to([128, HL, WIDE]),
                    ALU.mult).then_inc(sem["o_normed"], 1)

            shift(0)
            for n in range(NU):
                if n + 1 < NU:
                    shift(n + 1)
                norm(n)

        def attn_scalar(act, a, keys, scale):
            def exponential(n):
                act.wait_ge(sem["shifted"], NU * a + n + 1)
                nc.scalar.activation(e[:, n % 2, 0:HL * keys], e[:, n % 2, 0:HL * keys], ACT.Exp,
                                     scale=scale).then_inc(sem["exp_done"], 1)

            for n in range(NU):
                N = NU * a + n
                exponential(n)
                if N >= 2:
                    act.wait_ge(sem["pv_done"], N - 1)
                for b in range(2):
                    act.wait_ge(sem["turned"], 2 * N + b + 1)
                    nc.scalar.activation(pT[0:keys, n % 2, 4 * b:4 * b + 4, :],
                                         ps[0:keys, TURN + b, :].rearrange("p (h s) -> p h s", h=4),
                                         ACT.Copy).then_inc(sem["pT_ready"], 1)

        HP = HD + 1

        def masked_by_vector(h):
            return h % 8 < 5

        def mask_queries(eng, pair, src, qm, blocks):
            at = slice(pair * 2 * S, (pair + 1) * 2 * S)
            for h in range(NH):
                if eng == "vector" and masked_by_vector(h):
                    nc.vector.tensor_scalar(qm[:, h, at], src[:, at], blocks[:, h:h + 1], None, ALU.mult).then_inc(sem["masked_v"], 1)
                if eng == "scalar" and not masked_by_vector(h):
                    nc.scalar.activation(qm[:, h, at], src[:, at], ACT.Copy, scale=blocks[:, h:h + 1]).then_inc(sem["masked_a"], 1)

        PADDED = (U - 1) * CL + S

        def small_tensor(pe, a, keys, qm, kT, vp, low=None, values_split=1, turn_free=0, early=None, late_keys=0):
            def scores(n):
                u, half = n // 2, n % 2
                if n >= 2:
                    pe.wait_ge(sem["exp_done"], NU * a + n - 1)
                if u % 2 == 0:
                    k = 4 * a + 2 * (u // 2) + half + 1
                    pe.wait_ge(sem["masked_v"], 5 * k)
                    pe.wait_ge(sem["masked_a"], 3 * k)
                if u == 2 and late_keys:
                    pe.wait_ge(sem["table_ready"], late_keys)
                for c in range(2):
                    bank = SCORE + 2 * half + c
                    if low is not None:
                        nc.tensor.matmul(ps[:, bank, :].rearrange("p (s k) -> p s k", s=4), ones_b[0:1, :],
                                         low[0:1, u * keys:u * keys + S].unsqueeze(1).broadcast_to([1, 4, S]),
                                         start=True, stop=False, skip_group_check=True)
                    for slot in range(4):
                        h = HL * half + 4 * c + slot
                        last = nc.tensor.matmul(ps[:, bank, slot * S:(slot + 1) * S], qm[:, h, u * S:(u + 1) * S],
                                                kT[:, u * keys:u * keys + S], start=(low is None), stop=True,
                                                skip_group_check=True)
                last.then_inc(sem["scores_done"], 1)

            def turn(n):
                N = NU * a + n
                pe.wait_ge(sem["exp_done"], N + 1)
                if N >= 1:
                    pe.wait_ge(sem["rest_ready"], 2 * N)
                if n == 0 and turn_free:
                    pe.wait_ge(sem["rope_done"], turn_free)
                for i in range(HL):
                    last = nc.tensor.transpose(ps[0:keys, TURN + i // 4, (i % 4) * S:(i % 4 + 1) * S],
                                               e[:, n % 2, i * keys:(i + 1) * keys], ident[:, :])
                    if i % 4 == 3:
                        last.then_inc(sem["turned"], 1)

            def values(n):
                N, u, half = NU * a + n, n // 2, n % 2
                if n == 0:
                    pe.wait_ge(sem["v_read"], values_split)
                if N >= 2:
                    pe.wait_ge(sem["o_normed"], N - 1)
                for i in range(HL):
                    if i % 4 == 0:
                        pe.wait_ge(sem["rest_ready"], 2 * N + i // 4 + 1)
                    at = ps[:, OUT + n % 2, i * 3 * HP:(i + 1) * 3 * HP]
                    v = vp[0:keys, u, HL * half + i, :]
                    nc.tensor.matmul(at, ph[0:keys, n % 2, i, :], v, start=True, stop=False, skip_group_check=True)
                    last = nc.tensor.matmul(at[:, 0:2 * HP], pl[0:keys, n % 2, i, :], v[:, 0:2 * HP], start=False, stop=True,
                                            skip_group_check=True)
                last.then_inc(sem["pv_done"], 1)

            scores(0)
            scores(1)
            for n in range(NU):
                turn(n)
                if n + 2 < NU:
                    scores(n + 2)
                elif early:
                    early(n - NU + 2)
                values(n)

        def by_vector(keys):
            return 2 if keys == S else 4

        def small_vector(dve, step, a, keys, o_of, between=None, early=None):
            def shift(n):
                N, half, nd = NU * a + n, n % 2, by_vector(keys)
                view = ps[:, SCORE + 2 * half:SCORE + 2 * half + 2, :].rearrange(
                    "p b (s k) -> p (b s) k", s=4)[:, :, 0:keys]
                dve.wait_ge(sem["scores_done"], N + 1)
                if N >= 2:
                    dve.wait_ge(sem["turned"], 2 * N - 2)
                m = mx[:, n % 2, :]
                nc.vector.tensor_reduce(m, view, AX.X, ALU.max, negate=True).then_inc(sem["peaks_ready"], 1)
                dve.wait_ge(sem["peaks_ready"], N + 1)
                nc.vector.tensor_tensor(
                    e[:, n % 2, 0:nd * keys].rearrange("p (h k) -> p h k", h=nd), view[:, 0:nd],
                    m[:, 0:nd].unsqueeze(2).broadcast_to([128, nd, keys]), ALU.add).then_inc(sem["shifted"], 1)

            def rest_of(n):
                N = NU * a + n
                if N >= 2:
                    dve.wait_ge(sem["pv_done"], N - 1)
                for b in range(2):
                    dve.wait_ge(sem["pT_ready"], 2 * N + b + 1)
                    nc.vector.tensor_tensor(pl[0:keys, n % 2, 4 * b:4 * b + 4, :],
                                            ps[0:keys, TURN + b, :].rearrange("p (h s) -> p h s", h=4),
                                            ph[0:keys, n % 2, 4 * b:4 * b + 4, :], ALU.subtract).then_inc(sem["rest_ready"], 1)

            def norm(n):
                N, u, half = NU * a + n, n // 2, n % 2
                dve.wait_ge(sem["pv_done"], N + 1)
                p = ps[:, OUT + n % 2, 0:HL * 3 * HP].rearrange("p (h c d) -> p h d c", c=3, d=HP)
                step(nc.vector.tensor_reduce(osum[:, n % 2], p, AX.X, ALU.add))
                step(nc.vector.reciprocal(rec[:, n % 2, :], osum[:, n % 2, :, HD]))
                nc.vector.tensor_tensor(
                    o_of(u)[:, HL * half * HD:HL * (half + 1) * HD].rearrange("p (h d) -> p h d", d=HD),
                    osum[:, n % 2, :, 0:HD], rec[:, n % 2, :].unsqueeze(2).broadcast_to([128, HL, HD]),
                    ALU.mult).then_inc(sem["o_normed"], 1)

            for n in range(NU):
                shift(n)
                if n == 0 and between:
                    between()
                if n >= 2:
                    norm(n - 2)
                if n >= 1:
                    rest_of(n - 1)
            norm(NU - 2)
            if early:
                early(0)
            rest_of(NU - 1)
            if early:
                early(1)
            norm(NU - 1)

        def small_scalar(act, a, keys, early=None):
            nd = by_vector(keys)

            def own(n, i):
                return nc.scalar.activation(e[:, n % 2, i * keys:(i + 1) * keys],
                                            ps[:, SCORE + 2 * (n % 2) + i // 4, (i % 4) * S:(i % 4) * S + keys], ACT.Exp,
                                            bias=mx[:, n % 2, i:i + 1])

            def exponential(n):
                act.wait_ge(sem["peaks_ready"], NU * a + n + 1)
                for i in range(4, HL):
                    own(n, i)
                act.wait_ge(sem["shifted"], NU * a + n + 1)
                for i in range(nd, 4):
                    own(n, i)
                nc.scalar.activation(e[:, n % 2, 0:nd * keys], e[:, n % 2, 0:nd * keys], ACT.Exp).then_inc(sem["exp_done"], 1)

            for n in range(NU):
                N = NU * a + n
                exponential(n)
                if n == NU - 1 and early:
                    early()
                if N >= 2:
                    act.wait_ge(sem["pv_done"], N - 1)
                for b in range(2):
                    act.wait_ge(sem["turned"], 2 * N + b + 1)
                    nc.scalar.activation(ph[0:keys, n % 2, 4 * b:4 * b + 4, :],
                                         ps[0:keys, TURN + b, :].rearrange("p (h s) -> p h s", h=4),
                                         ACT.Copy).then_inc(sem["pT_ready"], 1)

        def split(step, src, part, rest_):
            step(nc.vector.tensor_copy(part(0), src))
            nc.vector.tensor_tensor(rest_, src, part(0), ALU.subtract)
            step(nc.vector.tensor_tensor(part(1), src, part(0), ALU.subtract))
            return nc.vector.tensor_tensor(part(2), rest_, part(1), ALU.subtract)

        def split_values(step, bank, vp, rows):
            return split(step, per(bank)[0:rows].rearrange("p u (h d) -> p u h d", d=HD),
                         lambda i: vp[0:rows, :, :, i * HP:i * HP + HD],
                         vrest[0:rows].rearrange("p u (h d) -> p u h d", d=HD))

        with nc.Block() as block:
            @block.sync
            def _(sp):
                sp.dma_start(ident[:], dram["ident"]).then_inc(sem["loaded"], 16)
                sp.dma_start(ctx_tm[:], dram["ctx_1024"].rearrange("b t d -> t b d")).then_inc(sem["loaded"], 16)
                sp.dma_start(x_all[:], dram["x"].rearrange("b t d -> t b d")).then_inc(sem["loaded_q"], 16)
                sp.dma_start(condT[:], dram["condT"]).then_inc(sem["loaded_q"], 16)
                sp.wait_ge(sem["loaded_q"], 32)

            @block.vector
            def _(dve):
                nc.vector.memset(ones[:], 1.0)
                nc.vector.memset(neghalf[:], -0.5)
                nc.vector.memset(ones_b[:], 1.0)
                nc.vector.memset(zn[:], 1.0)
                for b in range(B):
                    if b % U == U - 1:
                        g = b // U
                        dve.wait_ge(sem["zT_done"], g + 1)
                        nc.vector.tensor_copy(ctxT[:, g * UC:(g + 1) * UC],
                                              ps[:, g % 2, 0:UC]).then_inc(sem["xnT_ready"], 1)

            @block.tensor
            def _(pe):
                pe.wait_ge(sem["loaded"], 32)
                for g in range(NG):
                    if g >= 2:
                        pe.wait_ge(sem["xnT_ready"], g - 1)
                    for u in range(U):
                        last = nc.tensor.transpose(ps[:, g % 2, u * CL:(u + 1) * CL], ctx_tm[:, g * U + u, :],
                                                   ident[0:CL, 0:CL])
                    last.then_inc(sem["zT_done"], 1)
        rest()

        gram = sb("gram", [D, D + 1])
        def stage_slots():
            with ExitStack() as st:
                names = ["wk", "wv", "wq", "wu", "w1", "w2"]
                w = {n: sb("A_" + n, [D, D], scope=st) for n in names}
                cols = ["lnkv_g", "lnkv_b", "lnq_g", "lnq_b", "lnm_g", "lnm_b", "bk", "bv", "bq", "b1"]
                col = {n: sb("A_c_" + n, [D, 1], scope=st) for n in cols}
                wide = ["q_mu", "q_logsig", "lnp_g", "lnp_b"]
                row = {n: sb("A_r_" + n, [128, D], scope=st) for n in wide}
                bu = sb("A_bu", [1, D], scope=st)
                b2 = sb("A_b2", [1, D], scope=st)
                cond_bc = sb("A_cond", [128, B * D], scope=st)
                def each(name, shape, first=None):
                    return [first or sb(f"A_{name}0", shape, scope=st), sb(f"A_{name}1", shape, scope=st)]

                cTs = each("cT", [D, UC])
                kTs = each("kT", [D, UC])
                qTs = each("qT", [D, U * S])
                v1s = each("v1", [CL, U, D + 1])
                attns = each("attn", [CL, U, S])
                ams = each("am", [CL, U])
                ars = each("ar", [CL, U])
                urs = each("ur", [128, U])
                zns = each("zn", [128, U, D + 1], zn)
                xnTs = each("xnT", [D, U * S], xnT)
                xss = each("xs", [S, U, D], xs)
                statss = each("stats", [128, U, 6], stats)
                mvs = each("mv", [128, U, 2], mv)
                vepss = each("veps", [128, U], veps)
                rstds = each("rstd", [128, U], rstd)
                n_loads = len(names) + len(cols) + len(wide) + 3

                with nc.Block() as block:
                    @block.sync
                    def _(sp):
                        for n in names:
                            sp.dma_start(w[n][:], dram["L0_xcond_" + n]).then_inc(sem["loaded"], 16)
                        for n in cols:
                            sp.dma_start(col[n][:], dram["L0_xcond_" + n].unsqueeze(1)).then_inc(sem["loaded"], 16)
                        for n in wide:
                            src = dram["L0_xcond_" + n]
                            src = src.rearrange("a b d -> (a b d)") if n.startswith("q_") else src
                            sp.dma_start(row[n][:], src.partition_broadcast(128)).then_inc(sem["loaded"], 16)
                        sp.dma_start(bu[:], dram["L0_xcond_bu"].unsqueeze(0)).then_inc(sem["loaded"], 16)
                        sp.dma_start(b2[:], dram["L0_xcond_b2"].unsqueeze(0)).then_inc(sem["loaded"], 16)
                        sp.dma_start(cond_bc[:], dram["cond_1024"].rearrange("b d -> (b d)").partition_broadcast(128)).then_inc(sem["loaded"], 16)
                        sp.wait_ge(sem["loaded"], 16 * n_loads)

                    @block.scalar
                    def _(act):
                        act.wait_ge(sem["loaded"], 16 * n_loads)
                        nc.scalar.activation(row["q_logsig"][:], row["q_logsig"][:], ACT.Exp)

                    @block.vector
                    def _(dve):
                        for t in (*v1s, zns[1]):
                            nc.vector.memset(t[:], 1.0)
                        nc.vector.memset(gram[:], 0.0)
                rest()

                def over(t):
                    return t[:].unsqueeze(1).broadcast_to([128, U, D])

                def at(k, j):
                    return 2 * k + j + 1

                def bank(j, k):
                    return 4 * j + k

                with nc.Fori(0, NG // 2) as g2:
                    with nc.Block() as block:
                        @block.vector
                        def _(dve):
                            step = Steps(dve, sem["vector_step"])

                            def both(op):
                                for j in range(2):
                                    last = op(j)
                                return last

                            def ln(r, src, rows=128, signal=None):
                                for j in range(2):
                                    for u in range(U):
                                        last = nc.vector.bn_stats(statss[j][0:rows, u, :], src(j, u))
                                step(last)
                                for j in range(2):
                                    for u in range(U):
                                        last = nc.vector.bn_aggr(mvs[j][0:rows, u, :], statss[j][0:rows, u, :])
                                step(last)
                                for j in range(2):
                                    nc.vector.tensor_scalar(vepss[j][0:rows], mvs[j][0:rows, :, 1], LN_EPS, None, ALU.add).then_inc(sem["var_ready"], 1)
                                for j in range(2):
                                    dve.wait_ge(sem["rstd_ready"], at(r, j))
                                    for u in range(U):
                                        last = nc.vector.tensor_scalar(zns[j][0:rows, u, 0:D], src(j, u), mvs[j][0:rows, u, 0:1],
                                                                       rstds[j][0:rows, u:u + 1], ALU.subtract, ALU.mult)
                                    if signal:
                                        last.then_inc(sem[signal], 1)
                                return last

                            def add_in(j):
                                return nc.vector.tensor_tensor(xss[j][:], xss[j][:], per(bank(j, 1)), ALU.add)

                            def rows_of(j, u):
                                return xss[j][:, u, :]

                            ln(0, lambda j, u: ctx_tm[:, g2 * (2 * U) + j * U + u, :], rows=CL, signal="z_ready")
                            dve.wait_ge(sem["zT_done"], at(0, 1))
                            step(ln(1, lambda j, u: x_all[:, g2 * (2 * U) + j * U + u, :]))
                            step(both(lambda j: nc.vector.tensor_tensor(xss[j][:], zns[j][:, :, 0:D], over(row["q_logsig"]), ALU.mult)))
                            step(both(lambda j: nc.vector.tensor_tensor(xss[j][:], xss[j][:], over(row["q_mu"]), ALU.add)))
                            for j in range(2):
                                dve.wait_ge(sem["v_done"], at(0, j))
                                nc.vector.tensor_copy(v1s[j][:, :, 0:D], per(bank(j, 2))[0:CL]).then_inc(sem["v_read"], 1)
                            for it in range(3):
                                ln(3 * it + 2, rows_of, signal="z_ready")
                                for j in range(2):
                                    am, attn = ams[j], attns[j]
                                    dve.wait_ge(sem["scores_done"], at(it, j))
                                    step(nc.vector.tensor_reduce(am[:], per(bank(j, 2))[0:CL], AX.X, ALU.max))
                                    nc.vector.tensor_tensor(attn[:], per(bank(j, 2))[0:CL], am[:].unsqueeze(2).broadcast_to([CL, U, S]),
                                                            ALU.subtract).then_inc(sem["shifted"], 1)
                                for j in range(2):
                                    ar, attn = ars[j], attns[j]
                                    dve.wait_ge(sem["exp_done"], at(it, j))
                                    step(nc.vector.tensor_reduce(ar[:], attn[:], AX.X, ALU.add))
                                    step(nc.vector.reciprocal(ar[:], ar[:]))
                                    step(nc.vector.tensor_tensor(attn[:], attn[:], ar[:].unsqueeze(2).broadcast_to([CL, U, S]), ALU.mult))
                                    nc.vector.tensor_scalar(attn[:], attn[:], 1e-8, None, ALU.add).then_inc(sem["upd_ready"], 1)
                                for j in range(2):
                                    dve.wait_ge(sem["upd_done"], at(it, j))
                                    up = ps[:, bank(j, 2):bank(j, 4), 0:2 * (D + 1)].rearrange("p b (u d) -> p b u d", u=2)
                                    ur4 = urs[j][:].rearrange("p (b u) -> p b u", b=2)
                                    step(nc.vector.reciprocal(ur4, up[:, :, :, D]))
                                    nc.vector.tensor_tensor(zns[j][:, :, 0:D].rearrange("p (b u) d -> p b u d", b=2), up[:, :, :, 0:D],
                                                            ur4.unsqueeze(3).broadcast_to([128, 2, 2, D]), ALU.mult).then_inc(sem["o_normed"], 1)
                                for j in range(2):
                                    dve.wait_ge(sem["mix_done"], at(it, j))
                                    step(add_in(j))
                                ln(3 * it + 3, rows_of, signal="z_ready")
                                for j in range(2):
                                    dve.wait_ge(sem["ffn_done"], at(it, j))
                                    step(add_in(j))
                                step(both(lambda j: nc.vector.tensor_tensor(
                                    xss[j][:].rearrange("p u d -> p (u d)"), xss[j][:].rearrange("p u d -> p (u d)"),
                                    cond_bc[:, bass.ds(g2 * (2 * U * D) + j * U * D, U * D)], ALU.add)))
                                step(ln(3 * it + 4, rows_of))
                                step(both(lambda j: nc.vector.tensor_tensor(xss[j][:], zns[j][:, :, 0:D], over(row["lnp_g"]), ALU.mult)))
                                step(both(lambda j: nc.vector.tensor_tensor(xss[j][:], xss[j][:], over(row["lnp_b"]), ALU.add)))
                            xg = lambda j: x_all[:, bass.ds(g2 * (2 * U) + j * U, U), :]
                            step(both(lambda j: nc.vector.tensor_tensor(xg(j), xg(j), xss[j][:], ALU.add)))
                            ln(11, lambda j, u: x_all[:, g2 * (2 * U) + j * U + u, :], signal="x_ready")
                            for j in range(2):
                                dve.wait_ge(sem["gram_done"], at(0, j))
                                step(nc.vector.tensor_tensor(gram[:], gram[:], ps[:, bank(j, 0), 0:D + 1], ALU.add))

                        @block.gpsimd
                        def _(pool):
                            for r in range(12):
                                rows = CL if r == 0 else 128
                                for j in range(2):
                                    pool.wait_ge(sem["var_ready"], at(r, j))
                                    nc.gpsimd.tensor_tensor(rstds[j][0:rows], vepss[j][0:rows], neghalf[0:rows, 0:U],
                                                            ALU.pow).then_inc(sem["rstd_ready"], 1)

                        @block.scalar
                        def _(act):
                            def turned(j, bias, scale=None):
                                return nc.scalar.activation(xnTs[j][:], ps[:, bank(j, 0), :], ACT.Identity, bias=col[bias][:],
                                                            scale=col[scale][:] if scale else 1.0)

                            for j in range(2):
                                act.wait_ge(sem["zT_done"], at(0, j))
                                nc.scalar.activation(cTs[j][:], ps[:, bank(j, 0), 0:UC], ACT.Identity, bias=col["lnkv_b"][:],
                                                     scale=col["lnkv_g"][:]).then_inc(sem["xnT_ready"], 1)
                            for j in range(2):
                                act.wait_ge(sem["k_done"], at(0, j))
                                nc.scalar.activation(kTs[j][:], ps[:, bank(j, 1), 0:UC], ACT.Identity, bias=col["bk"][:]).then_inc(sem["k_read"], 1)
                            for it in range(3):
                                for j in range(2):
                                    act.wait_ge(sem["zT_done"], at(2 * it + 1, j))
                                    turned(j, "lnq_b", "lnq_g").then_inc(sem["xnT_ready"], 1)
                                for j in range(2):
                                    act.wait_ge(sem["q_done"], at(it, j))
                                    nc.scalar.activation(qTs[j][:], ps[:, bank(j, 1), :], ACT.Identity, bias=col["bq"][:]).then_inc(sem["q_read"], 1)
                                for j in range(2):
                                    act.wait_ge(sem["shifted"], at(it, j))
                                    nc.scalar.activation(attns[j][:], attns[j][:], ACT.Exp, scale=float(D) ** 0.5).then_inc(sem["exp_done"], 1)
                                for j in range(2):
                                    act.wait_ge(sem["o_turned"], at(it, j))
                                    turned(j, "bv").then_inc(sem["oT_ready"], 1)
                                for j in range(2):
                                    act.wait_ge(sem["zT_done"], at(2 * it + 2, j))
                                    turned(j, "lnm_b", "lnm_g").then_inc(sem["xnT_ready"], 1)
                                for j in range(2):
                                    act.wait_ge(sem["hid_done"], at(it, j))
                                    nc.scalar.activation(qTs[j][:], ps[:, bank(j, 1), :], ACT.Gelu, bias=col["b1"][:]).then_inc(sem["hid_ready"], 1)

                        @block.tensor
                        def _(pe):
                            def turn(k, rows=128):
                                for j in range(2):
                                    pe.wait_ge(sem["z_ready"], at(k, j))
                                    for u in range(U):
                                        last = nc.tensor.transpose(ps[:, bank(j, 0), u * rows:(u + 1) * rows], zns[j][0:rows, u, 0:D],
                                                                   ident[0:rows, 0:rows])
                                    last.then_inc(sem["zT_done"], 1)

                            def through(j, src, m, bias):
                                for u in range(U):
                                    nc.tensor.matmul(per(bank(j, 1))[:, u, :], src[:, u * S:(u + 1) * S], w[m][:], start=True, stop=False)
                                    last = nc.tensor.matmul(per(bank(j, 1))[:, u, :], ones[0:1, :], bias[:], start=False, stop=True)
                                return last

                            turn(0, rows=CL)
                            for j in range(2):
                                pe.wait_ge(sem["xnT_ready"], at(0, j))
                                nc.tensor.matmul(ps[:, bank(j, 1), 0:UC], w["wk"][:], cTs[j][:], start=True, stop=True).then_inc(sem["k_done"], 1)
                                for u in range(U):
                                    last = nc.tensor.matmul(ps[0:CL, bank(j, 2), u * D:(u + 1) * D], cTs[j][:, u * CL:(u + 1) * CL], w["wv"][:],
                                                            start=True, stop=True)
                                last.then_inc(sem["v_done"], 1)
                            pe.wait_ge(sem["k_read"], at(0, 1))
                            pe.wait_ge(sem["v_read"], at(0, 1))
                            for it in range(3):
                                turn(2 * it + 1)
                                for j in range(2):
                                    pe.wait_ge(sem["xnT_ready"], at(2 * it + 1, j))
                                    nc.tensor.matmul(ps[:, bank(j, 1), :], w["wq"][:], xnTs[j][:], start=True, stop=True).then_inc(sem["q_done"], 1)
                                for j in range(2):
                                    pe.wait_ge(sem["q_read"], at(it, j))
                                    for u in range(U):
                                        last = nc.tensor.matmul(ps[0:CL, bank(j, 2), u * S:(u + 1) * S], kTs[j][:, u * CL:(u + 1) * CL],
                                                                qTs[j][:, u * S:(u + 1) * S], start=True, stop=True)
                                    last.then_inc(sem["scores_done"], 1)
                                for j in range(2):
                                    pe.wait_ge(sem["upd_ready"], at(it, j))
                                    for u in range(U):
                                        last = nc.tensor.matmul(ps[:, bank(j, 2) + u // 2, (u % 2) * (D + 1):(u % 2 + 1) * (D + 1)],
                                                                attns[j][:, u, :], v1s[j][:, u, :], start=True, stop=True)
                                    last.then_inc(sem["upd_done"], 1)
                                for j in range(2):
                                    pe.wait_ge(sem["o_normed"], at(it, j))
                                    for u in range(U):
                                        last = nc.tensor.transpose(ps[:, bank(j, 0), u * S:(u + 1) * S], zns[j][:, u, 0:D], ident[:])
                                    last.then_inc(sem["o_turned"], 1)
                                for j in range(2):
                                    pe.wait_ge(sem["oT_ready"], at(it, j))
                                    through(j, xnTs[j], "wu", bu).then_inc(sem["mix_done"], 1)
                                turn(2 * it + 2)
                                for j in range(2):
                                    pe.wait_ge(sem["xnT_ready"], at(2 * it + 2, j))
                                    nc.tensor.matmul(ps[:, bank(j, 1), :], w["w1"][:], xnTs[j][:], start=True, stop=True).then_inc(sem["hid_done"], 1)
                                for j in range(2):
                                    pe.wait_ge(sem["hid_ready"], at(it, j))
                                    through(j, qTs[j], "w2", b2).then_inc(sem["ffn_done"], 1)
                            for j in range(2):
                                pe.wait_ge(sem["x_ready"], at(0, j))
                                for u in range(U):
                                    last = nc.tensor.matmul(ps[:, bank(j, 0), 0:D + 1], zns[j][:, u, 0:D], zns[j][:, u, :],
                                                            start=(u == 0), stop=(u == U - 1))
                                last.then_inc(sem["gram_done"], 1)
                    rest()

        if "A" in SECTIONS or "C" in SECTIONS:
            stage_slots()

        def stage_product_keys():
            QH, KEYS, HALF, TOP, E = 8, 32, 16, 4, D
            QD = 2 * HALF
            NQ = QH * QD
            CELLS = 2 * QH
            PAD, TAKEN = 3e38, -3e38
            with ExitStack() as st:
                wq = sb("C_wq", [D, NQ], scope=st)
                bq = sb("C_bq", [128, NQ], scope=st)
                gamma = sb("C_gamma", [128, QD], scope=st)
                beta = sb("C_beta", [128, QD], scope=st)
                keys = sb("C_keys", [KEYS, 2, HALF], scope=st)
                ksq = sb("C_ksq", [KEYS, 2, HALF], scope=st)
                kn2 = sb("C_kn2", [KEYS, 2], scope=st)
                keys4 = sb("C_keys4", [KEYS, 4, QD], scope=st)
                kblk = sb("C_kblk", [128, 8, KEYS], scope=st)
                blocks = sb("C_blocks", [128, 8], scope=st)
                keysT = sb("C_keysT", [128, KEYS], scope=st)
                down = sb("C_down", [D, E], scope=st)
                up = sb("C_up", [E, D], scope=st)
                mean_h = sb("C_mean_h", [128, D], scope=st)
                prod = sb("C_prod", [128, NQ], scope=st)
                mean_q = sb("C_mean_q", [128, NQ], scope=st)
                var_q = sb("C_var_q", [128, NQ], scope=st)
                m_r = sb("C_m_r", [128, QD], scope=st)
                v_r = sb("C_v_r", [128, QD], scope=st)
                a_r = sb("C_a_r", [128, QD], scope=st)
                wT = sb("C_wT", [128, 2 * NQ], scope=st)
                wkey = sb("C_wkey", [D, 2 * NQ], scope=st)
                bkey = sb("C_bkey", [1, 2 * NQ], scope=st)
                sq = sb("C_sq", [128, 2, NQ], scope=st)
                n2 = sb("C_n2", [128, 2, CELLS], scope=st)
                rn = sb("C_rn", [128, 2, CELLS], scope=st)
                cand = sb("C_cand", [128, 2, CELLS, KEYS + TOP], scope=st)
                best = sb("C_best", [128, 2, CELLS, 8], scope=st)
                left = sb("C_left", [128, CELLS, KEYS + TOP], scope=st)
                ex = sb("C_ex", [128, 2, CELLS, KEYS], scope=st)
                z = sb("C_z", [128, CELLS], scope=st)
                tail = sb("C_tail", [128, 2], scope=st)
                outer = sb("C_outer", [128, 2, QH, 4, KEYS], scope=st)
                coef = sb("C_coef", [128, E], scope=st)
                act_g = sb("C_act", [128, U, E], scope=st)
                yT = sb("C_yT", [E, U * S], scope=st)

                with nc.Block() as block:
                    @block.sync
                    def _(sp):
                        pairs = [(wq[:], dram["L0_ffn_Wq"]), (bq[:], dram["L0_ffn_bq"].partition_broadcast(128)),
                                 (gamma[:], dram["L0_ffn_bn_gamma"].partition_broadcast(128)),
                                 (beta[:], dram["L0_ffn_bn_beta"].partition_broadcast(128)),
                                 (keys[:, 0, :], dram["L0_ffn_sub_key0"]), (keys[:, 1, :], dram["L0_ffn_sub_key1"]),
                                 (down[:], dram["L0_ffn_expert_down"]), (up[:], dram["L0_ffn_expert_up"]),
                                 (blocks[:], dram["block_mask"])]
                        for dst, src in pairs:
                            sp.dma_start(dst, src).then_inc(sem["loaded"], 16)

                    @block.vector
                    def _(dve):
                        step = Steps(dve, sem["vector_step"])
                        heads = lambda t: t[:].rearrange("p (h r) -> p h r", h=QH)
                        over_h = lambda t: t[:].unsqueeze(1).broadcast_to([128, QH, QD])
                        nc.vector.memset(cand[:], PAD)
                        step(nc.vector.tensor_scalar(gram[:], gram[:], 1.0 / (B * S), None, ALU.mult))
                        nc.vector.tensor_scalar(mean_h[:], ones[:], gram[:, D:D + 1], None, ALU.mult).then_inc(sem["x_ready"], 1)
                        dve.wait_ge(sem["loaded"], 16 * 9)
                        dve.wait_ge(sem["q_done"], 1)
                        step(nc.vector.tensor_copy(mean_q[:], ps[:, 1, 0:NQ]))
                        nc.vector.tensor_tensor(prod[:], ps[:, 0, 0:NQ], wq[:], ALU.mult).then_inc(sem["upd_ready"], 1)
                        dve.wait_ge(sem["upd_done"], 1)
                        step(nc.vector.tensor_tensor(var_q[:], mean_q[:], mean_q[:], ALU.mult))
                        step(nc.vector.tensor_tensor(var_q[:], ps[:, 2, 0:NQ], var_q[:], ALU.subtract))
                        step(nc.vector.tensor_tensor(mean_q[:], mean_q[:], bq[:], ALU.add))
                        step(nc.vector.tensor_reduce(m_r[:], mean_q[:].rearrange("p (h r) -> p r h", h=QH), AX.X, ALU.add))
                        step(nc.vector.tensor_scalar(m_r[:], m_r[:], 1.0 / QH, None, ALU.mult))
                        step(nc.vector.tensor_tensor(heads(prod), heads(mean_q), over_h(m_r), ALU.subtract))
                        step(nc.vector.tensor_tensor(prod[:], prod[:], prod[:], ALU.mult))
                        step(nc.vector.tensor_tensor(var_q[:], var_q[:], prod[:], ALU.add))
                        step(nc.vector.tensor_reduce(v_r[:], var_q[:].rearrange("p (h r) -> p r h", h=QH), AX.X, ALU.add))
                        step(nc.vector.tensor_scalar(v_r[:], v_r[:], 1.0 / QH, 1e-5, ALU.mult, ALU.add))
                        step(nc.vector.tensor_tensor(ksq[:], keys[:], keys[:], ALU.mult))
                        step(nc.vector.tensor_reduce(kn2[:], ksq[:], AX.X, ALU.add))
                        nc.vector.tensor_scalar(kn2[:], kn2[:], 1e-24, None, ALU.max).then_inc(sem["var_ready"], 1)
                        dve.wait_ge(sem["rstd_ready"], 2)
                        step(nc.vector.tensor_tensor(a_r[:], a_r[:], gamma[:], ALU.mult))
                        step(nc.vector.tensor_tensor(m_r[:], m_r[:], a_r[:], ALU.mult))
                        step(nc.vector.tensor_tensor(m_r[:], beta[:], m_r[:], ALU.subtract))
                        step(nc.vector.tensor_tensor(heads(wq), heads(wq), over_h(a_r), ALU.mult))
                        step(nc.vector.tensor_tensor(heads(bq), heads(bq), over_h(a_r), ALU.mult))
                        step(nc.vector.tensor_tensor(heads(bq), heads(bq), over_h(m_r), ALU.add))
                        step(nc.vector.tensor_tensor(keys[:], keys[:], kn2[:].unsqueeze(2).broadcast_to([KEYS, 2, HALF]), ALU.mult))
                        nc.vector.tensor_copy(keys4[:], keys[:].rearrange("p a r -> p (a r)").unsqueeze(1).broadcast_to([KEYS, 4, QD])).then_inc(sem["z_ready"], 1)
                        dve.wait_ge(sem["zT_done"], 1)
                        step(nc.vector.tensor_copy(keysT[:], ps[:, 3, 0:KEYS]))
                        nc.vector.tensor_copy(wT[:], ps[:, 4, :])
                        nc.vector.tensor_tensor(kblk[:], keysT[:].unsqueeze(1).broadcast_to([128, 8, KEYS]),
                                                blocks[:].unsqueeze(2).broadcast_to([128, 8, KEYS]), ALU.mult).then_inc(sem["table_ready"], 1)
                        dve.wait_ge(sem["k_done"], 1)
                        nc.vector.tensor_copy(wkey[:], ps[:, 5, :])
                        nc.vector.tensor_copy(bkey[:], ps[0:1, 6, :])

                    @block.gpsimd
                    def _(pool):
                        pool.wait_ge(sem["var_ready"], 1)
                        nc.gpsimd.tensor_tensor(a_r[:], v_r[:], neghalf[:, 0:QD], ALU.pow).then_inc(sem["rstd_ready"], 1)
                        nc.gpsimd.tensor_tensor(kn2[:], kn2[:], neghalf[0:KEYS, 0:2], ALU.pow).then_inc(sem["rstd_ready"], 1)

                    @block.tensor
                    def _(pe):
                        pe.wait_ge(sem["loaded"], 16 * 9)
                        pe.wait_ge(sem["x_ready"], 1)
                        nc.tensor.matmul(ps[:, 0, 0:NQ], gram[:, 0:D], wq[:], start=True, stop=True)
                        nc.tensor.matmul(ps[:, 1, 0:NQ], mean_h[:], wq[:], start=True, stop=True).then_inc(sem["q_done"], 1)
                        pe.wait_ge(sem["upd_ready"], 1)
                        nc.tensor.matmul(ps[:, 2, 0:NQ], ones[:], prod[:], start=True, stop=True).then_inc(sem["upd_done"], 1)
                        pe.wait_ge(sem["z_ready"], 1)
                        nc.tensor.transpose(ps[:, 3, 0:KEYS], keys4[:].rearrange("p a r -> p (a r)"), ident[0:KEYS, 0:KEYS])
                        for c in range(2):
                            nc.tensor.transpose(ps[:, 4, c * 128:(c + 1) * 128], wq[:, c * 128:(c + 1) * 128], ident[:])
                            last = nc.tensor.transpose(ps[:, 4, NQ + c * 128:NQ + (c + 1) * 128], bq[:, c * 128:(c + 1) * 128], ident[:])
                        last.then_inc(sem["zT_done"], 1)
                        pe.wait_ge(sem["table_ready"], 1)
                        kb = kblk[:].rearrange("p a k -> p (a k)")
                        for c in range(2):
                            nc.tensor.matmul(ps[:, 5, c * NQ:(c + 1) * NQ], wT[:, c * 128:(c + 1) * 128], kb, start=True, stop=True)
                            last = nc.tensor.matmul(ps[:, 6, c * NQ:(c + 1) * NQ], wT[:, NQ + c * 128:NQ + (c + 1) * 128], kb, start=True, stop=True)
                        last.then_inc(sem["k_done"], 1)
                rest()

                with nc.Fori(0, NG) as g:
                    with nc.Block() as block:
                        @block.vector
                        def _(dve):
                            step = Steps(dve, sem["vector_step"])
                            ln_vector(dve, step, 0, lambda u: x_all[:, g * U + u, :]).then_inc(sem["z_ready"], 1)

                            def select(u):
                                b = u % 2
                                dve.wait_ge(sem["q_read"], u + 1)
                                step(nc.vector.tensor_reduce(n2[:, b, :], sq[:, b, :].rearrange("p (c r) -> p c r", r=HALF), AX.X, ALU.add))
                                nc.vector.tensor_scalar(n2[:, b, :], n2[:, b, :], 1e-24, None, ALU.max).then_inc(sem["var_ready"], 1)
                                dve.wait_ge(sem["rstd_ready"], u + 2)
                                nc.vector.tensor_tensor(cand[:, b, :, 0:KEYS], ps[:, b, :].rearrange("p (c k) -> p c k", k=KEYS),
                                                        rn[:, b, :].unsqueeze(2).broadcast_to([128, CELLS, KEYS]), ALU.mult).then_inc(sem["cand_ready"], 1)
                                dve.wait_ge(sem["cand_ready"], u + 1)
                                for c in range(CELLS):
                                    last = nc.vector.max(best[:, b, c, :], cand[:, b, c, 0:KEYS])
                                step(last)
                                step(nc.vector.memset(best[:, b, :, TOP:8], PAD))
                                for c in range(CELLS):
                                    last = nc.vector.match_replace(left[:, c, :], best[:, b, c, :], cand[:, b, c, :], TAKEN)
                                step(last)
                                dve.wait_ge(sem["exp_done"], u + 1)
                                step(nc.vector.scalar_tensor_tensor(out=ex[:, b], in0=left[:, :, 0:KEYS], scalar=0.5 * TAKEN, in1=ex[:, b],
                                                                    op0=ALU.is_lt, op1=ALU.mult))
                                step(nc.vector.tensor_reduce(z[:], ex[:, b], AX.X, ALU.add))
                                step(nc.vector.reciprocal(z[:], z[:]))
                                nc.vector.tensor_tensor(ex[:, b], ex[:, b], z[:].unsqueeze(2).broadcast_to([128, CELLS, KEYS]),
                                                        ALU.mult).then_inc(sem["shifted"], 1)
                                dve.wait_ge(sem["shifted"], u + 1)
                                first = ex[:, b].rearrange("p (h a) k -> p h a k", a=2)[:, :, 0, 4:KEYS]
                                nc.vector.tensor_reduce(tail[:, b:b + 1], first, AX.XY, ALU.add)

                            def weigh(u):
                                b = u % 2
                                dve.wait_ge(sem["outer_ready"], u + 1)
                                step(nc.vector.tensor_reduce(coef[:], outer[:, b].rearrange("p h i k -> p (i k) h"), AX.X, ALU.add))
                                step(nc.vector.tensor_tensor(coef[:, E - 1:E], coef[:, E - 1:E], tail[:, b:b + 1], ALU.add))
                                if u == 0:
                                    dve.wait_ge(sem["hid_ready"], 1)
                                nc.vector.tensor_tensor(xs[:, u, :], act_g[:, u, :], coef[:], ALU.mult).then_inc(sem["expert_ready"], 1)
                                dve.wait_ge(sem["expert_ready"], u + 1)

                            for u in range(U):
                                select(u)
                                if u:
                                    weigh(u - 1)
                            weigh(U - 1)
                            dve.wait_ge(sem["mix_done"], 1)
                            xg = x_all[:, bass.ds(g * U, U), :]
                            nc.vector.tensor_tensor(xg, xg, per(6), ALU.add)

                        @block.gpsimd
                        def _(pool):
                            ln_pool(pool, 0)
                            for u in range(U):
                                b = u % 2
                                pool.wait_ge(sem["var_ready"], u + 2)
                                if u >= 2:
                                    pool.wait_ge(sem["cand_ready"], u - 1)
                                nc.gpsimd.tensor_tensor(rn[:, b, :], n2[:, b, :], neghalf[:, 0:CELLS], ALU.pow).then_inc(sem["rstd_ready"], 1)
                                pool.wait_ge(sem["shifted"], u + 1)
                                if u >= 2:
                                    pool.wait_ge(sem["expert_ready"], u - 1)
                                halves = ex[:, b].rearrange("p (h a) k -> p h a k", a=2)
                                for i in range(4):
                                    last = nc.gpsimd.tensor_tensor(outer[:, b, :, i, :], halves[:, :, 0, i:i + 1].broadcast_to([128, QH, KEYS]),
                                                                   halves[:, :, 1, :], ALU.mult)
                                last.then_inc(sem["outer_ready"], 1)

                        @block.scalar
                        def _(act):
                            act.wait_ge(sem["zT_done"], 1)
                            nc.scalar.activation(xnT[:], ps[:, 4, :], ACT.Copy).then_inc(sem["xnT_ready"], 1)
                            act.wait_ge(sem["hid_done"], 1)
                            nc.scalar.activation(act_g[:], per(7), ACT.Gelu).then_inc(sem["hid_ready"], 1)
                            for u in range(U):
                                b = u % 2
                                act.wait_ge(sem["scores_done"], u + 1)
                                nc.scalar.activation(sq[:, b, :], ps[:, 2 + b, 0:NQ], ACT.Square).then_inc(sem["q_read"], 1)
                                act.wait_ge(sem["cand_ready"], u + 1)
                                if u >= 2:
                                    act.wait_ge(sem["outer_ready"], u - 1)
                                nc.scalar.activation(ex[:, b], cand[:, b, :, 0:KEYS], ACT.Exp).then_inc(sem["exp_done"], 1)
                            act.wait_ge(sem["o_turned"], 1)
                            nc.scalar.activation(yT[:], ps[:, 5, :], ACT.Copy).then_inc(sem["oT_ready"], 1)

                        @block.tensor
                        def _(pe):
                            turn_rows(pe, 0, bank=4)
                            pe.wait_ge(sem["xnT_ready"], 1)
                            for u in range(U):
                                last = nc.tensor.matmul(per(7)[:, u, :], xnT[:, u * S:(u + 1) * S], down[:], start=True, stop=True)
                            last.then_inc(sem["hid_done"], 1)
                            for u in range(U):
                                b, z_u = u % 2, xnT[:, u * S:(u + 1) * S]
                                if u >= 2:
                                    pe.wait_ge(sem["cand_ready"], u - 1)
                                    pe.wait_ge(sem["q_read"], u - 1)
                                nc.tensor.matmul(ps[:, b, :], z_u, wkey[:], start=True, stop=False)
                                nc.tensor.matmul(ps[:, b, :], ones[0:1, :], bkey[:], start=False, stop=True)
                                nc.tensor.matmul(ps[:, 2 + b, 0:NQ], z_u, wq[:], start=True, stop=False)
                                nc.tensor.matmul(ps[:, 2 + b, 0:NQ], ones[0:1, :], bq[0:1, :], start=False, stop=True).then_inc(sem["scores_done"], 1)
                            pe.wait_ge(sem["expert_ready"], U)
                            for u in range(U):
                                last = nc.tensor.transpose(ps[:, 5, u * S:(u + 1) * S], xs[:, u, :], ident[:])
                            last.then_inc(sem["o_turned"], 1)
                            pe.wait_ge(sem["oT_ready"], 1)
                            for u in range(U):
                                last = nc.tensor.matmul(per(6)[:, u, :], yT[:, u * S:(u + 1) * S], up[:], start=True, stop=True)
                            last.then_inc(sem["mix_done"], 1)
                    rest()

        if "C" in SECTIONS:
            stage_product_keys()

        def wait_all(eng, names, value):
            for n in names:
                eng.wait_ge(sem[n], value)

        def job_bank(pe, k):
            if k >= 4:
                pe.wait_ge(sem["q_read" if k % 2 == 0 else "k_read"], (k - 4) // 2 + 1)
            return k % 4

        def jobs_read(pe, n):
            pe.wait_ge(sem["q_read"], n // 2)
            pe.wait_ge(sem["k_read"], n // 2)

        def copy_job(eng, k, dst, src):
            eng.wait_ge(sem["proj_done"], k + 1)
            if k % 2 == 0:
                nc.scalar.activation(dst, src, ACT.Copy).then_inc(sem["q_read"], 1)
            else:
                nc.vector.tensor_copy(dst, src).then_inc(sem["k_read"], 1)

        def stage_block():
            W, INNER, NB = D // 2, NH * D // 2, NH // 2
            with ExitStack() as st:
                wa = {}
                for a in (1, 2):
                    for n in ("wq", "wk", "wv"):
                        wa[a, n] = sb(f"D_{n}{a}", [D, INNER], scope=st)
                    wa[a, "wo"] = sb(f"D_wo{a}", [D, NB, D], scope=st)
                    wa[a, "bo"] = sb(f"D_bo{a}", [1, D], scope=st)
                w1 = sb("D_w1", [D, 2 * FFN], scope=st)
                b1 = sb("D_b1", [D, 8], scope=st)
                w2 = sb("D_w2", [D, 4, D], scope=st)
                b2 = sb("D_b2", [1, D], scope=st)
                nw = sb("D_nw", [D, 3, 2 * D], scope=st)
                nb = sb("D_nb", [D, 3, 2], scope=st)
                gb = sb("D_gb", [D, 3, 2, B], scope=st)
                gb4 = sb("D_gb4", [D, 3, 2, U], scope=st)
                qz = sb("D_qz", [D, NH, U * S], scope=st)
                kT = sb("D_kT", [D, NB, U * S], scope=st)
                vv = sb("D_vv", [S, U * NH * (W + 1) + S - W - 1], scope=st)
                vh = vv[:, 0:U * NH * (W + 1)].rearrange("p (u h d) -> p u h d", u=U, d=W + 1)
                o_all = sb("D_o", [S, U, INNER], scope=st)
                loads = [(w1[:], dram["L1_xcond_ff_w1"]),
                         (b1[:], dram["L1_xcond_ff_b1"].rearrange("(c p) -> p c", p=D)),
                         (w2[:], dram["L1_xcond_ff_w2"].rearrange("(c p) n -> p c n", p=D)),
                         (b2[:], dram["L1_xcond_ff_b2"].unsqueeze(0))]
                for a in (1, 2):
                    for n in ("wq", "wk", "wv"):
                        loads.append((wa[a, n][:], dram[f"L1_xcond_attn{a}_{n}"]))
                    loads.append((wa[a, "wo"][:], dram[f"L1_xcond_attn{a}_wo"].rearrange("(c p) n -> p c n", p=D)))
                    loads.append((wa[a, "bo"][:], dram[f"L1_xcond_attn{a}_bo"].unsqueeze(0)))
                for n in range(3):
                    loads.append((nw[:, n, :], dram[f"L1_xcond_norm{n + 1}_w"]))
                    loads.append((nb[:, n, :], dram[f"L1_xcond_norm{n + 1}_b"].rearrange("(c p) -> p c", p=D)))

                with nc.Block() as block:
                    @block.sync
                    def _(sp):
                        for dst, src in loads:
                            sp.dma_start(dst, src, allow_slow_non_contiguous=True).then_inc(sem["loaded"], 16)

                    @block.tensor
                    def _(pe):
                        pe.wait_ge(sem["loaded"], 16 * len(loads))
                        for n in range(3):
                            for c in range(2):
                                last = nc.tensor.matmul(ps[:, 0, (2 * n + c) * B:(2 * n + c + 1) * B], nw[:, n, c * D:(c + 1) * D],
                                                        condT[:], start=True, stop=True)
                        last.then_inc(sem["proj_done"], 1)

                    @block.vector
                    def _(dve):
                        step = Steps(dve, sem["vector_step"])
                        nc.vector.memset(vv[:], 1.0)
                        nc.vector.memset(qz[:], 0.0)
                        dve.wait_ge(sem["loaded"], 16 * len(loads))
                        step(nc.vector.tensor_scalar(nb[:, :, 0], nb[:, :, 0], 1.0, None, ALU.add))
                        dve.wait_ge(sem["proj_done"], 1)
                        nc.vector.tensor_tensor(gb[:].rearrange("p n c b -> p (n c) b"),
                                                ps[:, 0, 0:6 * B].rearrange("p (n b) -> p n b", b=B),
                                                nb[:].rearrange("p n c -> p (n c)").unsqueeze(2).broadcast_to([D, 6, B]), ALU.add)
                rest()

                ctxg = sb("D_ctxg", [D, UC], scope=st)
                with nc.Fori(0, NG) as g:
                    with nc.Block() as block:
                        @block.tensor
                        def _(pe):
                            for a in (1, 2):
                                k0 = 32 * (a - 1)
                                keys = S if a == 1 else CL
                                src = xnT if a == 1 else ctxg
                                turn_rows(pe, a - 1, bank=TURN)
                                pe.wait_ge(sem["xnT_ready"], a)
                                for c in range(NB):
                                    bank = job_bank(pe, k0 + c)
                                    nc.tensor.matmul(ps[:, bank, :], wa[a, "wq"][:, c * D:(c + 1) * D], xnT[:],
                                                     start=True, stop=True).then_inc(sem["proj_done"], 1)
                                for c in range(NB):
                                    bank = job_bank(pe, k0 + NB + c)
                                    nc.tensor.matmul(ps[:, bank, 0:U * keys], wa[a, "wk"][:, c * D:(c + 1) * D], src[:, 0:U * keys],
                                                     start=True, stop=True).then_inc(sem["proj_done"], 1)
                                for c in range(2 * U):
                                    bank = job_bank(pe, k0 + 2 * NB + c)
                                    nc.tensor.matmul(ps[0:keys, bank, :], src[:, (c // 2) * keys:(c // 2 + 1) * keys],
                                                     wa[a, "wv"][:, (c % 2) * 512:(c % 2 + 1) * 512],
                                                     start=True, stop=True).then_inc(sem["proj_done"], 1)
                                jobs_read(pe, k0 + 24)
                                attn_tensor(pe, a - 1, keys,
                                            lambda h, u: qz[:, h, u * S:(u + 1) * S],
                                            lambda h, u: kT[:, h // 2, u * keys:u * keys + S],
                                            lambda h, u: vv[0:keys, (u * NH + h) * (W + 1):(u * NH + h) * (W + 1) + S])
                                pe.wait_ge(sem["o_normed"], NU * a)
                                for c in range(2 * U):
                                    bank = job_bank(pe, k0 + 24 + c)
                                    for i in range(4):
                                        last = nc.tensor.transpose(ps[:, bank, i * S:(i + 1) * S],
                                                                   o_all[:, c // 2, ((c % 2) * 4 + i) * D:((c % 2) * 4 + i + 1) * D], ident[:])
                                    last.then_inc(sem["proj_done"], 1)
                                jobs_read(pe, k0 + 32)
                                for u in range(U):
                                    for c in range(NB):
                                        nc.tensor.matmul(per(OUT)[:, u, :], kT[:, c, u * S:(u + 1) * S], wa[a, "wo"][:, c, :],
                                                         start=(c == 0), stop=False)
                                    last = nc.tensor.matmul(per(OUT)[:, u, :], ones[0:1, :], wa[a, "bo"][:], start=False, stop=True)
                                last.then_inc(sem["mix_done"], 1)
                            turn_rows(pe, 2, bank=TURN)
                            pe.wait_ge(sem["xnT_ready"], 3)
                            for j in range(4):
                                for c, k in ((4 + j, 64 + 2 * j), (j, 65 + 2 * j)):
                                    bank = job_bank(pe, k)
                                    nc.tensor.matmul(ps[:, bank, :], w1[:, c * D:(c + 1) * D], xnT[:],
                                                     start=True, stop=True).then_inc(sem["proj_done"], 1)
                            jobs_read(pe, 72)
                            for u in range(U):
                                for c in range(4):
                                    nc.tensor.matmul(per(OUT)[:, u, :], kT[:, 4 + c, u * S:(u + 1) * S], w2[:, c, :],
                                                     start=(c == 0), stop=False)
                                last = nc.tensor.matmul(per(OUT)[:, u, :], ones[0:1, :], b2[:], start=False, stop=True)
                            last.then_inc(sem["mix_done"], 1)

                        def empty(eng, k0, a, odd):
                            keys = S if a == 1 else CL
                            for c in range(odd, NB, 2):
                                eng.wait_ge(sem["proj_done"], k0 + c + 1)
                                for i in range(2):
                                    dst, src = qz[W * i:W * (i + 1), 2 * c + i, :], ps[W * i:W * (i + 1), (k0 + c) % 4, :]
                                    if odd:
                                        last = nc.vector.tensor_copy(dst, src)
                                    else:
                                        last = nc.scalar.activation(dst, src, ACT.Copy)
                                last.then_inc(sem["k_read" if odd else "q_read"], 1)
                            for c in range(odd, NB, 2):
                                copy_job(eng, k0 + NB + c, kT[:, c, 0:U * keys], ps[:, (k0 + NB + c) % 4, 0:U * keys])
                            for c in range(odd, 2 * U, 2):
                                copy_job(eng, k0 + 2 * NB + c, vh[0:keys, c // 2, (c % 2) * 8:(c % 2 + 1) * 8, 0:W],
                                         ps[0:keys, (k0 + 2 * NB + c) % 4, :].rearrange("p (h d) -> p h d", d=W))

                        def empty_turned(eng, k0, odd):
                            for c in range(odd, 2 * U, 2):
                                u, half = c // 2, c % 2
                                copy_job(eng, k0 + 24 + c, kT[:, 4 * half:4 * half + 4, u * S:(u + 1) * S],
                                         ps[:, (k0 + 24 + c) % 4, :].rearrange("p (c t) -> p c t", c=4))

                        @block.scalar
                        def _(act):
                            for a in (1, 2, 3):
                                act.wait_ge(sem["zT_done"], a)
                                if a == 1:
                                    act.wait_ge(sem["table_ready"], 1)
                                for u in range(U):
                                    last = nc.scalar.activation(xnT[:, u * S:(u + 1) * S], ps[:, TURN, u * S:(u + 1) * S], ACT.Identity,
                                                                bias=gb4[:, a - 1, 1, u:u + 1], scale=gb4[:, a - 1, 0, u:u + 1])
                                last.then_inc(sem["xnT_ready"], 1)
                                if a < 3:
                                    k0 = 32 * (a - 1)
                                    empty(act, k0, a, 0)
                                    attn_scalar(act, a - 1, S if a == 1 else CL, W ** -0.5)
                                    empty_turned(act, k0, 0)
                            for j in range(4):
                                act.wait_ge(sem["proj_done"], 64 + 2 * j + 1)
                                nc.scalar.activation(kT[:, j, :], ps[:, (64 + 2 * j) % 4, :], ACT.Gelu, bias=b1[:, 4 + j:5 + j]).then_inc(sem["q_read"], 1)

                        @block.vector
                        def _(dve):
                            step = Steps(dve, sem["vector_step"])
                            nc.vector.tensor_copy(ctxg[:], ctxT[:, bass.ds(g * UC, UC)])
                            nc.vector.tensor_copy(gb4[:].rearrange("p n c u -> p (n c) u"),
                                                  gb[:].rearrange("p n c b -> p (n c) b")[:, :, bass.ds(g * U, U)]).then_inc(sem["table_ready"], 1)
                            step(ln_vector(dve, step, 0, lambda u: x_all[:, g * U + u, :], lambda u: xs[:, u, :]))
                            for a in (1, 2):
                                k0 = 32 * (a - 1)
                                ln_vector(dve, step, a, lambda u: xs[:, u, :]).then_inc(sem["z_ready"], 1)
                                empty(dve, k0, a, 1)
                                attn_vector(dve, step, a - 1, S if a == 1 else CL, lambda u: o_all[:, u, :])
                                empty_turned(dve, k0, 1)
                                dve.wait_ge(sem["mix_done"], a)
                                step(nc.vector.tensor_tensor(xs[:], xs[:], per(OUT), ALU.add))
                            ln_vector(dve, step, 3, lambda u: xs[:, u, :]).then_inc(sem["z_ready"], 1)
                            for j in range(4):
                                dve.wait_ge(sem["q_read"], 32 + j + 1)
                                dve.wait_ge(sem["proj_done"], 65 + 2 * j + 1)
                                nc.vector.scalar_tensor_tensor(out=kT[:, 4 + j, :], in0=ps[:, (65 + 2 * j) % 4, :], scalar=b1[:, j:j + 1],
                                                               in1=kT[:, j, :], op0=ALU.add, op1=ALU.mult).then_inc(sem["k_read"], 1)
                            dve.wait_ge(sem["mix_done"], 3)
                            step(nc.vector.tensor_tensor(xs[:], xs[:], per(OUT), ALU.add))
                            xg = x_all[:, bass.ds(g * U, U), :]
                            nc.vector.tensor_tensor(xg, xg, xs[:], ALU.add)

                        @block.gpsimd
                        def _(pool):
                            for r in range(4):
                                ln_pool(pool, r)
                    rest()

        if "D" in SECTIONS:
            stage_block()

        vrest = sb("vrest", [S, U, D])
        PAD, TAKEN = 3e38, -3e38
        gates = sb("gates", [128, U, EXPERTS + 6])
        gbest = sb("gbest", [128, U, 8])
        gleft = sb("gleft", [128, U, EXPERTS + 6])
        gsum = sb("gsum", [128, U])
        chosen = sb("chosen", [128, U, EXPERTS])

        def route_vector(dve, step, bank, weighted):
            g8 = gates[:, :, 0:EXPERTS]
            over = lambda t: t[:].unsqueeze(2).broadcast_to([128, U, EXPERTS])
            dve.wait_ge(sem["gate_done"], 1)
            step(nc.vector.tensor_reduce(gsum[:], per(bank, EXPERTS), AX.X, ALU.max))
            nc.vector.tensor_tensor(g8, per(bank, EXPERTS), over(gsum), ALU.subtract).then_inc(sem["cand_ready"], 1)
            dve.wait_ge(sem["gate_ready"], 1)
            step(nc.vector.tensor_reduce(gsum[:], g8, AX.X, ALU.add))
            step(nc.vector.reciprocal(gsum[:], gsum[:]))
            step(nc.vector.tensor_tensor(g8, g8, over(gsum), ALU.mult))
            for u in range(U):
                last = nc.vector.max(gbest[:, u, :], gates[:, u, 0:EXPERTS])
            step(last)
            step(nc.vector.memset(gbest[:, :, 2:8], PAD))
            for u in range(U):
                last = nc.vector.match_replace(gleft[:, u, :], gbest[:, u, :], gates[:, u, :], TAKEN)
            step(last)
            if weighted:
                step(nc.vector.scalar_tensor_tensor(out=chosen[:], in0=gleft[:, :, 0:EXPERTS], scalar=0.5 * TAKEN, in1=g8,
                                                    op0=ALU.is_lt, op1=ALU.mult))
            else:
                step(nc.vector.tensor_scalar(chosen[:], gleft[:, :, 0:EXPERTS], 0.5 * TAKEN, None, ALU.is_lt))

        def route_scalar(act):
            act.wait_ge(sem["cand_ready"], 1)
            nc.scalar.activation(gates[:, :, 0:EXPERTS], gates[:, :, 0:EXPERTS], ACT.Exp).then_inc(sem["gate_ready"], 1)

        def stage_attn_experts():
            with ExitStack() as st:
                wqkv = sb("E_wqkv", [D, 3 * D], scope=st)
                bqk = sb("E_bqk", [D, 2], scope=st)
                bv = sb("E_bv", [1, D], scope=st)
                wg = sb("E_wg", [D, EXPERTS], scope=st)
                bg = sb("E_bg", [1, EXPERTS], scope=st)
                we = sb("E_we", [D, EXPERTS * D], scope=st)
                be = sb("E_be", [1, EXPERTS * D], scope=st)
                qr = sb("E_qr", [D, U * S], scope=st)
                kr = sb("E_kr", [D, U * S], scope=st)
                qm = sb("E_qm", [D, NH, U * S], scope=st)
                heads = sb("E_heads", [D, NH], scope=st)
                vp = sb("E_vp", [S, U, NH, 3 * HP], BF16, scope=st)
                o8 = sb("E_o8", [S, U, D], scope=st)
                moe = sb("E_moe", [S, U, D], scope=st)
                loads = [(heads[:], dram["head_mask"]), (wqkv[:], dram["L1_ffn_W_qkv"]),
                         (bqk[:], dram["L1_ffn_b_qkv"][0:2 * D].rearrange("(c p) -> p c", p=D)),
                         (bv[:], dram["L1_ffn_b_qkv"][2 * D:3 * D].unsqueeze(0)),
                         (wg[:], dram["L1_ffn_W_gate"]), (bg[:], dram["L1_ffn_b_gate"].unsqueeze(0)),
                         (we[:].rearrange("d (e f) -> d e f", f=D), dram["L1_ffn_W_experts"].rearrange("e d f -> d e f")),
                         (be[:], dram["L1_ffn_b_experts"].rearrange("e f -> (e f)").unsqueeze(0))]
                with nc.Block() as block:
                    @block.sync
                    def _(sp):
                        for dst, src in loads:
                            sp.dma_start(dst, src, allow_slow_non_contiguous=True).then_inc(sem["loaded"], 16)
                        sp.wait_ge(sem["loaded"], 16 * len(loads))

                    @block.vector
                    def _(dve):
                        Steps(dve, sem["vector_step"])(nc.vector.memset(vp[:], 0.0))
                        nc.vector.memset(vp[:, :, :, HD:HP], 1.0)
                        nc.vector.memset(gates[:], PAD)
                rest()

                with nc.Fori(0, NG) as g:
                    with nc.Block() as block:
                        @block.tensor
                        def _(pe):
                            turn_rows(pe, 0, bank=TURN)
                            pe.wait_ge(sem["xnT_ready"], 1)
                            for c in range(2):
                                nc.tensor.matmul(ps[:, TURN + 1 + c, :], wqkv[:, c * D:(c + 1) * D], xnT[:],
                                                 start=True, stop=True).then_inc(sem["q_done"], 1)
                            for u in range(U):
                                nc.tensor.matmul(per(7)[:, u, :], xnT[:, u * S:(u + 1) * S], wqkv[:, 2 * D:3 * D], start=True, stop=False)
                                last = nc.tensor.matmul(per(7)[:, u, :], ones[0:1, :], bv[:], start=False, stop=True)
                            last.then_inc(sem["v_done"], 1)
                            for u in range(U):
                                nc.tensor.matmul(per(TURN, EXPERTS)[:, u, :], xnT[:, u * S:(u + 1) * S], wg[:], start=True, stop=False)
                                last = nc.tensor.matmul(per(TURN, EXPERTS)[:, u, :], ones[0:1, :], bg[:], start=False, stop=True)
                            last.then_inc(sem["gate_done"], 1)
                            for u in range(U):
                                if u >= 2:
                                    pe.wait_ge(sem["expert_ready"], u - 1)
                                for c in range(2):
                                    bank = 2 * (u % 2) + c
                                    nc.tensor.matmul(ps[:, bank, :], xnT[:, u * S:(u + 1) * S], we[:, c * 512:(c + 1) * 512], start=True, stop=False)
                                    last = nc.tensor.matmul(ps[:, bank, :], ones[0:1, :], be[:, c * 512:(c + 1) * 512], start=False, stop=True)
                                last.then_inc(sem["expert_done"], 1)
                            pe.wait_ge(sem["expert_ready"], U)
                            pe.wait_ge(sem["q_read"], 2)
                            small_tensor(pe, 0, S, qm, kr, vp)

                        @block.scalar
                        def _(act):
                            act.wait_ge(sem["zT_done"], 1)
                            nc.scalar.activation(xnT[:], ps[:, TURN, :], ACT.Copy).then_inc(sem["xnT_ready"], 1)
                            for c, t in enumerate((qr, kr)):
                                act.wait_ge(sem["q_done"], c + 1)
                                nc.scalar.activation(t[:], ps[:, TURN + 1 + c, :], ACT.Identity, bias=bqk[:, c:c + 1]).then_inc(sem["q_read"], 1)
                            act.wait_ge(sem["q_read"], 1)
                            for pair in range(2):
                                mask_queries("scalar", pair, qr, qm, heads)
                            route_scalar(act)
                            small_scalar(act, 0, S)

                        @block.vector
                        def _(dve):
                            step = Steps(dve, sem["vector_step"])
                            ln_vector(dve, step, 0, lambda u: x_all[:, g * U + u, :]).then_inc(sem["z_ready"], 1)
                            dve.wait_ge(sem["q_read"], 1)
                            for pair in range(2):
                                mask_queries("vector", pair, qr, qm, heads)
                            dve.wait_ge(sem["v_done"], 1)
                            split_values(step, 7, vp, S).then_inc(sem["v_read"], 1)
                            route_vector(dve, step, TURN, True)
                            for u in range(U):
                                dve.wait_ge(sem["expert_done"], u + 1)
                                prod = e[:, u % 2, :].rearrange("p (e f) -> p e f", f=D)
                                nc.vector.tensor_tensor(prod, ps[:, 2 * (u % 2):2 * (u % 2) + 2, :].rearrange("p b (e f) -> p (b e) f", f=D),
                                                        chosen[:, u, :].unsqueeze(2).broadcast_to([128, EXPERTS, D]), ALU.mult).then_inc(sem["expert_ready"], 1)
                                dve.wait_ge(sem["expert_ready"], u + 1)
                                last = nc.vector.tensor_reduce(moe[:, u, :], prod.rearrange("p e f -> p f e"), AX.X, ALU.add)
                            step(last)
                            small_vector(dve, step, 0, S, lambda u: o8[:, u, :])
                            dve.wait_ge(sem["o_normed"], NU)
                            step(nc.vector.tensor_tensor(o8[:], o8[:], moe[:], ALU.add))
                            xg = x_all[:, bass.ds(g * U, U), :]
                            nc.vector.tensor_tensor(xg, xg, o8[:], ALU.add)

                        @block.gpsimd
                        def _(pool):
                            ln_pool(pool, 0)
                    rest()

        if "E" in SECTIONS:
            stage_attn_experts()

        def stage_gru():
            CH, CB = 2, B // 2
            RUN = 16
            with ExitStack() as st:
                wT = sb("F_wT", [D, D], scope=st)
                gate_w = {n: sb("F_" + n, [D, 3 * D], scope=st) for n in ("x", "c", "h")}
                gate_p = {n: sb("F_p" + n, [D, 3, 3 * D], BF16, scope=st) for n in ("x", "c", "h")}
                bias = sb("F_bias", [D, 3], scope=st)
                encW = sb("F_encW", [D, 3, B, 128], BF16, scope=st)
                ctxp = sb("F_ctxp", [CL, 3, B, D], BF16, scope=st)
                decT = sb("F_decT", [D, 3, S, B], BF16, scope=st)
                spare = sb("F_spare", [128, 2, U * D], scope=st)
                gru = sb("F_gru", [D, S, B], scope=st)
                xloc = sb("F_xloc", [D, 3, RUN, B], BF16, scope=st)
                hp = sb("F_hp", [D, B, 3], BF16, scope=st)
                hist = sb("F_hist", [D, RUN + 1, B], scope=st)
                sT = sb("F_sT", [CL, CH, CB], scope=st)
                nm = sb("F_nm", [CB, CH], scope=st)
                den = sb("F_den", [D, CH, CB], scope=st)
                keep = sb("F_keep", [D, CH, CB], scope=st)
                ones16 = sb("F_ones16", [128, 128], F16, scope=st)
                ex = sb("F_ex", [CB, CH, CL], scope=st)
                eT = sb("F_eT", [CL, CH, CB, 2], F16, scope=st)
                cv = sb("F_cv", [D, CH, CB], scope=st)
                cvp = sb("F_cvp", [D, CH, CB, 3], BF16, scope=st)
                left = sb("F_left", [D, CH, CB], scope=st)
                zt = sb("F_zt", [D, CH, CB], scope=st)
                rt = sb("F_rt", [D, CH, CB], scope=st)
                cand = sb("F_cand", [D, CH, CB], scope=st)
                t1 = sb("F_t1", [D, CH, CB], scope=st)
                loads = [(wT[:], dram["L2_xcond_W"]), (gate_w["x"][:], dram["L2_xcond_kernel"][0:D, :]),
                         (gate_w["c"][:], dram["L2_xcond_kernel"][D:2 * D, :]), (gate_w["h"][:], dram["L2_xcond_recurrent_kernel"]),
                         (bias[:], dram["L2_xcond_bias"].rearrange("(c p) -> p c", p=D))]
                SCALE = 1024.0
                PRODUCTS = [(0, 0), (0, 1), (0, 2), (1, 0), (1, 1), (2, 0)]

                def parts(step, made, src, part, rest_):
                    step(nc.vector.tensor_tensor(part(0), made[0], made[1], made[2]))
                    nc.vector.tensor_tensor(rest_, src, part(0), ALU.subtract)
                    step(nc.vector.tensor_tensor(part(1), src, part(0), ALU.subtract))
                    return nc.vector.tensor_tensor(part(2), rest_, part(1), ALU.subtract)

                with nc.Block() as block:
                    @block.sync
                    def _(sp):
                        for dst, src in loads:
                            sp.dma_start(dst, src, allow_slow_non_contiguous=True).then_inc(sem["loaded"], 16)

                    @block.vector
                    def _(dve):
                        step = Steps(dve, sem["vector_step"])
                        nc.vector.tensor_copy(hist[:, RUN, :], condT[:])
                        nc.vector.memset(encW[:], 0.0)
                        nc.vector.memset(ones16[:], 1.0)
                        step(split(step, condT[:], lambda i: hp[:, :, i], spare[:, 0, 0:B]))
                        dve.wait_ge(sem["loaded"], 16 * len(loads))
                        nc.vector.tensor_scalar(bias[:, 0:2], bias[:, 0:2], 0.5, None, ALU.mult)
                        for n in ("x", "c", "h"):
                            step(split(step, gate_w[n][:], lambda i: gate_p[n][:, i, :], spare[:, 0, 0:3 * D]))
                        for g in range(NG):
                            mine = slice(g * U, (g + 1) * U)
                            step(split(step, ctx_tm[:, mine, :], lambda i: ctxp[:, i, mine, :],
                                       spare[0:CL, 0, :].rearrange("p (u d) -> p u d", u=U)))
                            dve.wait_ge(sem["k_done"], g + 1)
                            step(split(step, per(g, CL), lambda i: encW[:, i, mine, 0:CL],
                                       spare[:, 0, 0:UC].rearrange("p (u k) -> p u k", u=U)))

                    @block.tensor
                    def _(pe):
                        pe.wait_ge(sem["loaded"], 16 * len(loads))
                        for g in range(NG):
                            nc.tensor.matmul(ps[:, g, 0:UC], wT[:], ctxT[:, g * UC:(g + 1) * UC], start=True, stop=True).then_inc(sem["k_done"], 1)
                rest()

                with nc.Fori(0, NG) as g:
                    with nc.Block() as block:
                        @block.vector
                        def _(dve):
                            step = Steps(dve, sem["vector_step"])
                            ln_vector(dve, step, 0, lambda u: x_all[:, g * U + u, :]).then_inc(sem["z_ready"], 1)
                            dve.wait_ge(sem["zT_done"], 1)
                            tok = per(0, S).rearrange("p u t -> p t u")
                            split(step, tok, lambda i: decT[:, i, :, bass.ds(g * U, U)],
                                  spare[:, 0, :].rearrange("p (t u) -> p t u", u=U))

                        @block.gpsimd
                        def _(pool):
                            ln_pool(pool, 0)

                        @block.tensor
                        def _(pe):
                            turn_rows(pe, 0)
                    rest()

                with nc.Fori(0, S // RUN) as n:
                    with nc.Block() as block:
                        mine = lambda c: slice(CB * c, CB * (c + 1))

                        def gate_bank(t, c):
                            return 4 * c + 3 - t % 2

                        def attended_bank(t, c):
                            return 4 * c + 2 + t % 2

                        @block.tensor
                        def _(pe):
                            def score(t, c):
                                k = CH * t + c
                                if t > 0:
                                    pe.wait_ge(sem["mix_added"], k - 1)
                                for j in range(CB):
                                    b = CB * c + j
                                    for i in range(3):
                                        last = nc.tensor.matmul(ps[:, 4 * c, 3 * j:3 * j + 3 - i], encW[:, i, b, :], hp[:, b, 0:3 - i],
                                                                start=(i == 0), stop=(i == 2), skip_group_check=True)
                                last.then_inc(sem["scores_done"], 1)

                            def of_token(t, c):
                                gate = lambda i: ps[:, gate_bank(t, c), i * CB:(i + 1) * CB]
                                if t > 0:
                                    pe.wait_ge(sem["o_normed"], CH * (t - 1) + c + 1)
                                for i in range(3):
                                    for a, b in PRODUCTS:
                                        nc.tensor.matmul(gate(i), gate_p["x"][:, a, i * D:(i + 1) * D], xloc[:, b, t, mine(c)],
                                                         start=(i == 0 and a + b == 0), stop=False, skip_group_check=True)

                            def of_state(t, c):
                                gate = lambda i: ps[:, gate_bank(t, c), i * CB:(i + 1) * CB]
                                for i in range(3):
                                    for a, b in PRODUCTS:
                                        nc.tensor.matmul(gate(i if i < 2 else 3), gate_p["h"][:, a, i * D:(i + 1) * D], hp[:, mine(c), b],
                                                         start=False, stop=(i == 2 and a == 2), skip_group_check=True)

                            def turn_scores(t, c):
                                pe.wait_ge(sem["k_read"], CH * t + c + 1)
                                nc.tensor.transpose(ps[0:CB, 4 * c + 1, 0:CL], sT[:, c, :], ident[0:CL, 0:CL]).then_inc(sem["turned"], 1)

                            def turn_weights(t, c):
                                pe.wait_ge(sem["exp_done"], CH * t + c + 1)
                                nc.tensor.transpose(ps[0:CL, 4 * c + 1, 128:128 + CB], ex[:, c, :], ident[0:CB, 0:CB]).then_inc(sem["o_turned"], 1)

                            def attend(t, c):
                                pe.wait_ge(sem["pT_ready"], CH * t + c + 1)
                                nc.tensor.matmul(ps[:, attended_bank(t, c), 128:128 + 2 * CB], ones16[0:CL, :], eT[:, c].rearrange("p j i -> p (j i)"),
                                                 start=True, stop=True, skip_group_check=True)
                                for j in range(CB):
                                    for i in range(3):
                                        m = 2 if i < 2 else 1
                                        last = nc.tensor.matmul(ps[:, attended_bank(t, c), 2 * j:2 * j + m], ctxp[:, i, CB * c + j, :], eT[:, c, j, 0:m],
                                                                start=(i == 0), stop=(i == 2), skip_group_check=True)
                                last.then_inc(sem["pv_done"], 1)

                            def late(t, c):
                                pe.wait_ge(sem["o_normed"], CH * t + c + 1)
                                for i in range(3):
                                    for a, b in PRODUCTS:
                                        last = nc.tensor.matmul(ps[:, gate_bank(t, c), i * CB:(i + 1) * CB], gate_p["c"][:, a, i * D:(i + 1) * D], cvp[:, c, :, b],
                                                                start=False, stop=(a == 2), skip_group_check=True)
                                last.then_inc(sem["gate_done"], 1)

                            pe.wait_ge(sem["x_ready"], 1)
                            for c in range(CH):
                                of_token(0, c)
                            for t in range(RUN):
                                for part in (score, turn_scores):
                                    for c in range(CH):
                                        part(t, c)
                                for c in range(CH):
                                    of_state(t, c)
                                    turn_weights(t, c)
                                for part in (attend, late):
                                    for c in range(CH):
                                        part(t, c)
                                if t + 1 < RUN:
                                    for c in range(CH):
                                        of_token(t + 1, c)

                        @block.vector
                        def _(dve):
                            step = Steps(dve, sem["vector_step"])
                            nc.vector.tensor_copy(xloc[:], decT[:, :, bass.ds(n * RUN, RUN), :])
                            nc.vector.tensor_copy(hist[:, 0, :], hist[:, RUN, :]).then_inc(sem["x_ready"], 1)
                            dve.wait_ge(sem["x_ready"], 1)

                            def scores(t, c):
                                dve.wait_ge(sem["scores_done"], CH * t + c + 1)
                                nc.vector.tensor_reduce(sT[:, c, :], ps[0:CL, 4 * c, 0:3 * CB].rearrange("p (j i) -> p j i", i=3), AX.X, ALU.add).then_inc(sem["k_read"], 1)

                            def maximum(t, c):
                                dve.wait_ge(sem["turned"], CH * t + c + 1)
                                nc.vector.tensor_reduce(nm[:, c:c + 1], ps[0:CB, 4 * c + 1, 0:CL], AX.X, ALU.max, negate=True).then_inc(sem["cand_ready"], 1)

                            def turned(t, c):
                                dve.wait_ge(sem["o_turned"], CH * t + c + 1)
                                src = ps[0:CL, 4 * c + 1, 128:128 + CB]
                                step(nc.vector.tensor_scalar(eT[:, c, :, 0], src, SCALE, None, ALU.mult))
                                nc.vector.scalar_tensor_tensor(out=eT[:, c, :, 1], in0=src, scalar=SCALE, in1=eT[:, c, :, 0],
                                                               op0=ALU.mult, op1=ALU.subtract).then_inc(sem["pT_ready"], 1)

                            def attended(t, c):
                                dve.wait_ge(sem["pv_done"], CH * t + c + 1)
                                nc.vector.tensor_reduce(den[:, c, :], ps[:, attended_bank(t, c), 128:128 + 2 * CB].rearrange("p (j i) -> p j i", i=2), AX.X, ALU.add)
                                step(nc.vector.tensor_reduce(t1[:, c, :], ps[:, attended_bank(t, c), 0:2 * CB].rearrange("p (j i) -> p j i", i=2), AX.X, ALU.add))
                                step(nc.vector.reciprocal(den[:, c, :], den[:, c, :]))
                                nc.vector.tensor_tensor(cv[:, c, :], t1[:, c, :], den[:, c, :], ALU.mult)
                                parts(step, (t1[:, c, :], den[:, c, :], ALU.mult), cv[:, c, :], lambda i: cvp[:, c, :, i],
                                      left[:, c, :]).then_inc(sem["o_normed"], 1)

                            def candidate(t, c):
                                dve.wait_ge(sem["gate_ready"], 2 * (CH * t + c) + 1)
                                gate = lambda i: ps[:, gate_bank(t, c), i * CB:(i + 1) * CB]
                                dve.wait_ge(sem["gate_ready"], 2 * (CH * t + c) + 2)
                                step(nc.vector.scalar_tensor_tensor(out=t1[:, c, :], in0=rt[:, c, :], scalar=1.0, in1=gate(3), op0=ALU.add, op1=ALU.mult))
                                nc.vector.scalar_tensor_tensor(out=t1[:, c, :], in0=t1[:, c, :], scalar=0.5, in1=gate(2), op0=ALU.mult, op1=ALU.add).then_inc(sem["hid_done"], 1)

                            def blend(t, c):
                                nc.vector.tensor_scalar(keep[:, c, :], zt[:, c, :], 0.5, 0.5, ALU.mult, ALU.add)
                                step(nc.vector.tensor_scalar(zt[:, c, :], zt[:, c, :], -0.5, 0.5, ALU.mult, ALU.add))
                                step(nc.vector.tensor_tensor(keep[:, c, :], keep[:, c, :], hist[:, t, mine(c)], ALU.mult))

                            def state(t, c):
                                dve.wait_ge(sem["hid_ready"], CH * t + c + 1)
                                step(nc.vector.tensor_tensor(t1[:, c, :], zt[:, c, :], cand[:, c, :], ALU.mult))
                                new = hist[:, t + 1, mine(c)]
                                nc.vector.tensor_tensor(new, t1[:, c, :], keep[:, c, :], ALU.add)
                                parts(step, (t1[:, c, :], keep[:, c, :], ALU.add), new, lambda i: hp[:, mine(c), i],
                                      left[:, c, :]).then_inc(sem["mix_added"], 1)

                            for t in range(RUN):
                                for part in (scores, maximum, turned, attended):
                                    for c in range(CH):
                                        part(t, c)
                                for c in range(CH):
                                    candidate(t, c)
                                    blend(t, c)
                                    state(t, c)
                            dve.wait_ge(sem["mix_added"], CH * RUN)
                            nc.vector.tensor_copy(gru[:, bass.ds(n * RUN, RUN), :], hist[:, 1:RUN + 1, :])

                        @block.scalar
                        def _(act):
                            def exponentials(t, c):
                                act.wait_ge(sem["cand_ready"], CH * t + c + 1)
                                nc.scalar.activation(ex[:, c, :], ps[0:CB, 4 * c + 1, 0:CL], ACT.Exp, bias=nm[:, c:c + 1]).then_inc(sem["exp_done"], 1)

                            def gates(t, c):
                                act.wait_ge(sem["gate_done"], CH * t + c + 1)
                                for i, dst in ((1, rt), (0, zt)):
                                    nc.scalar.activation(dst[:, c, :], ps[:, gate_bank(t, c), i * CB:(i + 1) * CB], ACT.Tanh, bias=bias[:, i:i + 1],
                                                         scale=0.5).then_inc(sem["gate_ready"], 1)

                            def candidates(t, c):
                                act.wait_ge(sem["hid_done"], CH * t + c + 1)
                                nc.scalar.activation(cand[:, c, :], t1[:, c, :], ACT.Tanh, bias=bias[:, 2:3]).then_inc(sem["hid_ready"], 1)

                            for t in range(RUN):
                                for c in range(CH):
                                    exponentials(t, c)
                                for c in range(CH):
                                    gates(t, c)
                                    candidates(t, c)
                    rest()

                with nc.Block() as block:
                    @block.tensor
                    def _(pe):
                        for i in range(NG):
                            for u in range(U):
                                last = nc.tensor.transpose(ps[:, i, u * D:(u + 1) * D], gru[:, :, i * U + u], ident[:])
                            last.then_inc(sem["turned"], 1)

                    @block.vector
                    def _(dve):
                        for i in range(NG):
                            dve.wait_ge(sem["turned"], i + 1)
                            nc.vector.tensor_tensor(x_all[:, i * U:(i + 1) * U, :], x_all[:, i * U:(i + 1) * U, :], per(i), ALU.add)
                rest()

        if "F" in SECTIONS:
            stage_gru()

        def stage_moe():
            with ExitStack() as st:
                wg = sb("G_wg", [D, EXPERTS], scope=st)
                bg = sb("G_bg", [1, EXPERTS], scope=st)
                w1 = sb("G_w1", [D, EXPERTS, FFN], scope=st)
                b1 = sb("G_b1", [D, EXPERTS, 4], scope=st)
                w2 = sb("G_w2", [D, EXPERTS, 4, D], scope=st)
                b2 = sb("G_b2", [1, EXPERTS, D], scope=st)
                hid = sb("G_hid", [D, 2, 4, U * S], scope=st)
                loads = [(wg[:], dram["L2_ffn_gate_w"]), (bg[:], dram["L2_ffn_gate_b"].unsqueeze(0)),
                         (b2[:], dram["L2_ffn_b2"].unsqueeze(0))]
                for x in range(EXPERTS):
                    loads.append((w1[:, x, :], dram["L2_ffn_w1"][x]))
                    loads.append((b1[:, x, :], dram["L2_ffn_b1"][x].rearrange("(c p) -> p c", p=D)))
                    loads.append((w2[:, x], dram["L2_ffn_w2"][x].rearrange("(c p) n -> p c n", p=D)))
                with nc.Block() as block:
                    @block.sync
                    def _(sp):
                        for dst, src in loads:
                            sp.dma_start(dst, src, allow_slow_non_contiguous=True).then_inc(sem["loaded"], 16)
                        sp.wait_ge(sem["loaded"], 16 * len(loads))

                    @block.vector
                    def _(dve):
                        nc.vector.memset(gates[:], PAD)
                rest()

                with nc.Fori(0, NG) as g:
                    with nc.Block() as block:
                        @block.tensor
                        def _(pe):
                            turn_rows(pe, 0, bank=TURN)
                            pe.wait_ge(sem["xnT_ready"], 1)
                            for u in range(U):
                                nc.tensor.matmul(per(TURN, EXPERTS)[:, u, :], xnT[:, u * S:(u + 1) * S], wg[:], start=True, stop=False)
                                last = nc.tensor.matmul(per(TURN, EXPERTS)[:, u, :], ones[0:1, :], bg[:], start=False, stop=True)
                            last.then_inc(sem["gate_done"], 1)

                            def hidden(x):
                                for c in range(4):
                                    bank = job_bank(pe, 4 * x + c)
                                    nc.tensor.matmul(ps[:, bank, :], w1[:, x, c * D:(c + 1) * D], xnT[:], start=True, stop=True).then_inc(sem["proj_done"], 1)

                            hidden(0)
                            for x in range(EXPERTS):
                                if x + 1 < EXPERTS:
                                    hidden(x + 1)
                                jobs_read(pe, 4 * x + 4)
                                if x >= 2:
                                    pe.wait_ge(sem["mix_added"], x - 1)
                                for u in range(U):
                                    for c in range(4):
                                        nc.tensor.matmul(per(OUT + x % 2)[:, u, :], hid[:, x % 2, c, u * S:(u + 1) * S], w2[:, x, c, :],
                                                         start=(c == 0), stop=False)
                                    last = nc.tensor.matmul(per(OUT + x % 2)[:, u, :], ones[0:1, :], b2[:, x, :], start=False, stop=True)
                                last.then_inc(sem["mix_done"], 1)

                        def relu_job(eng, k):
                            x, c = k // 4, k % 4
                            eng.wait_ge(sem["proj_done"], k + 1)
                            if x >= 2 and c < 2:
                                eng.wait_ge(sem["mix_done"], x - 1)
                            dst, src = hid[:, x % 2, c, :], ps[:, c, :]
                            if k % 2 == 0:
                                nc.scalar.activation(dst, src, ACT.Relu, bias=b1[:, x, c:c + 1]).then_inc(sem["q_read"], 1)
                            else:
                                nc.vector.tensor_scalar(dst, src, b1[:, x, c:c + 1], 0.0, ALU.add, ALU.max).then_inc(sem["k_read"], 1)

                        @block.scalar
                        def _(act):
                            act.wait_ge(sem["zT_done"], 1)
                            nc.scalar.activation(xnT[:], ps[:, TURN, :], ACT.Copy).then_inc(sem["xnT_ready"], 1)
                            route_scalar(act)
                            for k in range(0, 4 * EXPERTS, 2):
                                relu_job(act, k)

                        @block.vector
                        def _(dve):
                            step = Steps(dve, sem["vector_step"])
                            ln_vector(dve, step, 0, lambda u: x_all[:, g * U + u, :]).then_inc(sem["z_ready"], 1)
                            step(nc.vector.tensor_copy(xs[:], x_all[:, bass.ds(g * U, U), :]))
                            route_vector(dve, step, TURN, False)
                            relu_job(dve, 1)
                            relu_job(dve, 3)
                            for x in range(EXPERTS):
                                if x + 1 < EXPERTS:
                                    relu_job(dve, 4 * x + 5)
                                    relu_job(dve, 4 * x + 7)
                                dve.wait_ge(sem["mix_done"], x + 1)
                                for u in range(U):
                                    last = nc.vector.scalar_tensor_tensor(out=xs[:, u, :], in0=per(OUT + x % 2)[:, u, :], scalar=chosen[:, u, x:x + 1],
                                                                          in1=xs[:, u, :], op0=ALU.mult, op1=ALU.add)
                                last.then_inc(sem["mix_added"], 1)
                                dve.wait_ge(sem["mix_added"], x + 1)
                            nc.vector.tensor_copy(x_all[:, bass.ds(g * U, U), :], xs[:])

                        @block.gpsimd
                        def _(pool):
                            ln_pool(pool, 0)
                    rest()

        if "G" in SECTIONS:
            stage_moe()

        def stage_layers():
            with ExitStack() as st:
                y_all = sb("H_y", [S, B, D], scope=st)
                square = ["q_w", "qs_w", "k_w", "ks_w", "v_w", "cqs_w", "cks_w"]
                w = {n: sb("H_" + n, [D, D], scope=st) for n in square}
                plain = ["so_w", "cq_w", "ck_w", "cv_w", "co_w"]
                w.update({n: sb("H_" + n, [D, D], scope=st) for n in plain})
                f1 = sb("H_f1", [D, FFN], scope=st)
                f1b = sb("H_f1b", [D, 4], scope=st)
                f2 = sb("H_f2", [D, 4, D], scope=st)
                f2b = sb("H_f2b", [1, D], scope=st)
                nw = sb("H_nw", [D, 3, 2 * D], scope=st)
                nb = sb("H_nb", [D, 3, 2], scope=st)
                gb = sb("H_gb", [D, 3, 2, B], scope=st)
                gb4 = sb("H_gb4", [D, 3, 2, U], scope=st)
                cosT = sb("H_cos", [D, S], scope=st)
                sinT = sb("H_sin", [D, S], scope=st)
                ctxg = sb("H_ctxg", [D, UC], scope=st)
                ta = sb("H_ta", [D, 2 * U * S], scope=st)
                tb = sb("H_tb", [D, 2 * U * S], scope=st)
                qr = sb("H_qr", [D, U * S], scope=st)
                kr = sb("H_kr", [D, U * S], scope=st)
                cr = sb("H_cr", [D, PADDED], scope=st)
                qm = sb("H_qm", [D, NH, U * S], scope=st)
                heads = sb("H_heads", [D, NH], scope=st)
                vp = sb("H_vp", [S, U, NH, 3 * HP], BF16, scope=st)
                cvp = sb("H_cvp", [CL, U, NH, 3 * HP], BF16, scope=st)
                o8 = sb("H_o8", [S, U, D], scope=st)
                hid = sb("H_hid", [D, 4, U * S], scope=st)
                mask_s = sb("H_mask_s", [1, B * S // 4], mybir.dt.uint32, scope=st)
                mask_c = sb("H_mask_c", [1, B * CL // 4], mybir.dt.uint32, scope=st)
                low_s = sb("H_low_s", [1, B * S], BF16, scope=st)
                low_c = sb("H_low_c", [1, B * CL], BF16, scope=st)
                low4 = sb("H_low4", [1, U * S], BF16, scope=st)
                low4c = sb("H_low4c", [1, PADDED], BF16, scope=st)

                with nc.Block() as block:
                    @block.sync
                    def _(sp):
                        sp.dma_start(cosT[:], dram["cosT"]).then_inc(sem["loaded"], 16)
                        sp.dma_start(sinT[:], dram["sinT"]).then_inc(sem["loaded"], 16)
                        sp.dma_start(heads[:], dram["head_mask"]).then_inc(sem["loaded"], 16)
                        sp.dma_start(mask_s[:], dram["mask_BxS_bf0"].unsqueeze(0)).then_inc(sem["loaded"], 16)
                        sp.dma_start(mask_c[:], dram["mask_BxS2_bf0"].unsqueeze(0)).then_inc(sem["loaded"], 16)

                    @block.vector
                    def _(dve):
                        step = Steps(dve, sem["vector_step"])
                        nc.vector.memset(cr[:], 0.0)
                        nc.vector.memset(low4c[:], 0.0)
                        for t in (vp, cvp):
                            step(nc.vector.memset(t[:], 0.0))
                            nc.vector.memset(t[:, :, :, HD:HP], 1.0)
                        dve.wait_ge(sem["loaded"], 80)
                        nc.vector.tensor_scalar(low_s[:], mask_s[:].bitcast(U8), MASKED, None, ALU.mult)
                        nc.vector.tensor_scalar(low_c[:], mask_c[:].bitcast(U8), MASKED, None, ALU.mult)
                rest()

                with nc.Fori(0, NG) as g:
                    with nc.Block() as block:
                        @block.vector
                        def _(dve):
                            step = Steps(dve, sem["vector_step"])
                            ln_vector(dve, step, 0, lambda u: x_all[:, g * U + u, :], lambda u: y_all[:, g * U + u, :])

                        @block.gpsimd
                        def _(pool):
                            ln_pool(pool, 0)
                    rest()

                def layer_loads(l):
                    one = lambda name, pat, **kw: dram[name][bass.ds(l, 1)].rearrange(pat, **kw)
                    out = [(w[n][:], one("L3_" + n, "a p n -> p (a n)")) for n in square]
                    out += [(w[n][:], one("L3_xcond_" + n, "a p n -> p (a n)")) for n in plain]
                    out += [(f1[:], one("L3_xcond_f1_w", "a p n -> p (a n)")),
                            (f1b[:], one("L3_xcond_f1_b", "a (c p) -> p (a c)", p=D)),
                            (f2[:], one("L3_xcond_f2_w", "a (c p) n -> p (a c) n", p=D)),
                            (f2b[:], one("L3_xcond_f2_b", "a n -> a n"))]
                    for i in range(3):
                        out.append((nw[:, i, :], one(f"L3_xcond_n{i + 1}_w", "a p n -> p (a n)")))
                        out.append((nb[:, i, :], one(f"L3_xcond_n{i + 1}_b", "a (c p) -> p (a c)", p=D)))
                    return out

                with nc.Fori(0, LAYERS) as l:
                    with nc.Block() as block:
                        n_loads = 22

                        @block.sync
                        def _(sp):
                            loads = layer_loads(l)
                            assert len(loads) == n_loads
                            for dst, src in loads:
                                sp.dma_start(dst, src, allow_slow_non_contiguous=True).then_inc(sem["loaded"], 16)

                        @block.tensor
                        def _(pe):
                            pe.wait_ge(sem["loaded"], 16 * n_loads)
                            for n in range(3):
                                for c in range(2):
                                    last = nc.tensor.matmul(ps[:, 0, (2 * n + c) * B:(2 * n + c + 1) * B], nw[:, n, c * D:(c + 1) * D],
                                                            condT[:], start=True, stop=True)
                            last.then_inc(sem["proj_done"], 1)

                        @block.vector
                        def _(dve):
                            step = Steps(dve, sem["vector_step"])
                            dve.wait_ge(sem["loaded"], 16 * n_loads)
                            step(nc.vector.tensor_scalar(nb[:, :, 0], nb[:, :, 0], 1.0, None, ALU.add))
                            dve.wait_ge(sem["proj_done"], 1)
                            nc.vector.tensor_tensor(gb[:].rearrange("p n c b -> p (n c) b"),
                                                    ps[:, 0, 0:6 * B].rearrange("p (n b) -> p n b", b=B),
                                                    nb[:].rearrange("p n c -> p (n c)").unsqueeze(2).broadcast_to([D, 6, B]), ALU.add)
                    rest()

                    with nc.Fori(0, NG) as g:
                        with nc.Block() as block:
                            P2 = 2 * S
                            rope_banks = ((4, 5), (0, 0), (1, 1), (4, 4), (5, 5), (0, 0), (4, 4))
                            rope_slot = (slice(0, UC), slice(512, 768), slice(768, 1024), slice(0, 256), slice(256, 512),
                                         slice(512, 768), slice(768, 1024))
                            rope_to = (cr[:, 0:UC], qr[:, 0:P2], kr[:, 0:P2], qr[:, P2:], kr[:, P2:], qr[:, 0:P2], qr[:, P2:])
                            EARLY, LATE = 1, 3

                            @block.tensor
                            def _(pe):
                                def turn_pair(r, pair, bank):
                                    pe.wait_ge(sem["z_ready"], 2 * r + pair + 1)
                                    for k in range(2):
                                        last = nc.tensor.transpose(ps[:, bank, k * S:(k + 1) * S], zn[:, 2 * pair + k, 0:D], ident[:])
                                    last.then_inc(sem["zT_done"], 1)

                                def project(pair, bank, a, b):
                                    for k, m in enumerate((a, b)):
                                        last = nc.tensor.matmul(ps[:, bank, k * P2:(k + 1) * P2], w[m][:], xnT[:, pair * P2:(pair + 1) * P2],
                                                                start=True, stop=True)
                                    last.then_inc(sem["q_done"], 1)

                                def outputs(a, pair, m, part):
                                    if part == 0:
                                        pe.wait_ge(sem["o_normed"], NU * a + 4 * (pair + 1))
                                        for k in range(2):
                                            last = nc.tensor.transpose(ps[:, 2 * pair, k * S:(k + 1) * S], o8[:, 2 * pair + k, :], ident[:])
                                        last.then_inc(sem["o_turned"], 1)
                                    else:
                                        pe.wait_ge(sem["oT_ready"], 2 * a + pair + 1)
                                        for k in range(2):
                                            u = 2 * pair + k
                                            last = nc.tensor.matmul(ps[:, (EARLY, LATE)[pair], k * D:(k + 1) * D], xnT[:, u * S:(u + 1) * S],
                                                                    w[m][:], start=True, stop=True)
                                        last.then_inc(sem["mix_done"], 1)

                                pe.wait_ge(sem["x_ready"], 1)
                                for bank, m in ((4, "ck_w"), (5, "cks_w")):
                                    last = nc.tensor.matmul(ps[:, bank, 0:UC], w[m][:], ctxg[:], start=True, stop=True)
                                last.then_inc(sem["q_done"], 1)
                                for u in range(U):
                                    last = nc.tensor.matmul(per(7)[0:CL, u, :], ctxg[:, u * CL:(u + 1) * CL], w["cv_w"][:], start=True, stop=True)
                                last.then_inc(sem["v_done"], 1)
                                turn_pair(0, 0, 6)
                                turn_pair(0, 1, 2)
                                pe.wait_ge(sem["xnT_ready"], 1)
                                project(0, 0, "q_w", "qs_w")
                                project(0, 1, "k_w", "ks_w")
                                pe.wait_ge(sem["xnT_ready"], 2)
                                pe.wait_ge(sem["rope_done"], 1)
                                project(1, 4, "q_w", "qs_w")
                                project(1, 5, "k_w", "ks_w")
                                pe.wait_ge(sem["v_read"], 1)
                                for u in range(U):
                                    last = nc.tensor.matmul(per(7)[:, u, :], xnT[:, u * S:(u + 1) * S], w["v_w"][:], start=True, stop=True)
                                last.then_inc(sem["v_done"], 1)
                                pe.wait_ge(sem["rope_done"], 3)
                                pe.wait_ge(sem["table_ready"], 3)
                                pe.wait_ge(sem["low_ready"], 1)
                                small_tensor(pe, 0, S, qm, kr, vp, low4, 2, 5, lambda part: outputs(0, 0, "so_w", part), 5)
                                outputs(0, 1, "so_w", 0)
                                outputs(0, 1, "so_w", 1)
                                turn_pair(1, 0, TURN)
                                turn_pair(1, 1, TURN + 1)
                                pe.wait_ge(sem["xnT_ready"], 3)
                                project(0, 0, "cq_w", "cqs_w")
                                pe.wait_ge(sem["xnT_ready"], 4)
                                project(1, 4, "cq_w", "cqs_w")
                                pe.wait_ge(sem["rope_done"], 6)
                                small_tensor(pe, 1, CL, qm, cr, cvp, low4c, 2, 7, lambda part: outputs(1, 0, "co_w", part))
                                outputs(1, 1, "co_w", 0)
                                outputs(1, 1, "co_w", 1)
                                nc.tensor.matmul(per(OUT), ones[0:1, :], f2b[:].unsqueeze(1).broadcast_to([1, U, D]), start=True,
                                                 stop=False, skip_group_check=True)
                                turn_pair(2, 0, TURN)
                                turn_pair(2, 1, TURN + 1)
                                pe.wait_ge(sem["xnT_ready"], 6)
                                for c in range(4):
                                    nc.tensor.matmul(ps[:, c, :], f1[:, c * D:(c + 1) * D], xnT[:], start=True, stop=True).then_inc(sem["hid_done"], 1)
                                for c in range(4):
                                    pe.wait_ge(sem["hid_ready"], c + 1)
                                    for u in range(U):
                                        last = nc.tensor.matmul(per(OUT)[:, u, :], hid[:, c, u * S:(u + 1) * S], f2[:, c, :], start=False,
                                                                stop=(c == 3), skip_group_check=True)
                                last.then_inc(sem["mix_done"], 1)

                            @block.scalar
                            def _(act):
                                def affine(r, pair, bank):
                                    act.wait_ge(sem["zT_done"], 2 * r + pair + 1)
                                    for k in range(2):
                                        u = 2 * pair + k
                                        last = nc.scalar.activation(xnT[:, u * S:(u + 1) * S], ps[:, bank, k * S:(k + 1) * S], ACT.Identity,
                                                                    bias=gb4[:, r, 1, u:u + 1], scale=gb4[:, r, 0, u:u + 1])
                                    last.then_inc(sem["xnT_ready"], 1)

                                def outputs(a, pair):
                                    act.wait_ge(sem["o_turned"], 2 * a + pair + 1)
                                    nc.scalar.activation(xnT[:, pair * P2:(pair + 1) * P2], ps[:, 2 * pair, 0:P2], ACT.Copy).then_inc(sem["oT_ready"], 1)

                                nc.scalar.activation(gb4[:].rearrange("p n c u -> p (n c) u"),
                                                     gb[:].rearrange("p n c b -> p (n c) b")[:, :, bass.ds(g * U, U)],
                                                     ACT.Copy).then_inc(sem["scalar_step"], 1)
                                act.wait_ge(sem["scalar_step"], 1)
                                affine(0, 0, 6)
                                affine(0, 1, 2)
                                act.wait_ge(sem["table_ready"], 2)
                                mask_queries("scalar", 0, qr, qm, heads)
                                act.wait_ge(sem["table_ready"], 4)
                                mask_queries("scalar", 1, qr, qm, heads)
                                small_scalar(act, 0, S, lambda: outputs(0, 0))
                                outputs(0, 1)
                                affine(1, 0, TURN)
                                affine(1, 1, TURN + 1)
                                act.wait_ge(sem["table_ready"], 6)
                                mask_queries("scalar", 0, qr, qm, heads)
                                act.wait_ge(sem["table_ready"], 7)
                                mask_queries("scalar", 1, qr, qm, heads)
                                small_scalar(act, 1, CL, lambda: outputs(1, 0))
                                outputs(1, 1)
                                affine(2, 0, TURN)
                                affine(2, 1, TURN + 1)
                                for c in range(4):
                                    act.wait_ge(sem["hid_done"], c + 1)
                                    nc.scalar.activation(hid[:, c, :], ps[:, c, :], ACT.Gelu, bias=f1b[:, c:c + 1]).then_inc(sem["hid_ready"], 1)

                            @block.vector
                            def _(dve):
                                step = Steps(dve, sem["vector_step"])

                                def rotate(p):
                                    n = CL if p == 0 else S
                                    k = U if p == 0 else 2
                                    dve.wait_ge(sem["q_done"], p + 1)
                                    if p in (3, 5, 6):
                                        dve.wait_ge(sem["table_ready"], {3: 1, 5: 2, 6: 3}[p])
                                    b0, b1 = rope_banks[p]
                                    second = 0 if b0 != b1 else P2
                                    for bank, at, table, t in ((b0, 0, cosT, ta), (b1, second, sinT, tb)):
                                        last = nc.vector.tensor_tensor(t[:, rope_slot[p]].rearrange("p (u t) -> p u t", u=k),
                                                                       ps[:, bank, at:at + k * n].rearrange("p (u t) -> p u t", u=k),
                                                                       table[:, 0:n].unsqueeze(1).broadcast_to([D, k, n]), ALU.mult)
                                    last.then_inc(sem["rope_done"], 1)

                                def statistics(us):
                                    for u in us:
                                        last = nc.vector.bn_stats(stats[:, u, :], xs[:, u, :])
                                    return last

                                def normalise(r, meanwhile=None):
                                    for u in range(U):
                                        last = nc.vector.bn_aggr(mv[:, u, :], stats[:, u, :])
                                    step(last)
                                    nc.vector.tensor_scalar(veps[:], mv[:, :, 1], LN_EPS, None, ALU.add).then_inc(sem["var_ready"], 1)
                                    if meanwhile:
                                        meanwhile()
                                    dve.wait_ge(sem["rstd_ready"], r + 1)
                                    for u in range(U):
                                        last = nc.vector.tensor_scalar(zn[:, u, 0:D], xs[:, u, :], mv[:, u, 0:1], rstd[:, u:u + 1],
                                                                       ALU.subtract, ALU.mult)
                                        if u % 2:
                                            last.then_inc(sem["z_ready"], 1)

                                def add_outputs(a, pair):
                                    at = slice(2 * pair, 2 * pair + 2)
                                    dve.wait_ge(sem["mix_done"], 2 * a + pair + 1)
                                    step(nc.vector.tensor_tensor(xs[:, at], xs[:, at],
                                                                 ps[:, (EARLY, LATE)[pair], 0:P2].rearrange("p (u d) -> p u d", u=2), ALU.add))

                                def early(a, part):
                                    if part == 1:
                                        add_outputs(a, 0)
                                        statistics((0, 1))

                                def late(a):
                                    add_outputs(a, 1)
                                    step(statistics((2, 3)))

                                nc.vector.tensor_copy(ctxg[:], ctxT[:, bass.ds(g * UC, UC)]).then_inc(sem["x_ready"], 1)
                                step(nc.vector.tensor_copy(xs[:], y_all[:, bass.ds(g * U, U), :]))
                                step(statistics(range(U)))
                                normalise(0, lambda: rotate(0))
                                nc.vector.tensor_copy(low4[:], low_s[:, bass.ds(g * U * S, U * S)])
                                nc.vector.tensor_copy(low4c[:, 0:UC], low_c[:, bass.ds(g * UC, UC)]).then_inc(sem["low_ready"], 1)
                                dve.wait_ge(sem["v_done"], 1)
                                split_values(step, 7, cvp, CL).then_inc(sem["v_read"], 1)
                                rotate(1)
                                rotate(2)
                                dve.wait_ge(sem["table_ready"], 2)
                                mask_queries("vector", 0, qr, qm, heads)
                                rotate(3)
                                rotate(4)
                                dve.wait_ge(sem["table_ready"], 4)
                                mask_queries("vector", 1, qr, qm, heads)

                                def own_values():
                                    dve.wait_ge(sem["v_done"], 2)
                                    split_values(step, 7, vp, S).then_inc(sem["v_read"], 1)

                                small_vector(dve, step, 0, S, lambda u: o8[:, u, :], own_values, lambda part: early(0, part))
                                late(0)
                                normalise(1)
                                rotate(5)
                                dve.wait_ge(sem["table_ready"], 6)
                                mask_queries("vector", 0, qr, qm, heads)
                                rotate(6)
                                dve.wait_ge(sem["table_ready"], 7)
                                mask_queries("vector", 1, qr, qm, heads)
                                small_vector(dve, step, 1, CL, lambda u: o8[:, u, :], None, lambda part: early(1, part))
                                late(1)
                                normalise(2)
                                dve.wait_ge(sem["mix_done"], 5)
                                nc.vector.tensor_tensor(y_all[:, bass.ds(g * U, U), :], xs[:], per(OUT), ALU.add)

                            @block.gpsimd
                            def _(pool):
                                def add_products(p):
                                    pool.wait_ge(sem["rope_done"], p + 1)
                                    nc.gpsimd.tensor_tensor(rope_to[p], ta[:, rope_slot[p]], tb[:, rope_slot[p]], ALU.add).then_inc(sem["table_ready"], 1)

                                ln_pool(pool, 0)
                                for p in range(5):
                                    add_products(p)
                                ln_pool(pool, 1)
                                add_products(5)
                                add_products(6)
                                ln_pool(pool, 2)
                        rest()

                with nc.Block() as block:
                    @block.vector
                    def _(dve):
                        nc.vector.tensor_tensor(x_all[:], x_all[:], y_all[:], ALU.add)
                rest()

        if "H" in SECTIONS:
            stage_layers()

        def stage_ternary():
            with ExitStack() as st:
                wfc = sb("I_wfc", [D, FFN], scope=st)
                wpj = sb("I_wpj", [D, FFN], scope=st)
                neg = sb("I_neg", [D, FFN], scope=st)
                lnw = sb("I_lnw", [D, 4], scope=st)
                lnb = sb("I_lnb", [D, 4], scope=st)
                mag = sb("I_mag", [D, 2], scope=st)
                thr = sb("I_thr", [D, 2], scope=st)
                nthr = sb("I_nthr", [D, 2], scope=st)
                hid = sb("I_hid", [S, U, FFN], scope=st)
                hidT = sb("I_hidT", [D, 4, U * S], scope=st)
                loads = [(wfc[:], dram["L3_ffn_W_fc"]),
                         (wpj[:].rearrange("p (c n) -> p c n", c=4), dram["L3_ffn_W_proj"].rearrange("(c p) n -> p c n", p=D)),
                         (lnw[:], dram["L3_ffn_ln_w"].rearrange("(c p) -> p c", p=D)),
                         (lnb[:], dram["L3_ffn_ln_b"].rearrange("(c p) -> p c", p=D))]
                with nc.Block() as block:
                    @block.sync
                    def _(sp):
                        for dst, src in loads:
                            sp.dma_start(dst, src, allow_slow_non_contiguous=True).then_inc(sem["loaded"], 16)

                    @block.vector
                    def _(dve):
                        step = Steps(dve, sem["vector_step"])
                        dve.wait_ge(sem["loaded"], 16 * len(loads))
                        nc.vector.tensor_reduce(mag[:, 0:1], wfc[:], AX.X, ALU.add, apply_absolute_value=True)
                        nc.vector.tensor_reduce(mag[:, 1:2], wpj[:], AX.X, ALU.add, apply_absolute_value=True).then_inc(sem["z_ready"], 1)
                        dve.wait_ge(sem["zT_done"], 1)
                        step(nc.vector.tensor_scalar(thr[:], ps[:, 0, 0:2], 1.0 / (D * FFN), 1e-6, ALU.mult, ALU.add))
                        step(nc.vector.tensor_scalar(thr[:], thr[:], 0.5, None, ALU.mult))
                        step(nc.vector.tensor_scalar(nthr[:], thr[:], -1.0, None, ALU.mult))
                        for i, w in enumerate((wfc, wpj)):
                            step(nc.vector.tensor_scalar(neg[:], w[:], nthr[:, i:i + 1], None, ALU.is_lt))
                            step(nc.vector.scalar_tensor_tensor(out=w[:], in0=w[:], scalar=thr[:, i:i + 1], in1=neg[:],
                                                                op0=ALU.is_gt, op1=ALU.subtract))

                    @block.tensor
                    def _(pe):
                        pe.wait_ge(sem["z_ready"], 1)
                        nc.tensor.matmul(ps[:, 0, 0:2], ones[:], mag[:], start=True, stop=True).then_inc(sem["zT_done"], 1)
                rest()

                with nc.Fori(0, NG) as g:
                    with nc.Block() as block:
                        @block.tensor
                        def _(pe):
                            turn_rows(pe, 0, bank=TURN)
                            pe.wait_ge(sem["xnT_ready"], 1)
                            for u in range(U):
                                nc.tensor.matmul(ps[:, u, :], xnT[:, u * S:(u + 1) * S], wfc[:], start=True, stop=True).then_inc(sem["hid_done"], 1)
                            pe.wait_ge(sem["z_ready"], 2)
                            for c in range(4):
                                for u in range(U):
                                    last = nc.tensor.transpose(ps[:, c, u * S:(u + 1) * S], hid[:, u, c * D:(c + 1) * D], ident[:])
                                last.then_inc(sem["turned"], 1)
                            pe.wait_ge(sem["pT_ready"], 4)
                            for u in range(U):
                                for c in range(4):
                                    last = nc.tensor.matmul(per(OUT)[:, u, :], hidT[:, c, u * S:(u + 1) * S], wpj[:, c * D:(c + 1) * D],
                                                            start=(c == 0), stop=(c == 3))
                            last.then_inc(sem["mix_done"], 1)

                        @block.scalar
                        def _(act):
                            act.wait_ge(sem["zT_done"], 1)
                            nc.scalar.activation(xnT[:], ps[:, TURN, :], ACT.Copy).then_inc(sem["xnT_ready"], 1)
                            for u in range(U):
                                act.wait_ge(sem["hid_done"], u + 1)
                                last = nc.scalar.activation(hid[:, u, :], ps[:, u, :], ACT.Gelu).then_inc(sem["hid_ready"], 1)
                            for c in range(4):
                                act.wait_ge(sem["turned"], c + 1)
                                nc.scalar.activation(hidT[:, c, :], ps[:, c, :], ACT.Identity, bias=lnb[:, c:c + 1],
                                                     scale=lnw[:, c:c + 1]).then_inc(sem["pT_ready"], 1)

                        @block.vector
                        def _(dve):
                            step = Steps(dve, sem["vector_step"])
                            ln_vector(dve, step, 0, lambda u: x_all[:, g * U + u, :]).then_inc(sem["z_ready"], 1)
                            dve.wait_ge(sem["hid_ready"], U)
                            ln_vector(dve, step, 1, lambda u: hid[:, u, :], lambda u: hid[:, u, :]).then_inc(sem["z_ready"], 1)
                            dve.wait_ge(sem["mix_done"], 1)
                            xg = x_all[:, bass.ds(g * U, U), :]
                            nc.vector.tensor_tensor(xg, xg, per(OUT), ALU.add)

                        @block.gpsimd
                        def _(pool):
                            ln_pool(pool, 0)
                            ln_pool(pool, 1)
                    rest()

        if "I" in SECTIONS:
            stage_ternary()

        with nc.Block() as block:
            @block.sync
            def _(sp):
                sp.dma_start(out.rearrange("b t d -> t b d"), x_all[:]).then_inc(sem["stored"], 16)
                sp.wait_ge(sem["stored"], 16)


_TRANSPOSED = ["L0_ffn_expert_down", "L2_xcond_W", "L3_ffn_W_fc", "L3_ffn_W_proj"]


def kernel(**inputs):
    import concourse.bacc as _bacc
    from concourse.bass_utils import run_bass_kernel_spmd as _run

    f32 = np.float32
    arrays = {}
    for name, a in inputs.items():
        a = np.asarray(a)
        if a.dtype == np.bool_:
            a = np.ascontiguousarray(a).reshape(-1).view(np.uint32)
        arrays[name] = a
    for name in _TRANSPOSED:
        arrays[name] = arrays[name].T
    arrays["condT"] = arrays["cond_1024"].T
    for name in ("n1_w", "n2_w", "n3_w", "qkv_w", "so_w", "cq_w", "ck_w", "cv_w", "co_w", "f1_w", "f2_w"):
        arrays["L3_xcond_" + name] = arrays["L3_xcond_" + name].transpose(0, 2, 1)
    swap = np.arange(D).reshape(NH, 2, HD // 2)[:, ::-1, :].reshape(-1)
    qkv = arrays["L3_xcond_qkv_w"]
    arrays["L3_q_w"], arrays["L3_k_w"], arrays["L3_v_w"] = qkv[:, :, 0:D], qkv[:, :, D:2 * D], qkv[:, :, 2 * D:]
    arrays["L3_qs_w"] = arrays["L3_q_w"][:, :, swap]
    arrays["L3_ks_w"] = arrays["L3_k_w"][:, :, swap]
    arrays["L3_cqs_w"] = arrays["L3_xcond_cq_w"][:, :, swap]
    arrays["L3_cks_w"] = arrays["L3_xcond_ck_w"][:, :, swap]
    arrays["ident"] = np.eye(128, dtype=f32)
    half = HD // 2
    inv = (1.0 / 10000.0 ** (np.arange(half, dtype=f32) / f32(half))).astype(f32)
    ang = np.arange(S, dtype=f32)[:, None] * inv
    cos = np.cos(ang).astype(f32).T
    sin = np.sin(ang).astype(f32).T
    arrays["cosT"] = np.tile(np.concatenate([cos, cos]), (NH, 1))
    arrays["sinT"] = np.tile(np.concatenate([-sin, sin]), (NH, 1))
    rows = np.arange(D) // 16
    arrays["head_mask"] = np.repeat(np.eye(NH, dtype=f32), HD, axis=0) * f32(HD ** -0.5)
    arrays["block_mask"] = (rows[:, None] == np.arange(8)[None, :]).astype(f32)

    nc = _bacc.Bacc("TRN2", target_bir_lowering=False, num_devices=1)
    dram, given = {}, {}
    for name, a in arrays.items():
        a = np.ascontiguousarray(a)
        given["in_" + name] = a
        dram[name] = nc.dram_tensor("in_" + name, a.shape, mybir.dt.from_np(a.dtype), kind="ExternalInput").ap()
    out = nc.dram_tensor("out_x", (B, S, D), F32, kind="ExternalOutput").ap()
    build(nc, dram, out)
    r = _run(nc, [given], core_ids=[0])
    return r.results[0]["out_x"]
```
